# Optimizing a Trainium2 kernel written in Bass

```python
import numpy as np
import jax
import jax.numpy as jnp

def _softmax(x, axis=-1):
    return jax.nn.softmax(x, axis=axis)

def _gelu(x):
    return jax.nn.gelu(x, approximate=True)

def _silu(x):
    return jax.nn.silu(x)

def _sigmoid(x):
    return jax.nn.sigmoid(x)

def _layernorm(x, axis=-1, eps=1e-05):
    m = jnp.mean(x, axis=axis, keepdims=True)
    v = jnp.var(x, axis=axis, keepdims=True)
    return (x - m) / jnp.sqrt(v + eps)

def _scatter_add(tgt, idx, src, axis=0):
    return tgt.at[idx].add(src)

def _segment_sum(src, seg, n):
    return jax.ops.segment_sum(src, seg, n)
kernel_name = 'mk_decoder_preln_d1_seqx_r8_6a8113'

def setup_inputs(seed: int=0):
    np.random.seed(seed)
    _w = jnp.asarray

    def _rec_inputs():
        import jax
        import jax.numpy as jnp
        _rk = jax.random.key(seed)
        x = -0.0003929 + 0.9999 * jax.random.normal(jax.random.fold_in(_rk, 1), (8, 256, 128), jnp.float32)
        _lenS = 256 - jax.random.randint(jax.random.fold_in(_rk, 7), (8,), 0, max(1, 256 // 4) + 1, jnp.int32)
        _lenS2 = 512 - jax.random.randint(jax.random.fold_in(_rk, 8), (8,), 0, max(1, 512 // 4) + 1, jnp.int32)
        _ctx_1024P = jax.random.normal(jax.random.fold_in(_rk, 11), (8, 16, 128), jnp.float32)
        _ctx_1024c = jax.random.dirichlet(jax.random.fold_in(_rk, 511), 0.3 * jnp.ones((16,), jnp.float32), (8, 512))
        _ctx_1024t = jnp.einsum('bsk,bkd->bsd', _ctx_1024c, _ctx_1024P)
        _ctx_1024t = _ctx_1024t * jax.lax.rsqrt(jnp.mean(jnp.square(_ctx_1024t)) + 1e-12) * 0.953939
        ctx_1024 = 2.81802e-05 + 1.00001 * (_ctx_1024t + 0.3 * jax.random.normal(jax.random.fold_in(_rk, 611), (8, 512, 128), jnp.float32))
        _validS = jnp.arange(256)[None, :] < _lenS[:, None]
        _validS2 = jnp.arange(512)[None, :] < _lenS2[:, None]
        _causal = jnp.tril(jnp.ones((256, 256), dtype=bool))
        mask_S2_ik0 = jnp.where(_validS2[0], 0, 1).astype(jnp.int32)
        return (x, ctx_1024, mask_S2_ik0)
    x, ctx_1024, mask_S2_ik0 = _rec_inputs()

    def _L0_attn_setup():
        import jax, jax.numpy as jnp
        import numpy as np
        HEAD = 64

        def wkv6(r, k, v, w, u):
            B, T, C = r.shape
            N = C // HEAD
            shp = lambda a: a.reshape(B, T, N, HEAD).transpose(1, 0, 2, 3)
            rT, kT, vT = (shp(r), shp(k), shp(v))
            dT = jnp.exp(shp(w))
            uu = u[None]

            def step(S, inp):
                rt, kt, vt, dt = inp
                kv = vt[..., :, None] * kt[..., None, :]
                yt = jnp.einsum('bnj,bnij->bni', rt, S + uu[..., None, :] * kv)
                S = S * dt[..., None, :] + kv
                return (S, yt)
            S0 = jnp.zeros((B, N, HEAD, HEAD), r.dtype)
            _, ys = jax.lax.scan(step, S0, (rT, kT, vT, dT))
            return ys.transpose(1, 0, 2, 3).reshape(B, T, C)
        key = jax.random.key(seed)
        B, T, C = (2, 128, 128)
        N = C // HEAD
        depth, layer_id = (24, 12)
        r01 = layer_id / (depth - 1)
        r1a0 = 1.0 - layer_id / depth
        ddd = np.arange(C, dtype=np.float64) / C
        miu_x = (1.0 - ddd ** (0.6 * r1a0 ** 0.9)).reshape(1, 1, C).astype(np.float32)
        lam = np.stack([1.0 - ddd ** (0.9 * r1a0), 1.0 - ddd ** (0.9 * r1a0) - 0.4 * r01, 1.0 - ddd ** (0.4 * r1a0) - 0.6 * r01, 1.0 - ddd ** (0.2 * r1a0), 1.0 - ddd ** (0.2 * r1a0)]).reshape(5, 1, 1, C).astype(np.float32)
        n = np.arange(C, dtype=np.float64)
        td_miu = (-6.0 + 5.5 * (n / (C - 1)) ** (0.85 + 1.0 * r01 ** 0.5)).reshape(1, 1, C).astype(np.float32)
        zigzag = ((n + 1) % 3 - 1) * 0.1
        u = (r01 * (2.5 - n / (C - 1)) + zigzag).reshape(N, HEAD).astype(np.float32)
        ks = jax.random.split(key, 12)
        unif = lambda k, shape, s: jax.random.uniform(k, shape, jnp.float32, -s, s)
        x = jax.random.normal(ks[0], (B, T, C), jnp.float32)
        return {'x': x, 'miu_x': jnp.asarray(miu_x), 'lam': jnp.asarray(lam), 'A': unif(ks[1], (C, 160), 0.01), 'Bp': unif(ks[2], (5, 32, C), 0.01), 'td_miu': jnp.asarray(td_miu), 'tdA': unif(ks[3], (C, 64), 0.01), 'tdB': unif(ks[4], (64, C), 0.01), 'u': jnp.asarray(u), 'Wk': unif(ks[5], (C, C), 0.05 / C ** 0.5), 'Wv': unif(ks[6], (C, C), 0.5 / C ** 0.5), 'Wr': unif(ks[7], (C, C), 0.5 / C ** 0.5), 'Wo': unif(ks[8], (C, C), 0.5 / C ** 0.5), 'Wg1': unif(ks[9], (C, 160), 0.01), 'Wg2': unif(ks[10], (160, C), 0.01), 'gamma': jnp.ones((C,), jnp.float32), 'beta': jnp.zeros((C,), jnp.float32)}
    _L0_attn_all = _L0_attn_setup()
    _L0_attn_in = {k: v for k, v in _L0_attn_all.items() if k in ('miu_x', 'lam', 'A', 'Bp', 'td_miu', 'tdA', 'tdB', 'u', 'Wk', 'Wv', 'Wr', 'Wo', 'Wg1', 'Wg2', 'gamma', 'beta')}
    del _L0_attn_all

    def _L0_xattn_setup():
        import jax, jax.numpy as jnp
        import numpy as np
        DIM = 128
        NUM_HEADS = 8
        SCALE = (DIM // NUM_HEADS) ** (-0.5)
        key = jax.random.key(seed)
        k1, k2, k3, k4, k5, k6 = jax.random.split(key, 6)
        B, N, M, C = (8, 256, 256, DIM)
        x = jax.random.normal(k1, (B, N, C), dtype=jnp.float32)
        support = jax.random.normal(k2, (B, M, C), dtype=jnp.float32)
        attn_mask = jax.random.randint(k3, (M,), 0, 2, dtype=jnp.int32)
        qkv_w = jax.random.normal(k4, (3 * C, C), dtype=jnp.float32) * C ** (-0.5)
        proj_w = jax.random.normal(k5, (C, C), dtype=jnp.float32) * C ** (-0.5)
        proj_b = jax.random.normal(k6, (C,), dtype=jnp.float32) * 0.01
        return {'x': x, 'support': support, 'attn_mask': attn_mask, 'qkv_w': qkv_w, 'proj_w': proj_w, 'proj_b': proj_b}
    _L0_xattn_all = _L0_xattn_setup()
    _L0_xattn_in = {k: v for k, v in _L0_xattn_all.items() if k in ('qkv_w', 'proj_w', 'proj_b')}
    del _L0_xattn_all

    def _L0_ffn_setup():
        import jax, jax.numpy as jnp
        import numpy as np
        B, S, D = (1, 256, 128)
        E, F = (16, 128)
        NG, TKG, K = (4, 2, 4)
        NSH = 2
        SCALE = 2.5
        STD = 0.02
        EPG = E // NG

        def _route(x_flat, router_w, bias):
            logits = x_flat.astype(jnp.float32) @ router_w.T
            scores = jax.nn.sigmoid(logits)
            s = scores + bias[None, :]
            sg = s.reshape(-1, NG, EPG)
            group_score = jax.lax.top_k(sg, 2)[0].sum(-1)
            gidx = jax.lax.top_k(group_score, TKG)[1]
            gmask = jnp.sum(jax.nn.one_hot(gidx, NG, dtype=jnp.float32), axis=1) > 0
            emask = jnp.repeat(gmask, EPG, axis=1)
            masked = jnp.where(emask, s, -1.0)
            topk_idx = jax.lax.top_k(masked, K)[1]
            tw = jnp.take_along_axis(scores, topk_idx, axis=1)
            tw = tw / (tw.sum(-1, keepdims=True) + 1e-20)
            tw = tw * SCALE
            return (topk_idx, tw)
        key = jax.random.key(seed)
        ks = jax.random.split(key, 8)
        return {'hidden_states': jax.random.normal(ks[0], (B, S, D), jnp.float32), 'router_w': jax.random.normal(ks[1], (E, D), jnp.float32) * STD, 'bias': jnp.zeros((E,), jnp.float32), 'gate_w': jax.random.normal(ks[2], (E, D, F), jnp.float32) * STD, 'up_w': jax.random.normal(ks[3], (E, D, F), jnp.float32) * STD, 'down_w': jax.random.normal(ks[4], (E, F, D), jnp.float32) * STD, 'sh_gate_w': jax.random.normal(ks[5], (D, NSH * F), jnp.float32) * STD, 'sh_up_w': jax.random.normal(ks[6], (D, NSH * F), jnp.float32) * STD, 'sh_down_w': jax.random.normal(ks[7], (NSH * F, D), jnp.float32) * STD}
    _L0_ffn_all = _L0_ffn_setup()
    _L0_ffn_in = {k: v for k, v in _L0_ffn_all.items() if k in ('router_w', 'bias', 'gate_w', 'up_w', 'down_w', 'sh_gate_w', 'sh_up_w', 'sh_down_w')}
    del _L0_ffn_all
    return {'x': x, 'ctx_1024': ctx_1024, 'mask_S2_ik0': mask_S2_ik0, 'L0_attn_miu_x': _L0_attn_in['miu_x'], 'L0_attn_lam': _L0_attn_in['lam'], 'L0_attn_A': _L0_attn_in['A'], 'L0_attn_Bp': _L0_attn_in['Bp'], 'L0_attn_td_miu': _L0_attn_in['td_miu'], 'L0_attn_tdA': _L0_attn_in['tdA'], 'L0_attn_tdB': _L0_attn_in['tdB'], 'L0_attn_u': _L0_attn_in['u'], 'L0_attn_Wk': _L0_attn_in['Wk'], 'L0_attn_Wv': _L0_attn_in['Wv'], 'L0_attn_Wr': _L0_attn_in['Wr'], 'L0_attn_Wo': _L0_attn_in['Wo'], 'L0_attn_Wg1': _L0_attn_in['Wg1'], 'L0_attn_Wg2': _L0_attn_in['Wg2'], 'L0_attn_gamma': _L0_attn_in['gamma'], 'L0_attn_beta': _L0_attn_in['beta'], 'L0_xattn_qkv_w': _L0_xattn_in['qkv_w'], 'L0_xattn_proj_w': _L0_xattn_in['proj_w'], 'L0_xattn_proj_b': _L0_xattn_in['proj_b'], 'L0_ffn_router_w': _L0_ffn_in['router_w'], 'L0_ffn_bias': _L0_ffn_in['bias'], 'L0_ffn_gate_w': _L0_ffn_in['gate_w'], 'L0_ffn_up_w': _L0_ffn_in['up_w'], 'L0_ffn_down_w': _L0_ffn_in['down_w'], 'L0_ffn_sh_gate_w': _L0_ffn_in['sh_gate_w'], 'L0_ffn_sh_up_w': _L0_ffn_in['sh_up_w'], 'L0_ffn_sh_down_w': _L0_ffn_in['sh_down_w']}

def reference(x, ctx_1024, mask_S2_ik0, L0_attn_miu_x, L0_attn_lam, L0_attn_A, L0_attn_Bp, L0_attn_td_miu, L0_attn_tdA, L0_attn_tdB, L0_attn_u, L0_attn_Wk, L0_attn_Wv, L0_attn_Wr, L0_attn_Wo, L0_attn_Wg1, L0_attn_Wg2, L0_attn_gamma, L0_attn_beta, L0_xattn_qkv_w, L0_xattn_proj_w, L0_xattn_proj_b, L0_ffn_router_w, L0_ffn_bias, L0_ffn_gate_w, L0_ffn_up_w, L0_ffn_down_w, L0_ffn_sh_gate_w, L0_ffn_sh_up_w, L0_ffn_sh_down_w):
    import jax
    import jax.numpy as jnp

    def _L0_attn_ref(x, miu_x, lam, A, Bp, td_miu, tdA, tdB, u, Wk, Wv, Wr, Wo, Wg1, Wg2, gamma, beta):
        import jax, jax.numpy as jnp
        import numpy as np
        HEAD = 64

        def wkv6(r, k, v, w, u):
            B, T, C = r.shape
            N = C // HEAD
            shp = lambda a: a.reshape(B, T, N, HEAD).transpose(1, 0, 2, 3)
            rT, kT, vT = (shp(r), shp(k), shp(v))
            dT = jnp.exp(shp(w))
            uu = u[None]

            def step(S, inp):
                rt, kt, vt, dt = inp
                kv = vt[..., :, None] * kt[..., None, :]
                yt = jnp.einsum('bnj,bnij->bni', rt, S + uu[..., None, :] * kv)
                S = S * dt[..., None, :] + kv
                return (S, yt)
            S0 = jnp.zeros((B, N, HEAD, HEAD), r.dtype)
            _, ys = jax.lax.scan(step, S0, (rT, kT, vT, dT))
            return ys.transpose(1, 0, 2, 3).reshape(B, T, C)
        B, T, C = x.shape
        N = C // HEAD
        x_last = jnp.concatenate([jnp.zeros_like(x[:, :1]), x[:, :-1]], axis=1)
        b_a = x_last - x
        xx = x + b_a * miu_x
        h = jnp.tanh(xx @ A).reshape(5, B * T, 32)
        miu = jnp.einsum('smk,skc->smc', h, Bp).reshape(5, B, T, C) + lam
        x5 = x[None] + b_a[None] * miu
        w_in, k_in, v_in, r_in, g_in = (x5[0], x5[1], x5[2], x5[3], x5[4])
        w = td_miu + jnp.tanh(w_in @ tdA) @ tdB
        k = k_in @ Wk.T * jnp.exp(jnp.minimum(w, 0.0))
        v = v_in @ Wv.T
        r = r_in @ Wr.T
        g = jnp.tanh(g_in @ Wg1) @ Wg2
        y = wkv6(r, k, v, w, u)
        yh = y.reshape(B, T, N, HEAD)
        mean = yh.mean(-1, keepdims=True)
        var = yh.var(-1, keepdims=True)
        yn = (yh - mean) / jnp.sqrt(var + 1e-05 * N)
        yn = yn.reshape(B, T, C) * gamma + beta
        return yn * g @ Wo.T

    def _L0_xattn_ref(x, support, attn_mask, qkv_w, proj_w, proj_b):
        import jax, jax.numpy as jnp
        import numpy as np
        DIM = 128
        NUM_HEADS = 8
        SCALE = (DIM // NUM_HEADS) ** (-0.5)
        B, N, C = x.shape
        wq, wk, wv = (qkv_w[:C], qkv_w[C:2 * C], qkv_w[2 * C:])
        q = jnp.einsum('bnc,dc->bnd', x, wq)
        k = jnp.einsum('bmc,dc->bmd', support, wk)
        v = jnp.einsum('bmc,dc->bmd', support, wv)
        attn = jnp.einsum('bnd,bmd->bnm', q, k) * SCALE
        attn = jax.nn.softmax(attn, axis=-1)
        attn = jnp.where(attn_mask[None, None, :] == 0, 0.0, attn)
        out = jnp.einsum('bnm,bmd->bnd', attn, v)
        out = jnp.swapaxes(out, 1, 2).reshape(B, N, C)
        out = jnp.einsum('bnc,dc->bnd', out, proj_w) + proj_b
        return out

    def _L0_ffn_ref(hidden_states, router_w, bias, gate_w, up_w, down_w, sh_gate_w, sh_up_w, sh_down_w):
        import jax, jax.numpy as jnp
        import numpy as np
        B, S, D = (1, 256, 128)
        E, F = (16, 128)
        NG, TKG, K = (4, 2, 4)
        NSH = 2
        SCALE = 2.5
        STD = 0.02
        EPG = E // NG

        def _route(x_flat, router_w, bias):
            logits = x_flat.astype(jnp.float32) @ router_w.T
            scores = jax.nn.sigmoid(logits)
            s = scores + bias[None, :]
            sg = s.reshape(-1, NG, EPG)
            group_score = jax.lax.top_k(sg, 2)[0].sum(-1)
            gidx = jax.lax.top_k(group_score, TKG)[1]
            gmask = jnp.sum(jax.nn.one_hot(gidx, NG, dtype=jnp.float32), axis=1) > 0
            emask = jnp.repeat(gmask, EPG, axis=1)
            masked = jnp.where(emask, s, -1.0)
            topk_idx = jax.lax.top_k(masked, K)[1]
            tw = jnp.take_along_axis(scores, topk_idx, axis=1)
            tw = tw / (tw.sum(-1, keepdims=True) + 1e-20)
            tw = tw * SCALE
            return (topk_idx, tw)
        x = hidden_states.reshape(-1, D)
        topk_idx, tw = _route(x, router_w, bias)
        combine = (jax.nn.one_hot(topk_idx, E, dtype=tw.dtype) * tw[..., None]).sum(1)
        h = jnp.einsum('td,edf->etf', x, gate_w)
        u = jnp.einsum('td,edf->etf', x, up_w)
        y = jnp.einsum('etf,efd->etd', jax.nn.silu(h) * u, down_w)
        routed = jnp.einsum('etd,te->td', y, combine)
        sh = jax.nn.silu(x @ sh_gate_w) * (x @ sh_up_w) @ sh_down_w
        return (routed + sh).reshape(hidden_states.shape)
    x = x + _L0_attn_ref(_layernorm(x, axis=-1), L0_attn_miu_x, L0_attn_lam, L0_attn_A, L0_attn_Bp, L0_attn_td_miu, L0_attn_tdA, L0_attn_tdB, L0_attn_u, L0_attn_Wk, L0_attn_Wv, L0_attn_Wr, L0_attn_Wo, L0_attn_Wg1, L0_attn_Wg2, L0_attn_gamma, L0_attn_beta)
    x = x + _L0_xattn_ref(_layernorm(x, axis=-1), ctx_1024, mask_S2_ik0, L0_xattn_qkv_w, L0_xattn_proj_w, L0_xattn_proj_b)
    x = x + _L0_ffn_ref(_layernorm(x, axis=-1), L0_ffn_router_w, L0_ffn_bias, L0_ffn_gate_w, L0_ffn_up_w, L0_ffn_down_w, L0_ffn_sh_gate_w, L0_ffn_sh_up_w, L0_ffn_sh_down_w)
    return x

_drawn_inputs = setup_inputs


def setup_inputs(seed=0):
    import zlib

    import numpy as np

    out = dict(_drawn_inputs(seed))
    spreads = {'L0_attn_gamma': (1.0, 0.6), 'L0_attn_beta': (0.0, 0.8), 'L0_ffn_bias': (0.0, 0.8)}
    factors = {'L0_attn_miu_x': 8.0,
     'L0_attn_lam': 8.0,
     'L0_attn_A': 8.0,
     'L0_attn_Bp': 8.0,
     'L0_attn_td_miu': 8.0,
     'L0_attn_tdA': 8.0,
     'L0_attn_tdB': 8.0,
     'L0_attn_u': 8.0,
     'L0_attn_Wk': 8.0,
     'L0_attn_Wv': 8.0,
     'L0_attn_Wr': 8.0,
     'L0_attn_Wo': 8.0,
     'L0_attn_Wg1': 8.0,
     'L0_attn_Wg2': 8.0,
     'L0_xattn_proj_b': 4.894,
     'L0_ffn_router_w': 8.0,
     'L0_ffn_gate_w': 7.874,
     'L0_ffn_up_w': 7.801,
     'L0_ffn_down_w': 7.845,
     'L0_ffn_sh_gate_w': 7.019,
     'L0_ffn_sh_up_w': 6.925,
     'L0_ffn_sh_down_w': 6.938}
    for name, (base, spread) in spreads.items():
        noise = np.random.default_rng([zlib.crc32(name.encode()), seed]).standard_normal(out[name].shape)
        drawn = base * np.exp(spread * noise) if base else spread * noise
        out[name] = jnp.asarray(drawn.astype(out[name].dtype))
    for name, factor in factors.items():
        out[name] = (out[name] * factor).astype(out[name].dtype)
    return out
```

```python
from contextlib import ExitStack

import numpy as np
import concourse.bass as bass
from concourse import mybir

F32 = mybir.dt.float32
F32R = mybir.dt.float32r
I32 = mybir.dt.int32
ALU = mybir.AluOpType
ACT = mybir.ActivationFunctionType
X = mybir.AxisListType.X

P = 128
B = 8
S = 256
M = 512
C = 128
T = B * S
NT = T // P
CH = 512
NCH = T // CH
HD = 64
NH = C // HD
NS = 5
LR = 32
GR = 160
TDR = 64
E = 16
EX = E + 2
NG = 4
EPG = E // NG
TOPG = 2
TOPK = 4
SCALE_TW = 2.5
WB = 3
LEVELS = 8
MASKED = 6
SCALE_QK = 0.25

PACK = {}
_at = 0
for _name, _n in (("A", GR), ("tdA", TDR), ("WkT", C), ("WvT", C), ("WrT", C), ("WoT", C), ("Wg1", GR),
                  ("Wg2a", C), ("wq", C), ("wk", C), ("xvT", C), ("pwT", C), ("rT", E), ("tdB", C),
                  ("Wg2b", C), ("ident", P), ("cols", 10), ("hsel", NH), ("mask", M // P)):
    PACK[_name] = (_at, _n)
    _at += _n
NPACK = _at
COL = {n: i for i, n in enumerate(("miu_x", "lam0", "lam1", "lam2", "lam3", "lam4", "td_miu", "u", "gamma", "beta"))}


CREDIT = 5


def after(n):
    return n + CREDIT


def bc(ap, shape):
    return ap.unsqueeze(len(shape) - 1).to_broadcast(shape)


def decoder_layer(nc, x_d, pack_d, bp_d, ctx_d, ctxT_d, rows_d, maskc_d, lvl_d, wffn_d, tri_d, out_d, tw_d):
    x_v = x_d.rearrange("b (p h) c -> p b (h c)", h=2)
    out_v = out_d.rearrange("b (p h) c -> p b (h c)", h=2)

    with ExitStack() as stack:
        scope = [stack]

        def sb(name, shape, dt=F32):
            return scope[-1].enter_context(nc.sbuf_tensor(name, shape, dt))

        producers = {}

        def sem(name, eng=None):
            s = stack.enter_context(nc.semaphore(name))
            if eng:
                producers.setdefault(eng, []).append(s)
            return s

        bank = [stack.enter_context(nc.psum_tensor(f"bank{i}", [P, 512], F32)) for i in range(8)]

        xtok = sb("xtok", [P, NT, C])
        pack = sb("pack", [P, NPACK])
        W = {n: pack[:, o:o + w] for n, (o, w) in PACK.items()}
        col = {n: W["cols"][:, i:i + 1] for n, i in COL.items()}
        ident = W["ident"]
        bp = sb("bp", [LR, NS * C])
        pb_row = sb("pb_row", [P, C])
        bias_row = sb("bias_row", [P, E])
        mask_i = sb("mask_i", [P, M // P], I32)
        mask = sb("mask", [P, M // P])
        lvl = sb("lvl", [P, MASKED, HD], I32)
        tri = sb("tri", [P, NG * NG])
        seg = sb("seg", [P, E])
        neghalf = sb("neghalf", [P, 16])
        ctxn = sb("ctxn", [P, B * (M // P), C])
        ctxT = sb("ctxT", [C, B * M])
        stat = {n: sb("st_" + n, [P, NT]) for n in ("sum", "mean", "var", "ve", "rstd")}
        zero_r = sb("zero_r", [P, CH], F32R)
        one_r = sb("one_r", [2, P], F32R)
        xc = sb("xc", [P, NT, C])
        sq = sb("sq", [P, NT, C])
        xn = sq
        scope.append(ExitStack())
        xTp = sb("xTp", [C, B, S + 1])
        bA = sb("bA", [C, B, S])
        xx = sb("xx", [C, CH])
        HF = sb("HF", [LR, NS * T])
        tmp_s = sb("tmp_s", [C, 2, CH])
        xs = sb("xs", [C, NS, CH])
        w1 = sb("w1", [TDR, CH])
        dec = sb("dec", [C, T])
        kq = sb("kq", [C, T])
        kqc = sb("kqc", [C, 2, S])
        rpc = xx[:].rearrange("p (q t) -> p q t", q=2)
        rp = sb("rp", [C, T])
        vv = sb("vv", [P, NT, C])
        gT = sb("gT", [C, T])
        g1a = sb("g1a", [P, CH])
        g1b = sb("g1b", [LR, CH])
        ruk = sb("ruk", [C, CH])
        dsum = sb("dsum", [P, NT, NH])
        tot = [None] + [sb(f"tot{j}", [C, 2, S >> j]) for j in range(1, LEVELS - 1)]
        at = sb("at", [P, 2, NH, 2, P])
        at2 = sb("at2", [P, 2, NH, P])
        yc = sb("yc", [P, 8, HD])
        gstat = {n: sb("gs_" + n, [P, 8]) for n in ("sum", "mean", "var", "ve", "rstd")}
        yxc = yc
        ysq = sb("ysq", [P, 8, HD])
        yn = ysq
        z1 = sb("z1", [C, CH])
        z = z1
        scope.pop().close()
        mqk = sb("mqk", [C, C])
        xT2 = sb("xT2", [C, T])
        q2 = sb("q2", [C, 2, S])
        nmax = sb("nmax", [P, 4])
        psum_ = sb("psums", [P, 4])
        rsum = sb("rsum", [P, 4])
        pr = sb("pr", [P, 4, M])
        pt = sb("pt", [P, 2, M // P, P])
        pcs = sb("pcs", [P, 2, C])
        t1s = sb("t1s", [C, 2 * C])
        xpb = sb("xpb", [P, NT, C])
        xh = sb("xh", [C, T], F32R)
        xl = sb("xl", [C, T], F32R)
        rth = sb("rth", [C, E], F32R)
        rtl = sb("rtl", [C, E], F32R)
        R = {n: sb("r_" + n, [P, NT, E]) for n in ("e", "e1", "sc", "s", "m", "gt", "eq", "cum", "le", "sel", "tw")}
        pair = sb("pair", [P, NT * NG, 6])
        gs = sb("gsc", [P, NT * NG])
        ggt = sb("ggt", [P, NT, NG * NG])
        geq = sb("geq", [P, NT, NG * NG])
        grk = sb("grk", [P, NT * NG])
        gm = sb("gm", [P, NT * NG])
        gm1 = sb("gm1", [P, NT * NG])
        top8 = sb("top8", [P, NT, 8])
        ngt = sb("ngt", [P, NT])
        tws = sb("tws", [P, NT])
        twr = sb("twr", [P, NT])
        combT = sb("combT", [EX, T])
        combh = sb("combh", [EX, T], F32R)
        combl = sb("combl", [EX, T], F32R)
        wf = sb("wf", [P, WB, 3 * C])
        wfh = sb("wfh", [P, WB, 3 * C], F32R)
        wfl = sb("wfl", [P, WB, 3 * C], F32R)
        twrow = sb("twrow", [2, WB, 2 * CH], F32R)
        sg = sb("sg", [P, 2, CH])
        stw = sb("stw", [P, 2, CH])
        aa = sb("aa", [P, 2, CH])
        ah = sb("ah", [P, 2, CH], F32R)
        al = sb("al", [P, 2, CH], F32R)
        yTs = pr[:, 0:2, :]

        d_x, d_w, d_ctx, d_small = sem("d_x"), sem("d_w"), sem("d_ctx"), sem("d_small")
        d_tw, d_out = sem("d_tw"), sem("d_out")
        d_wf = [sem(f"d_wf{i}") for i in range(WB)]
        init_v, init_p = sem("init_v", "dve"), sem("init_p", "pool")
        ln_sum, ln_mean, ln_xc, ln_var, ln_xn = (sem(n, "dve") for n in ("ln_sum", "ln_mean", "ln_xc", "ln_var", "ln_xn"))
        ln_sq = sem("ln_sq", "act")
        ln_ve, ln_rstd = sem("ln_ve", "pool"), sem("ln_rstd", "pool")
        tr = sem("tr", "pe")
        tr_act, tr_dve = sem("tr_act", "act"), sem("tr_dve", "dve")
        ba_done, xx_done = sem("ba_done", "dve"), sem("xx_done", "dve")
        h_pe, h_act = sem("h_pe", "pe"), sem("h_act", "act")
        miu_pe, miu_t, xs_done = sem("miu_pe", "pe"), sem("miu_t", "dve"), sem("xs_done", "pool")
        w1_pe, w1_act, w2_pe, dec_done = sem("w1_pe", "pe"), sem("w1_act", "act"), sem("w2_pe", "pe"), sem("dec_done", "act")
        k_pe, k_done = sem("k_pe", "pe"), sem("k_done", "dve")
        v_pe, v_done = sem("v_pe", "pe"), sem("v_done", "act")
        r_pe, r_done = sem("r_pe", "pe"), sem("r_done", "act")
        ruk_done, ds_pe, ds_done = sem("ruk_done", "dve"), sem("ds_pe", "pe"), sem("ds_done", "act")
        g1_pe, g1_act, g_pe, g_done = sem("g1_pe", "pe"), sem("g1_act", "act"), sem("g_pe", "pe"), sem("g_done", "act")
        lv = [sem(f"lv{q}", "pe") for q in range(2)]
        lv_at = [sem(f"lv_at{q}", "dve") for q in range(2)]
        lv_act = [sem(f"lv_act{q}", "act") for q in range(2)]
        rp_up = [sem(f"rp_up{q}", "dve") for q in range(2)]
        rp_in = sem("rp_in", "act")
        kq_in = sem("kq_in", "pool")
        kq_up = [sem(f"kq_up{q}", "pool") for q in range(2)]
        tot_up = [sem(f"tot_up{q}", "pool") for q in range(2)]
        y_pe, y_done = sem("y_pe", "pe"), sem("y_done", "dve")
        gn_sum, gn_mean, gn_xc, gn_var, gn_yn = (sem(n, "dve") for n in ("gn_sum", "gn_mean", "gn_xc", "gn_var", "gn_yn"))
        gn_sq = sem("gn_sq", "act")
        gn_ve, gn_rstd = sem("gn_ve", "pool"), sem("gn_rstd", "pool")
        yt_pe, z1_done, z_done = sem("yt_pe", "pe"), sem("z1_done", "dve"), sem("z_done", "pool")
        wo_pe, x1_done = sem("wo_pe", "pe"), sem("x1_done", "dve")
        m_pe, m_act = sem("m_pe", "pe"), sem("m_act", "act")
        q_pe, q_act = sem("q_pe", "pe"), sem("q_act", "act")
        s_pe, mx_done, ex_done = sem("s_pe", "pe"), sem("mx_done", "dve"), sem("ex_done", "act")
        rs_done = sem("rs_done", "dve")
        pt_pe, pt_done = sem("pt_pe", "pe"), sem("pt_done", "dve")
        pc_pe, pc_done = sem("pc_pe", "pe"), sem("pc_done", "act")
        t1_pe, t1_done = sem("t1_pe", "pe"), sem("t1_done", "act")
        fin_pe, x2_done = sem("fin_pe", "pe"), sem("x2_done", "dve")
        xpb_done = sem("xpb_done", "pool")
        lg_pe, lg_act = sem("lg_pe", "pe"), sem("lg_act", "act")
        chain = sem("chain", "dve")
        ct_pe, ct_act, ch_done, cl_done = sem("ct_pe", "pe"), sem("ct_act", "act"), sem("ch_done", "act"), sem("cl_done", "dve")
        wfh_done, wfl_done = sem("wfh_done", "pool"), sem("wfl_done", "pool")
        h2_pe, u2_pe, tw_pe = sem("h2_pe", "pe"), sem("u2_pe", "pe"), sem("tw_pe", "pe")
        sg_done, stw_done, aa_done = sem("sg_done", "act"), sem("stw_done", "dve"), sem("aa_done", "dve")
        ah_done, al_done = sem("ah_done", "act"), sem("al_done", "dve")
        y2_pe, yacc_pe = sem("y2_pe", "pe"), sem("yacc_pe", "pe")
        yts_done, yo_pe, out_done = sem("yts_done", "act"), sem("yo_pe", "pe"), sem("out_done", "dve")

        carrier = {n: sem("carrier_" + n) for n in ("pool", "dve", "pe")}

        block = stack.enter_context(nc.Block())

        def credit(eng, name):
            for s in producers[name]:
                eng.sem_inc(s, CREDIT)

        def carry(eng, which):
            eng.sem_inc(carrier[which], 1)

        @block.sync
        def _(sp):
            sp.dma_start(xtok[:].rearrange("p (b h) c -> p b (h c)", h=2), x_v).then_inc(d_x, 16)
            sp.dma_start(pack[:], pack_d).then_inc(d_w, 16)
            sp.dma_start(bp[:], bp_d).then_inc(d_w, 16)
            sp.dma_start(lvl[:], lvl_d).then_inc(d_small, 16)
            sp.dma_start(tri[:], tri_d[:, 0:NG * NG]).then_inc(d_small, 16)
            sp.dma_start(seg[:], tri_d[:, NG * NG:NG * NG + E]).then_inc(d_small, 16)
            sp.dma_start(mask_i[:], maskc_d).then_inc(d_small, 16)
            sp.dma_start(pb_row[:], rows_d[0:C].unsqueeze(0).to_broadcast([P, C])).then_inc(d_small, 16)
            sp.dma_start(bias_row[:], rows_d[C:C + E].unsqueeze(0).to_broadcast([P, E])).then_inc(d_small, 16)
            sp.dma_start(ctxT[:], ctxT_d).then_inc(d_ctx, 16)
            sp.dma_start(ctxn[:], ctx_d).then_inc(d_ctx, 16)
            sp.wait_ge(ch_done, after(1))
            sp.dma_start(tw_d[:, 0, :], combh[:].bitcast(F32)).then_inc(d_tw, 16)
            sp.wait_ge(cl_done, after(1))
            sp.dma_start(tw_d[:, 1, :], combl[:].bitcast(F32)).then_inc(d_tw, 16)
            sp.wait_ge(d_tw, 32)

            def load_expert(hf, e, par):
                sp.dma_start(wf[:, par, :], wffn_d[bass.ds(e, 1), :, :].rearrange("o p n -> (o p) n")).then_inc(d_wf[par], 16)
                sp.dma_start(twrow[:, par, :].bitcast(F32), tw_d[bass.ds(e, 1), :, bass.ds(hf * 2 * CH, 2 * CH)]
                             .rearrange("o k n -> (o k) n")).then_inc(d_wf[par], 16)

            with sp.Fori(0, 2) as hf:
                with sp.Fori(0, EX // WB) as turn:
                    for par in range(WB):
                        n = hf * EX + turn * WB + par
                        sp.wait_ge(wfl_done, after(n) - (WB - 1))
                        sp.wait_ge(tw_pe, 2 * n + after(0) - 2 * (WB - 1))
                        load_expert(hf, turn * WB + par, par)
            for hf in range(2):
                sp.wait_ge(out_done, after(2 * (hf + 1)))
                sp.dma_start(out_v[:, 4 * hf:4 * hf + 4, :],
                             xtok[:, 8 * hf:8 * hf + 8, :].rearrange("p (b h) c -> p b (h c)", h=2)).then_inc(d_out, 16)
            sp.wait_ge(d_out, 32)

        @block.gpsimd
        def _(pool):
            credit(pool, "pool")
            g = nc.gpsimd
            g.memset(neghalf[:], -0.5).then_inc(init_p, 1)
            g.memset(xTp[:], 0.0).then_inc(init_p, 1)
            g.memset(at[:], 0.0).then_inc(init_p, 1)
            pool.wait_ge(init_p, after(3))

            def norm_rstd(k):
                pool.wait_ge(ln_var, after(k + 1))
                g.tensor_scalar(stat["ve"][:], stat["var"][:], 1.0 / C, 1e-5, ALU.mult, ALU.add).then_inc(ln_ve, 1)
                pool.wait_ge(ln_ve, after(k + 1))
                g.tensor_tensor(stat["rstd"][:], stat["ve"][:], neghalf[:], ALU.pow).then_inc(ln_rstd, 1)

            norm_rstd(0)
            with pool.Fori(0, NCH) as c:
                for s in range(NS):
                    pool.wait_ge(miu_t, c * NS + after(s + 1))
                    if s == 0:
                        pool.wait_ge(g_pe, c + after(0))
                    carry(pool, "pool")
                    g.tensor_tensor(xs[:, s, :].rearrange("p (b t) -> p b t", b=2), tmp_s[:, s % 2, :].rearrange("p (b t) -> p b t", b=2),
                                    xTp[:, bass.ds(c * 2, 2), 1:S + 1], ALU.add).then_inc(xs_done, 1)
            with pool.Fori(0, NCH) as c:
                pool.wait_ge(k_done, c + after(1))
                for q in range(2):
                    pool.wait_ge(lv[q], c * LEVELS + after(0))
                g.tensor_copy(kqc[:], kq[:, bass.ds(c * CH, CH)].rearrange("p (q t) -> p q t", q=2)).then_inc(kq_in, 1)
                pool.wait_ge(kq_in, c + after(1))
                for j in range(LEVELS - 1):
                    h = 1 << j
                    for q in range(2):
                        def t_of(lev):
                            if lev == 0:
                                return dec[:, bass.ds(c * CH + q * S, S)]
                            return tot[lev][:, q, :]
                        kqv = kqc[:, q, :].rearrange("p (n two h) -> p n two h", two=2, h=h)
                        tv = t_of(j).rearrange("p (n two) -> p n two", two=2)
                        pool.wait_ge(lv[q], c * LEVELS + after(j + 1))
                        if j > 0:
                            pool.wait_ge(tot_up[q], c * (LEVELS - 2) + after(j))
                            pool.wait_ge(kq_up[q], c * (LEVELS - 1) + after(j))
                        g.tensor_tensor(kqv[:, :, 0, :], kqv[:, :, 0, :], bc(tv[:, :, 1], [P, S // 2 // h, h]), ALU.mult).then_inc(kq_up[q], 1)
                        if j < LEVELS - 2:
                            pool.wait_ge(rp_up[q], c * (LEVELS - 1) + after(0))
                            g.tensor_tensor(tot[j + 1][:, q, :], tv[:, :, 0], tv[:, :, 1], ALU.mult).then_inc(tot_up[q], 1)
                pool.wait_ge(gn_var, c + after(1))
                carry(pool, "pool")
                g.tensor_scalar(gstat["ve"][:], gstat["var"][:], 1.0 / HD, 1e-5 * NH, ALU.mult, ALU.add).then_inc(gn_ve, 1)
                pool.wait_ge(gn_ve, c + after(1))
                g.tensor_tensor(gstat["rstd"][:], gstat["ve"][:], neghalf[:, 0:8], ALU.pow).then_inc(gn_rstd, 1)
                pool.wait_ge(z1_done, c + after(1))
                pool.wait_ge(wo_pe, c + after(0))
                g.tensor_tensor(z[:], z1[:], gT[:, bass.ds(c * CH, CH)], ALU.mult).then_inc(z_done, 1)
            norm_rstd(1)
            pool.wait_ge(d_small, 96)
            g.tensor_tensor(xpb[:], xtok[:], pb_row[:].unsqueeze(1).to_broadcast([P, NT, C]), ALU.add).then_inc(xpb_done, 1)
            norm_rstd(2)
            with pool.Fori(0, 2) as hf:
                with pool.Fori(0, EX // WB) as turn:
                    for par in range(WB):
                        n = hf * EX + turn * WB + par
                        pool.wait_ge(d_wf[par], (hf * (EX // WB) + turn) * 32 + 32)
                        pool.wait_ge(y2_pe, 2 * n + after(0) - 2 * (WB - 1))
                        carry(pool, "pool")
                        g.tensor_copy(wfh[:, par, :], wf[:, par, :]).then_inc(wfh_done, 1)
                        pool.wait_ge(wfh_done, n + after(1))
                        g.tensor_tensor(wfl[:, par, :], wf[:, par, :], wfh[:, par, :].bitcast(F32), ALU.subtract).then_inc(wfl_done, 1)

        @block.scalar
        def _(act):
            a = nc.scalar
            credit(act, "act")

            def norm_sq(k):
                act.wait_ge(ln_xc, after(k + 1))
                a.activation(sq[:], xc[:], ACT.Square).then_inc(ln_sq, 1)

            act.preload_act_table(ACT.Exp)
            norm_sq(0)
            with act.Fori(0, NCH) as c:
                act.wait_ge(tr, c + after(1))
                act.wait_ge(init_p, after(3))
                for q in range(2):
                    src = bank[0][:, q * S:(q + 1) * S].rearrange("p (h j) -> p h j", h=2)
                    dst = xTp[:, bass.ds(c * 2 + q, 1), 1:S + 1].rearrange("p o (j h) -> p (o h) j", h=2)
                    last = a.activation(dst, src, ACT.Copy)
                last.then_inc(tr_act, 1)
                act.wait_ge(h_pe, c + after(1))
                hfv = HF[:, bass.ds(c * CH * NS, CH * NS)].rearrange("p (t i) -> p t i", i=NS)
                for i in range(NS):
                    src = bank[1][LR * i:LR * (i + 1), :] if i < 4 else bank[2][0:LR, :]
                    last = a.activation(hfv[:, :, i], src, ACT.Tanh)
                last.then_inc(h_act, 1)
            with act.Fori(0, NCH) as c:
                cs = bass.ds(c * CH, CH)
                act.wait_ge(w1_pe, c + after(1))
                act.wait_ge(w2_pe, c + after(0))
                a.activation(w1[:], bank[2][0:TDR, :], ACT.Tanh).then_inc(w1_act, 1)
                act.wait_ge(w2_pe, c + after(1))
                a.activation(dec[:, cs], bank[3][:], ACT.Exp, bias=col["td_miu"]).then_inc(dec_done, 1)
                act.wait_ge(v_pe, c + after(1))
                a.activation(vv[:, bass.ds(c * 4, 4), :], bank[5][:].rearrange("p (i n) -> p i n", i=4), ACT.Copy).then_inc(v_done, 1)
                act.wait_ge(r_pe, c + after(1))
                a.activation(rp[:, cs], bank[6][:], ACT.Copy).then_inc(r_done, 1)
                act.wait_ge(g1_pe, c + after(1))
                act.wait_ge(g_pe, c + after(0))
                a.activation(g1a[:], bank[2][:], ACT.Tanh)
                a.activation(g1b[:], bank[7][0:LR, :], ACT.Tanh).then_inc(g1_act, 1)
                act.wait_ge(g_pe, c + after(1))
                a.activation(gT[:, cs], bank[3][:], ACT.Copy).then_inc(g_done, 1)
                act.wait_ge(ds_pe, c + after(1))
                a.activation(dsum[:, bass.ds(c * 4, 4), :], bank[7][:, 0:4 * NH].rearrange("p (i n) -> p i n", i=4), ACT.Copy).then_inc(ds_done, 1)
            with act.Fori(0, NCH) as c:
                act.wait_ge(r_done, after(NCH))
                for q in range(2):
                    act.wait_ge(lv[q], c * LEVELS + after(0))
                    act.wait_ge(rp_up[q], c * (LEVELS - 1) + after(0))
                a.activation(rpc, rp[:, bass.ds(c * CH, CH)].rearrange("p (q t) -> p q t", q=2), ACT.Copy).then_inc(rp_in, 1)
                for q in range(2):
                    act.wait_ge(lv[q], c * LEVELS + after(7))
                    act.wait_ge(lv_at[q], c * MASKED + after(MASKED))
                    act.wait_ge(y_pe, c * 2 + after(0))
                    for hd in range(NH):
                        src = bank[2 * q + hd][0:HD, 0:2 * HD].rearrange("p (k t) -> p k t", k=2)
                        last = a.activation(at[0:HD, q, hd, :, HD:P], src, ACT.Copy)
                    last.then_inc(lv_act[q], 1)
                for q in range(2):
                    act.wait_ge(lv[q], c * LEVELS + after(8))
                    for hd in range(NH):
                        last = a.activation(at2[:, q, hd, :], bank[4 + 2 * q + hd][:, 0:P], ACT.Copy)
                    last.then_inc(lv_act[q], 1)
                act.wait_ge(gn_xc, c + after(1))
                a.activation(ysq[:], yxc[:], ACT.Square).then_inc(gn_sq, 1)
            act.wait_ge(m_pe, after(1))
            a.activation(mqk[:], bank[0][:, 0:C], ACT.Copy).then_inc(m_act, 1)
            norm_sq(1)
            with act.Fori(0, NCH) as c:
                act.wait_ge(tr, c + after(NCH + 1))
                for q in range(2):
                    src = bank[0][:, q * S:(q + 1) * S].rearrange("p (h j) -> p h j", h=2)
                    dst = xT2[:, bass.ds(c * CH + q * S, S)].rearrange("p (j h) -> p h j", h=2)
                    last = a.activation(dst, src, ACT.Copy)
                last.then_inc(tr_act, 1)

            def q_copy(b, par):
                act.wait_ge(q_pe, b + after(1))
                a.activation(q2[:, par, :], bank[4][:, 0:S], ACT.Copy, scale=SCALE_QK).then_inc(q_act, 1)

            def x_rest(b, par):
                for i in range(2):
                    k = 2 * par + i
                    act.wait_ge(mx_done, 2 * b + after(i + 1))
                    a.activation(pr[:, k, :], bank[k][:], ACT.Exp, bias=nmax[:, k:k + 1],
                                 accum_out=psum_[:, k:k + 1]).then_inc(ex_done, 1)
                for i in range(2):
                    act.wait_ge(pc_pe, 2 * b + after(2))
                    act.wait_ge(rs_done, 2 * b + after(i + 1))
                    if i == 0:
                        act.wait_ge(t1_pe, b + after(0))
                    a.activation(pcs[:, i, :], bank[7][:, i * C:(i + 1) * C], ACT.Copy, scale=rsum[:, 2 * par + i:2 * par + i + 1]).then_inc(pc_done, 1)
                act.wait_ge(t1_pe, b + after(1))
                act.wait_ge(fin_pe, b + after(0))
                a.activation(t1s[:], bank[7][:, 256:512], ACT.Copy).then_inc(t1_done, 1)

            q_copy(0, 0)
            with act.Fori(0, B // 2 - 1) as bp2:
                for par in range(2):
                    q_copy(bp2 * 2 + par + 1, 1 - par)
                    x_rest(bp2 * 2 + par, par)
            q_copy(B - 1, 1)
            x_rest(B - 2, 0)
            x_rest(B - 1, 1)
            a.activation(rth[:], W["rT"], ACT.Copy).then_inc(lg_act, 1)
            norm_sq(2)
            with act.Fori(0, NCH) as c:
                act.wait_ge(tr, c + after(2 * NCH + 1))
                a.activation(xh[:, bass.ds(c * CH, CH)], bank[0][:], ACT.Copy).then_inc(tr_act, 1)
            act.wait_ge(lg_pe, after(1))
            a.activation(R["e"][:], bank[1][:, 0:NT * E].rearrange("p (t e) -> p t e", t=NT), ACT.Exp, scale=-1.0).then_inc(lg_act, 1)
            for k in range(4):
                act.wait_ge(ct_pe, after(k + 1))
                if k == 0:
                    act.wait_ge(init_v, after(4))
                a.activation(combT[0:E, k * CH:(k + 1) * CH], bank[2 + k][0:E, :], ACT.Copy).then_inc(ct_act, 1)
            act.preload_act_table(ACT.Silu)
            act.wait_ge(ct_act, after(4))
            a.activation(combh[:], combT[:], ACT.Copy).then_inc(ch_done, 1)

            def silu_of(n, cc):
                act.wait_ge(h2_pe, n + after(1))
                act.wait_ge(stw_done, n + after(0) - 1)
                a.activation(sg[:, cc, :], bank[2 + cc][:], ACT.Silu).then_inc(sg_done, 1)

            def high_of(n, cc):
                act.wait_ge(aa_done, n + after(1))
                act.wait_ge(y2_pe, n + after(0) - 1)
                a.activation(ah[:, cc, :], aa[:, cc, :], ACT.Copy).then_inc(ah_done, 1)

            with act.Fori(0, 2) as hf:
                silu_of(hf * (2 * EX), 0)
                silu_of(hf * (2 * EX) + 1, 1)
                high_of(hf * (2 * EX), 0)
                with act.Fori(1, EX) as e:
                    for cc in range(2):
                        n = hf * (2 * EX) + e * 2 + cc
                        silu_of(n, cc)
                        high_of(n - 1, 1 - cc)
                high_of(hf * (2 * EX) + (2 * EX - 1), 1)
                for cc in range(2):
                    act.wait_ge(yacc_pe, hf + after(1))
                    act.wait_ge(yo_pe, hf * 2 + after(0))
                    a.activation(yTs[:, cc, :], bank[cc][:], ACT.Copy).then_inc(yts_done, 1)

        @block.vector
        def _(dve):
            v = nc.vector
            credit(dve, "dve")
            v.memset(zero_r[:].bitcast(F32), 0.0).then_inc(init_v, 1)
            v.memset(one_r[:].bitcast(F32), 1.0).then_inc(init_v, 1)
            dve.wait_ge(d_small, 96)
            v.tensor_scalar(mask[:], mask_i[:], 0.0, None, ALU.not_equal).then_inc(init_v, 1)

            def norm(k):
                v.tensor_reduce(stat["sum"][:], xtok[:], X, ALU.add).then_inc(ln_sum, 1)
                dve.wait_ge(ln_sum, after(k + 1))
                v.tensor_scalar(stat["mean"][:], stat["sum"][:], 1.0 / C, None, ALU.mult).then_inc(ln_mean, 1)
                dve.wait_ge(ln_mean, after(k + 1))
                v.tensor_tensor(xc[:], xtok[:], bc(stat["mean"][:], [P, NT, C]), ALU.subtract).then_inc(ln_xc, 1)
                dve.wait_ge(ln_sq, after(k + 1))
                v.tensor_reduce(stat["var"][:], sq[:], X, ALU.add).then_inc(ln_var, 1)
                dve.wait_ge(ln_rstd, after(k + 1))
                dve.wait_ge(ln_xc, after(k + 1))
                v.tensor_tensor(xn[:], xc[:], bc(stat["rstd"][:], [P, NT, C]), ALU.mult).then_inc(ln_xn, 1)

            dve.wait_ge(d_x, 16)
            norm(0)
            dve.wait_ge(d_w, 32)
            with dve.Fori(0, NCH) as c:
                two = bass.ds(c * 2, 2)
                dve.wait_ge(tr_act, c + after(1))
                v.tensor_tensor(bA[:, two, :], xTp[:, two, 0:S], xTp[:, two, 1:S + 1], ALU.subtract).then_inc(ba_done, 1)
                dve.wait_ge(ba_done, c + after(1))
                dve.wait_ge(h_pe, c + after(0))
                v.scalar_tensor_tensor(xx[:].rearrange("p (b t) -> p b t", b=2), bA[:, two, :], col["miu_x"], xTp[:, two, 1:S + 1],
                                       ALU.mult, ALU.add).then_inc(xx_done, 1)
            with dve.Fori(0, NCH) as c:
                two = bass.ds(c * 2, 2)
                cs = bass.ds(c * CH, CH)

                def shift(s):
                    dve.wait_ge(miu_pe, c * NS + after(s + 1))
                    dve.wait_ge(xs_done, c * NS + after(s) - 1)
                    v.scalar_tensor_tensor(tmp_s[:, s % 2, :].rearrange("p (b t) -> p b t", b=2),
                                           bank[s % 2][:].rearrange("p (b t) -> p b t", b=2), col[f"lam{s}"],
                                           bA[:, two, :], ALU.add, ALU.mult).then_inc(miu_t, 1)
                shift(0)
                shift(1)
                shift(2)
                shift(3)
                dve.wait_ge(k_pe, c + after(1))
                dve.wait_ge(dec_done, c + after(1))
                v.scalar_tensor_tensor(kq[:, cs], dec[:, cs], 1.0, bank[4][:], ALU.min, ALU.mult).then_inc(k_done, 1)
                shift(4)
                dve.wait_ge(r_done, c + after(1))
                dve.wait_ge(k_done, c + after(1))
                dve.wait_ge(ds_pe, c + after(0))
                v.scalar_tensor_tensor(ruk[:], rp[:, cs], col["u"], kq[:, cs], ALU.mult, ALU.mult).then_inc(ruk_done, 1)
            with dve.Fori(0, NCH) as c:
                for j in range(LEVELS - 1):
                    h = 1 << j
                    for q in range(2):
                        dve.wait_ge(lv[q], c * LEVELS + after(j + 1))
                        if 0 < j < MASKED:
                            dve.wait_ge(lv_at[q], c * MASKED + after(j))
                        rpv = rpc[:, q, :].rearrange("p (n two h) -> p n two h", two=2, h=h)
                        if j == 0:
                            tv = dec[:, bass.ds(c * CH + q * S, S)].rearrange("p (n two) -> p n two", two=2)
                        else:
                            tv = tot[j][:, q, :].rearrange("p (n two) -> p n two", two=2)
                            dve.wait_ge(tot_up[q], c * (LEVELS - 2) + after(j))
                            dve.wait_ge(rp_up[q], c * (LEVELS - 1) + after(j))
                        v.tensor_tensor(rpv[:, :, 1, :], rpv[:, :, 1, :], bc(tv[:, :, 0], [P, S // 2 // h, h]), ALU.mult).then_inc(rp_up[q], 1)
                        if j >= MASKED:
                            continue
                        if j == 0:
                            dve.wait_ge(y_pe, c * 2 + after(0))
                            carry(dve, "dve")
                            dve.wait_ge(init_p, after(3))
                            dve.wait_ge(d_small, 96)
                        n = P // (2 * h)
                        for hd in range(NH):
                            dst = at[:, q, hd, :, :].rearrange("p k (n two h) -> p k n two h", two=2, h=h)[:, :, :, 1, :]
                            src = bank[4 * (j % 2) + 2 * q + hd][:, 0:P].rearrange("p (k n h) -> p k n h", k=2, h=h)
                            msk = lvl[:, j, :].rearrange("p (n h) -> p n h", h=h).unsqueeze(1).to_broadcast([P, 2, n, h])
                            last = v.copy_predicated(dst, msk, src)
                        last.then_inc(lv_at[q], 1)
                for q in range(2):
                    dve.wait_ge(y_pe, c * 2 + after(q + 1))
                    if q == 0:
                        dve.wait_ge(gn_yn, c + after(0))
                    for k in range(2):
                        for hd in range(NH):
                            i = (q * 2 + k) * 2 + hd
                            tile = bass.ds(c * 4 + q * 2 + k, 1)
                            last = v.scalar_tensor_tensor(yc[:, i, :], vv[:, tile, hd * HD:(hd + 1) * HD].rearrange("p o n -> p (o n)"),
                                                          dsum[:, tile, hd:hd + 1].rearrange("p o n -> p (o n)"),
                                                          bank[q][:, (2 * k + hd) * HD:(2 * k + hd + 1) * HD], ALU.mult, ALU.add)
                    last.then_inc(y_done, 1)
                dve.wait_ge(y_done, c * 2 + after(2))
                v.tensor_reduce(gstat["sum"][:], yc[:], X, ALU.add).then_inc(gn_sum, 1)
                dve.wait_ge(gn_sum, c + after(1))
                v.tensor_scalar(gstat["mean"][:], gstat["sum"][:], 1.0 / HD, None, ALU.mult).then_inc(gn_mean, 1)
                dve.wait_ge(gn_mean, c + after(1))
                v.tensor_tensor(yxc[:], yc[:], bc(gstat["mean"][:], [P, 8, HD]), ALU.subtract).then_inc(gn_xc, 1)
                dve.wait_ge(gn_sq, c + after(1))
                v.tensor_reduce(gstat["var"][:], ysq[:], X, ALU.add).then_inc(gn_var, 1)
                dve.wait_ge(gn_rstd, c + after(1))
                dve.wait_ge(gn_xc, c + after(1))
                dve.wait_ge(yt_pe, c + after(0))
                v.tensor_tensor(yn[:], yxc[:], bc(gstat["rstd"][:], [P, 8, HD]), ALU.mult).then_inc(gn_yn, 1)
                dve.wait_ge(yt_pe, c + after(1))
                dve.wait_ge(z_done, c + after(0))
                v.tensor_scalar(z1[:], bank[2][:], col["gamma"], col["beta"], ALU.mult, ALU.add).then_inc(z1_done, 1)
                dve.wait_ge(wo_pe, c + after(1))
                xt4 = xtok[:, bass.ds(c * 4, 4), :]
                v.tensor_tensor(xt4, xt4, bank[3][:].rearrange("p (i n) -> p i n", i=4), ALU.add).then_inc(x1_done, 1)
            dve.wait_ge(x1_done, after(NCH))
            norm(1)

            def x_max(b, par):
                for i in range(2):
                    k = 2 * par + i
                    dve.wait_ge(s_pe, 2 * b + after(i + 1))
                    v.tensor_reduce(nmax[:, k:k + 1], bank[k][:], X, ALU.max, negate=True).then_inc(mx_done, 1)

            def x_rest(b, par):
                for i in range(2):
                    k = 2 * par + i
                    dve.wait_ge(ex_done, 2 * b + after(i + 1))
                    dve.wait_ge(pc_done, 2 * b + after(i) - 1)
                    v.reciprocal(rsum[:, k:k + 1], psum_[:, k:k + 1]).then_inc(rs_done, 1)
                    dve.wait_ge(pt_pe, 2 * b + after(i + 1))
                    dve.wait_ge(pc_pe, 2 * b + after(i) - 1)
                    v.tensor_tensor(pt[:, i, :, :], bank[5 + i][:].rearrange("p (k n) -> p k n", k=4), bc(mask[:], [P, 4, P]),
                                    ALU.mult).then_inc(pt_done, 1)
                dve.wait_ge(fin_pe, b + after(1))
                dve.wait_ge(xpb_done, after(1))
                v.tensor_tensor(xtok[:, bass.ds(b * 2, 2), :], xpb[:, bass.ds(b * 2, 2), :],
                                bank[7][:, 0:2 * C].rearrange("p (i n) -> p i n", i=2), ALU.add).then_inc(x2_done, 1)

            x_max(0, 0)
            with dve.Fori(0, B // 2 - 1) as bp2:
                for par in range(2):
                    x_max(bp2 * 2 + par + 1, 1 - par)
                    x_rest(bp2 * 2 + par, par)
            x_max(B - 1, 1)
            x_rest(B - 2, 0)
            x_rest(B - 1, 1)
            dve.wait_ge(x2_done, after(B))
            v.memset(combT[:], 1.0).then_inc(init_v, 1)
            norm(2)
            dve.wait_ge(lg_act, after(1))
            v.tensor_tensor(rtl[:], W["rT"], rth[:].bitcast(F32), ALU.subtract).then_inc(init_v, 1)
            with dve.Fori(0, NCH) as c:
                dve.wait_ge(tr_act, c + after(2 * NCH + 1))
                v.tensor_tensor(xl[:, bass.ds(c * CH, CH)], bank[0][:], xh[:, bass.ds(c * CH, CH)].bitcast(F32), ALU.subtract).then_inc(tr_dve, 1)

            count = [0]

            def step(ins):
                count[0] += 1
                ins.then_inc(chain, 1)
                dve.wait_ge(chain, after(count[0]))

            r = {n: t[:] for n, t in R.items()}
            dve.wait_ge(lg_act, after(2))
            step(v.tensor_scalar(r["e1"], r["e"], 1.0, None, ALU.add))
            step(v.reciprocal(r["sc"], r["e1"]))
            step(v.tensor_tensor(r["s"], r["sc"], bias_row[:].unsqueeze(1).to_broadcast([P, NT, E]), ALU.add))
            s4 = r["s"].rearrange("p t (g k) -> p (t g) k", k=EPG)
            v.tensor_tensor(pair[:, :, 0:3], s4[:, :, 0:3], s4[:, :, 1:4], ALU.add)
            v.tensor_tensor(pair[:, :, 3:5], s4[:, :, 0:2], s4[:, :, 2:4], ALU.add)
            step(v.tensor_tensor(pair[:, :, 5:6], s4[:, :, 0:1], s4[:, :, 3:4], ALU.add))
            step(v.tensor_reduce(gs[:], pair[:], X, ALU.max))
            g3 = gs[:].rearrange("p (t g) -> p t g", g=NG)
            other = g3.unsqueeze(2).to_broadcast([P, NT, NG, NG])
            own = g3.unsqueeze(3).to_broadcast([P, NT, NG, NG])
            v4 = lambda t: t[:].rearrange("p t (g k) -> p t g k", k=NG)
            v.tensor_tensor(v4(ggt), other, own, ALU.is_gt)
            step(v.tensor_tensor(v4(geq), other, own, ALU.is_equal))
            step(v.tensor_tensor(geq[:], geq[:], tri[:].unsqueeze(1).to_broadcast([P, NT, NG * NG]), ALU.mult))
            step(v.tensor_tensor(ggt[:], ggt[:], geq[:], ALU.add))
            step(v.tensor_reduce(grk[:], ggt[:].rearrange("p t (g k) -> p (t g) k", k=NG), X, ALU.add))
            step(v.tensor_scalar(gm[:], grk[:], float(TOPG), None, ALU.is_lt))
            step(v.tensor_scalar(gm1[:], gm[:], -1.0, None, ALU.add))
            m4 = r["m"].rearrange("p t (g k) -> p (t g) k", k=EPG)
            step(v.tensor_tensor(m4, s4, bc(gm[:], [P, NT * NG, EPG]), ALU.mult))
            step(v.tensor_tensor(m4, m4, bc(gm1[:], [P, NT * NG, EPG]), ALU.add))
            for t in range(NT):
                last = v.max(top8[:, t, :], R["m"][:, t, :])
            step(last)
            fourth = top8[:, :, TOPK - 1:TOPK].to_broadcast([P, NT, E])
            v.tensor_tensor(r["gt"], r["m"], fourth, ALU.is_gt)
            step(v.tensor_tensor(r["eq"], r["m"], fourth, ALU.is_equal))
            v.tensor_reduce(ngt[:], r["gt"], X, ALU.add)
            fl = lambda t: t[:].rearrange("p t e -> p (t e)")
            v.tensor_copy(r["le"], seg[:].unsqueeze(1).to_broadcast([P, NT, E])).then_inc(init_v, 1)
            dve.wait_ge(init_v, after(6))
            step(v.tensor_tensor_scan(fl(R["cum"]), fl(R["le"]), fl(R["eq"]), 0.0, ALU.mult, ALU.add))
            step(v.tensor_tensor(r["cum"], r["cum"], bc(ngt[:], [P, NT, E]), ALU.add))
            step(v.scalar_tensor_tensor(fl(R["le"]), fl(R["cum"]), float(TOPK), fl(R["eq"]), ALU.is_le, ALU.mult))
            step(v.tensor_tensor(r["sel"], r["gt"], r["le"], ALU.add))
            step(v.tensor_tensor(r["tw"], r["sc"], r["sel"], ALU.mult))
            step(v.tensor_reduce(tws[:], r["tw"], X, ALU.add))
            step(v.tensor_scalar(tws[:], tws[:], 1e-20, None, ALU.add))
            step(v.reciprocal(twr[:], tws[:]))
            step(v.tensor_tensor(r["tw"], r["tw"], bc(twr[:], [P, NT, E]), ALU.mult))
            step(v.tensor_scalar(r["tw"], r["tw"], SCALE_TW, None, ALU.mult))
            dve.wait_ge(ch_done, after(1))
            v.tensor_tensor(combl[:], combT[:], combh[:].bitcast(F32), ALU.subtract).then_inc(cl_done, 1)

            def weigh_of(n, cc):
                dve.wait_ge(sg_done, n + after(1))
                dve.wait_ge(tw_pe, n + after(1))
                dve.wait_ge(aa_done, n + after(0) - 1)
                v.tensor_tensor(stw[:, cc, :], sg[:, cc, :], bank[6 + cc][:], ALU.mult).then_inc(stw_done, 1)
                dve.wait_ge(stw_done, n + after(1))
                dve.wait_ge(u2_pe, n + after(1))
                dve.wait_ge(al_done, n + after(0) - 1)
                v.tensor_tensor(aa[:, cc, :], stw[:, cc, :], bank[4 + cc][:], ALU.mult).then_inc(aa_done, 1)

            def low_of(n, cc):
                dve.wait_ge(ah_done, n + after(1))
                dve.wait_ge(y2_pe, n + after(0) - 1)
                v.tensor_tensor(al[:, cc, :], aa[:, cc, :], ah[:, cc, :].bitcast(F32), ALU.subtract).then_inc(al_done, 1)

            with dve.Fori(0, 2) as hf:
                weigh_of(hf * (2 * EX), 0)
                weigh_of(hf * (2 * EX) + 1, 1)
                low_of(hf * (2 * EX), 0)
                with dve.Fori(1, EX) as e:
                    for cc in range(2):
                        n = hf * (2 * EX) + e * 2 + cc
                        weigh_of(n, cc)
                        low_of(n - 1, 1 - cc)
                low_of(hf * (2 * EX) + (2 * EX - 1), 1)
                for cc in range(2):
                    dve.wait_ge(yo_pe, hf * 2 + after(cc + 1))
                    o = xtok[:, bass.ds(hf * 8 + cc * 4, 4), :]
                    v.tensor_tensor(o, o, bank[2 + cc][:].rearrange("p (i n) -> p i n", i=4), ALU.add).then_inc(out_done, 1)

        @block.tensor
        def _(pe):
            t = nc.tensor
            credit(pe, "pe")
            pe.wait_ge(d_w, 32)

            def transpose_chunk(c, k):
                for i in range(4):
                    last = t.transpose(bank[0][:, i * P:(i + 1) * P], xn[:, c * 4 + i, :], ident)
                last.then_inc(tr, 1)

            pe.wait_ge(ln_xn, after(1))
            for c in range(NCH):
                pe.wait_ge(tr_act, c + after(0))
                transpose_chunk(c, 0)
                pe.wait_ge(xx_done, c + after(1))
                pe.wait_ge(h_act, c + after(0))
                t.matmul(bank[1][:], W["A"][:, 0:P], xx[:], start=True, stop=True)
                t.matmul(bank[2][0:LR, :], W["A"][:, P:GR], xx[:], start=True, stop=True).then_inc(h_pe, 1)
            pe.wait_ge(h_act, after(NCH))
            with pe.Fori(0, NCH) as c:
                def miu(s):
                    pe.wait_ge(miu_t, c * NS + after(s) - 1)
                    t.matmul(bank[s % 2][:], bp[:, s * C:(s + 1) * C], HF[:, bass.ds(c * CH + s * T, CH)],
                             start=True, stop=True).then_inc(miu_pe, 1)

                def got(s):
                    pe.wait_ge(xs_done, c * NS + after(s + 1))

                miu(0)
                miu(1)
                got(0)
                pe.wait_ge(g1_act, c + after(0))
                t.matmul(bank[2][0:TDR, :], W["tdA"], xs[:, 0, :], start=True, stop=True).then_inc(w1_pe, 1)
                miu(2)
                got(1)
                pe.wait_ge(k_done, c + after(0))
                t.matmul(bank[4][:], W["WkT"], xs[:, 1, :], start=True, stop=True).then_inc(k_pe, 1)
                pe.wait_ge(w1_act, c + after(1))
                pe.wait_ge(g_done, c + after(0))
                t.matmul(bank[3][:], W["tdB"][0:TDR, :], w1[:], start=True, stop=True).then_inc(w2_pe, 1)
                miu(3)
                got(2)
                pe.wait_ge(v_done, c + after(0))
                for i in range(4):
                    last = t.matmul(bank[5][:, i * C:(i + 1) * C], xs[:, 2, i * P:(i + 1) * P], W["WvT"], start=True, stop=True)
                last.then_inc(v_pe, 1)
                miu(4)
                got(3)
                pe.wait_ge(r_done, c + after(0))
                t.matmul(bank[6][:], W["WrT"], xs[:, 3, :], start=True, stop=True).then_inc(r_pe, 1)
                got(4)
                pe.wait_ge(ds_done, c + after(0))
                t.matmul(bank[2][:], W["Wg1"][:, 0:P], xs[:, 4, :], start=True, stop=True)
                t.matmul(bank[7][0:LR, :], W["Wg1"][:, P:GR], xs[:, 4, :], start=True, stop=True).then_inc(g1_pe, 1)
                pe.wait_ge(g1_act, c + after(1))
                pe.wait_ge(dec_done, c + after(1))
                t.matmul(bank[3][:], W["Wg2a"], g1a[:], start=True, stop=False)
                t.matmul(bank[3][:], W["Wg2b"][0:LR, :], g1b[:], start=False, stop=True).then_inc(g_pe, 1)
                pe.wait_ge(ruk_done, c + after(1))
                for i in range(4):
                    last = t.matmul(bank[7][:, i * NH:(i + 1) * NH], ruk[:, i * P:(i + 1) * P], W["hsel"], start=True, stop=True)
                last.then_inc(ds_pe, 1)
            pe.wait_ge(ds_done, after(NCH))
            pe.wait_ge(g_done, after(NCH))
            with pe.Fori(0, NCH) as c:
                for j in range(LEVELS):
                    h = 1 << j
                    for q in range(2):
                        if j == 0:
                            pe.wait_ge(x1_done, c + after(0))
                            pe.wait_ge(lv_act[q], c * 2 + after(0))
                            pe.wait_ge(kq_in, c + after(1))
                            pe.wait_ge(rp_in, c + after(1))
                        else:
                            pe.wait_ge(rp_up[q], c * (LEVELS - 1) + after(j))
                            pe.wait_ge(kq_up[q], c * (LEVELS - 1) + after(j))
                        if j >= 2:
                            pe.wait_ge(lv_at[q], c * MASKED + after(j - 1))
                        if j == MASKED:
                            carry(pe, "pe")
                        for hd in range(NH):
                            rows = slice(hd * HD, (hd + 1) * HD)
                            dst = bank[4 * (j % 2) + 2 * q + hd]
                            if j == LEVELS - 1:
                                last = t.matmul(dst[:, 0:P], kqc[rows, q, 0:P], rpc[rows, q, P:2 * P], start=True, stop=True)
                                continue
                            m = P if j < MASKED else HD
                            for k in range(2):
                                odd = rpc[rows, q, k * P:(k + 1) * P].rearrange("p (n two h) -> p n two h", two=2, h=h)[:, :, 1, :]
                                last = t.matmul(dst[0:m, k * HD:(k + 1) * HD].rearrange("p (n h) -> p n h", h=h),
                                                kqc[rows, q, k * P:k * P + m], odd, start=True, stop=True)
                        last.then_inc(lv[q], 1)
                for q in range(2):
                    pe.wait_ge(lv_at[q], c * MASKED + after(MASKED))
                    pe.wait_ge(lv_act[q], c * 2 + after(2))
                    for k in range(2):
                        for hd in range(NH):
                            dst = bank[q][:, (2 * k + hd) * HD:(2 * k + hd + 1) * HD]
                            vt = lambda kk: vv[:, bass.ds(c * 4 + q * 2 + kk, 1), hd * HD:(hd + 1) * HD].rearrange("p o n -> p (o n)")
                            last = t.matmul(dst, at[:, q, hd, k, :], vt(k), start=True, stop=(k == 0))
                            if k == 1:
                                last = t.matmul(dst, at2[:, q, hd, :], vt(0), start=False, stop=True)
                    last.then_inc(y_pe, 1)
                pe.wait_ge(gn_yn, c + after(1))
                for i in range(4):
                    last = t.transpose(bank[2][:, i * P:(i + 1) * P], yn[:, 2 * i:2 * i + 2, :].rearrange("p a b -> p (a b)"), ident)
                last.then_inc(yt_pe, 1)
                pe.wait_ge(z_done, c + after(1))
                zv = z[:].rearrange("p (q j h) -> p q h j", q=2, h=2)
                for q in range(2):
                    for hh in range(2):
                        i = 2 * q + hh
                        last = t.matmul(bank[3][:, i * C:(i + 1) * C], zv[:, q, hh, :], W["WoT"], start=True, stop=True)
                last.then_inc(wo_pe, 1)
            pe.wait_ge(y_done, after(2 * NCH))
            t.matmul(bank[0][:, 0:C], W["wq"], W["wk"], start=True, stop=True).then_inc(m_pe, 1)
            pe.wait_ge(ln_xn, after(2))
            pe.wait_ge(m_act, after(1))
            for c in range(NCH):
                pe.wait_ge(tr_act, c + after(NCH))
                transpose_chunk(c, 1)
            pe.wait_ge(tr_act, after(2 * NCH))
            pe.wait_ge(x1_done, after(NCH))
            pe.wait_ge(d_ctx, 32)
            pe.wait_ge(init_v, after(3))

            def scores(b, par):
                pe.wait_ge(q_act, b + after(0))
                t.matmul(bank[4][:, 0:S], mqk[:], xT2[:, bass.ds(b * S, S)], start=True, stop=True).then_inc(q_pe, 1)
                pe.wait_ge(q_act, b + after(1))
                for i in range(2):
                    t.matmul(bank[2 * par + i][:], q2[:, par, i * P:(i + 1) * P], ctxT[:, bass.ds(b * M, M)],
                             start=True, stop=True).then_inc(s_pe, 1)

            def x_rest(b, par):
                for i in range(2):
                    pe.wait_ge(ex_done, 2 * b + after(i + 1))
                    pe.wait_ge(pt_done, 2 * b + after(i) - 1)
                    for k in range(4):
                        last = t.transpose(bank[5 + i][:, k * P:(k + 1) * P], pr[:, 2 * par + i, k * P:(k + 1) * P], ident)
                    last.then_inc(pt_pe, 1)
                pe.wait_ge(x2_done, b + after(0))
                for i in range(2):
                    pe.wait_ge(pt_done, 2 * b + after(i + 1))
                    for k in range(4):
                        last = t.matmul(bank[7][:, i * C:(i + 1) * C], pt[:, i, k, :],
                                        ctxn[:, bass.ds(b * 4 + k, 1), :].rearrange("p o n -> p (o n)"), start=(k == 0), stop=(k == 3))
                    last.then_inc(pc_pe, 1)
                pe.wait_ge(pc_done, 2 * b + after(2))
                for i in range(2):
                    last = t.matmul(bank[7][:, 256 + i * C:256 + (i + 1) * C], pcs[:, i, :], W["pwT"], start=True, stop=True)
                last.then_inc(t1_pe, 1)
                pe.wait_ge(t1_done, b + after(1))
                t.matmul(bank[7][:, 0:2 * C], W["xvT"], t1s[:], start=True, stop=True).then_inc(fin_pe, 1)

            scores(0, 0)
            with pe.Fori(0, B // 2 - 1) as bp2:
                for par in range(2):
                    scores(bp2 * 2 + par + 1, 1 - par)
                    x_rest(bp2 * 2 + par, par)
            scores(B - 1, 1)
            x_rest(B - 2, 0)
            x_rest(B - 1, 1)
            def split_mm(dst, wh, wl, mh, ml, first, last_):
                t.matmul(dst, wh, mh, start=first, stop=False)
                t.matmul(dst, wh, ml, start=False, stop=False)
                return t.matmul(dst, wl, mh, start=False, stop=last_)

            pe.wait_ge(ln_xn, after(3))
            for c in range(NCH):
                pe.wait_ge(tr_dve, c + after(0))
                transpose_chunk(c, 2)
            pe.wait_ge(tr_dve, after(NCH))
            pe.wait_ge(init_v, after(5))
            for i in range(NT):
                ts = slice(i * P, (i + 1) * P)
                last = split_mm(bank[1][:, i * E:(i + 1) * E], xh[:, ts], xl[:, ts], rth[:], rtl[:], True, True)
            last.then_inc(lg_pe, 1)
            pe.wait_ge(chain, after(N_ROUTER))
            for k in range(4):
                for i in range(4):
                    last = t.transpose(bank[2 + k][0:E, i * P:(i + 1) * P], R["tw"][:, 4 * k + i, :], ident)
                last.then_inc(ct_pe, 1)
            pe.wait_ge(ct_act, after(4))

            def front(hf, n, par, cc, grp):
                cs = bass.ds(hf * 2 * CH + cc * CH, CH)
                if cc == 0:
                    pe.wait_ge(wfl_done, grp + after(1))
                wh = lambda m: wfh[:, par, m * C:(m + 1) * C]
                wl = lambda m: wfl[:, par, m * C:(m + 1) * C]
                pe.wait_ge(sg_done, n + after(0) - 1)
                split_mm(bank[2 + cc][:], wh(0), wl(0), xh[:, cs], xl[:, cs], True, True).then_inc(h2_pe, 1)
                pe.wait_ge(aa_done, n + after(0) - 1)
                split_mm(bank[4 + cc][:], wh(1), wl(1), xh[:, cs], xl[:, cs], True, True).then_inc(u2_pe, 1)
                t.matmul(bank[6 + cc][:], one_r[:], twrow[:, par, cc * CH:(cc + 1) * CH], start=True, stop=True).then_inc(tw_pe, 1)

            def back(n, par, cc):
                pe.wait_ge(al_done, n + after(1))
                split_mm(bank[cc][:], wfh[:, par, 2 * C:3 * C], wfl[:, par, 2 * C:3 * C], ah[:, cc, :], al[:, cc, :],
                         False, False).then_inc(y2_pe, 1)

            def turn_of(hf, turn, first):
                for k in range(2 * WB):
                    e = hf * EX + turn * WB + k // 2
                    n = (hf * EX + turn * WB) * 2 + k
                    front(hf, n, k // 2, k % 2, e)
                    if not (first and k < 2):
                        back(n - 2, (k - 2) % (2 * WB) // 2, k % 2)

            with pe.Fori(0, 2) as hf:
                pe.wait_ge(out_done, hf * 2 + after(0))
                pe.wait_ge(yts_done, hf * 2 + after(0))
                for cc in range(2):
                    t.matmul(bank[cc][:], zero_r[:, 0:P], zero_r[:], start=True, stop=False)
                turn_of(hf, 0, True)
                with pe.Fori(1, EX // WB) as turn:
                    turn_of(hf, turn, False)
                for k in range(2):
                    back((hf * EX + EX) * 2 - 2 + k, WB - 1, k)
                for cc in range(2):
                    last = t.matmul(bank[cc][:], zero_r[:, 0:P], zero_r[:], start=False, stop=True)
                last.then_inc(yacc_pe, 1)
                for cc in range(2):
                    pe.wait_ge(yts_done, hf * 2 + after(cc + 1))
                    for i in range(4):
                        last = t.transpose(bank[2 + cc][:, i * P:(i + 1) * P], yTs[:, cc, i * P:(i + 1) * P], ident)
                    last.then_inc(yo_pe, 1)


N_ROUTER = 25
_INS = ("x", "pack", "bp", "ctx", "ctxT", "rows", "maskc", "lvl", "wffn", "tri")


def _lay_out(i):
    g = lambda n: np.asarray(i[n])
    pack = np.zeros((P, NPACK), np.float32)

    def put(name, a):
        o, n = PACK[name]
        pack[:a.shape[0], o:o + a.shape[1]] = a

    put("A", g("L0_attn_A"))
    put("tdA", g("L0_attn_tdA"))
    for name in ("Wk", "Wv", "Wr", "Wo"):
        put(name + "T", g("L0_attn_" + name).T)
    put("Wg1", g("L0_attn_Wg1"))
    put("Wg2a", g("L0_attn_Wg2")[:P])
    put("Wg2b", g("L0_attn_Wg2")[P:])
    put("tdB", g("L0_attn_tdB"))
    qkv = g("L0_xattn_qkv_w")
    put("wq", qkv[:C])
    put("wk", qkv[C:2 * C])
    put("xvT", qkv[2 * C:].T)
    put("pwT", g("L0_xattn_proj_w").T)
    put("rT", g("L0_ffn_router_w").T)
    put("ident", np.eye(P, dtype=np.float32))
    put("hsel", np.repeat(np.eye(NH, dtype=np.float32), HD, axis=0))
    cols = [g("L0_attn_miu_x").reshape(1, C), g("L0_attn_lam").reshape(NS, C), g("L0_attn_td_miu").reshape(1, C),
            g("L0_attn_u").reshape(1, C), g("L0_attn_gamma").reshape(1, C), g("L0_attn_beta").reshape(1, C)]
    put("cols", np.concatenate(cols).T)
    ctx = g("ctx_1024")
    levels = np.zeros((P, MASKED, HD), np.int32)
    for j in range(MASKED):
        h = 1 << j
        for s in range(P):
            for n in range(HD // h):
                levels[s, j, n * h:(n + 1) * h] = s // h == 2 * n
    tri = np.zeros((P, NG * NG + E), np.float32)
    tri[:, :NG * NG] = (np.arange(NG)[None, :] < np.arange(NG)[:, None]).reshape(1, -1)
    tri[:, NG * NG + 1:] = 1.0
    split = lambda a: a.reshape(C, 2, C).transpose(1, 0, 2)
    gate = np.concatenate([g("L0_ffn_gate_w"), split(g("L0_ffn_sh_gate_w"))])
    up = np.concatenate([g("L0_ffn_up_w"), split(g("L0_ffn_sh_up_w"))])
    down = np.concatenate([g("L0_ffn_down_w"), g("L0_ffn_sh_down_w").reshape(2, C, C)])
    return {
        "x": g("x"), "pack": pack,
        "bp": g("L0_attn_Bp").transpose(1, 0, 2).reshape(LR, NS * C),
        "ctx": ctx.reshape(B * (M // P), P, C).transpose(1, 0, 2),
        "ctxT": ctx.transpose(2, 0, 1).reshape(C, B * M),
        "rows": np.concatenate([g("L0_xattn_proj_b"), g("L0_ffn_bias")]),
        "maskc": g("mask_S2_ik0").reshape(M // P, P).T,
        "lvl": levels, "tri": tri,
        "wffn": np.concatenate([gate, up, down], axis=2),
    }


def kernel(**inputs):
    import concourse.bacc as bacc
    from concourse.bass_utils import run_bass_kernel_spmd

    nc = bacc.Bacc("TRN2", target_bir_lowering=False, num_devices=1)
    laid = _lay_out(inputs)
    arrays, args = {}, []
    for name in _INS:
        arr = np.ascontiguousarray(laid[name])
        arrays["in_" + name] = arr
        args.append(nc.dram_tensor("in_" + name, arr.shape, mybir.dt.from_np(arr.dtype), kind="ExternalInput").ap())
    args.append(nc.dram_tensor("out_0", (B, S, C), F32, kind="ExternalOutput").ap())
    args.append(nc.dram_tensor("combine_rows", (EX, 2, T), F32, kind="Internal").ap())
    decoder_layer(nc, *args)
    r = run_bass_kernel_spmd(nc, [arrays], core_ids=[0])
    return r.results[0]["out_0"]
```

```python
from contextlib import ExitStack

import numpy as np
import concourse.bass as bass
from concourse import mybir

F32 = mybir.dt.float32
F32R = mybir.dt.float32r
I32 = mybir.dt.int32
ALU = mybir.AluOpType
ACT = mybir.ActivationFunctionType
X = mybir.AxisListType.X

P = 128
B = 8
S = 256
M = 512
C = 128
T = B * S
NT = T // P
CH = 512
NCH = T // CH
HD = 64
NH = C // HD
NS = 5
LR = 32
GR = 160
TDR = 64
E = 16
EX = E + 2
NG = 4
EPG = E // NG
TOPG = 2
TOPK = 4
SCALE_TW = 2.5
WB = 3
TURNS = EX // WB
SIDE = 4
LEVELS = 8
MASKED = 6
SQ = 4
NSC = B // SQ
SCALE_QK = 0.25

PACK = {}
_at = 0
for _name, _n in (("WoT", C), ("wq", C), ("wk", C), ("xvT", C), ("pwT", C), ("rT", E),
                  ("ident", P), ("cols", 10), ("hsel", NH)):
    PACK[_name] = (_at, _n)
    _at += _n
NPACK = _at
SPLIT = {}
_at = 0
for _name, _n in (("A", NS * P), ("tdA", P), ("WkT", C), ("WvT", C), ("WrT", C), ("Wg1a", P), ("Wg1b", P),
                  ("tdB", C), ("Wg2a", C)):
    SPLIT[_name] = (_at, _n)
    _at += _n
NSPLIT = _at
NSTACK = NS * C + C
STREAMS = (0, 4, 1, 3, 2)
SLOT = (0, 1, 2, 0, 1)
COL = {n: i for i, n in enumerate(("miu_x", "lam0", "lam1", "lam2", "lam3", "lam4", "td_miu", "u", "gamma", "beta"))}


CREDIT = 5


def after(n):
    return n + CREDIT


def bc(ap, shape):
    return ap.unsqueeze(len(shape) - 1).to_broadcast(shape)


def decoder_layer(nc, x_d, pack_d, split_d, stack_d, ctx_d, ctxT_d, rows_d, maskc_d, lvl_d, wffn_d, tri_d, out_d, tw_d):
    x_v = x_d.rearrange("b (p h) c -> p b (h c)", h=2)
    out_v = out_d.rearrange("b (p h) c -> p b (h c)", h=2)

    with ExitStack() as stack:
        scope = [stack]

        def sb(name, shape, dt=F32):
            return scope[-1].enter_context(nc.sbuf_tensor(name, shape, dt))

        producers = {}

        def sem(name, eng=None):
            s = stack.enter_context(nc.semaphore(name))
            if eng:
                producers.setdefault(eng, []).append(s)
            return s

        bank = [stack.enter_context(nc.psum_tensor(f"bank{i}", [P, 512], F32)) for i in range(8)]

        xtok = sb("xtok", [P, NT, C])
        pack = sb("pack", [P, NPACK])
        W = {n: pack[:, o:o + w] for n, (o, w) in PACK.items()}
        col = {n: W["cols"][:, i:i + 1] for n, i in COL.items()}
        ident = W["ident"]
        wh_all = sb("wh_all", [P, NSPLIT], F32R)
        wl_all = sb("wl_all", [P, NSPLIT], F32R)
        WH = {n: wh_all[:, o:o + w] for n, (o, w) in SPLIT.items()}
        WL = {n: wl_all[:, o:o + w] for n, (o, w) in SPLIT.items()}
        wst = sb("wst", [P, NSTACK], F32R)
        pb_row = sb("pb_row", [P, C])
        bias_row = sb("bias_row", [P, E])
        mask_i = sb("mask_i", [P, M // P], I32)
        mask = sb("mask", [P, M // P])
        lvl = sb("lvl", [P, MASKED, HD], I32)
        tri = sb("tri", [P, NG * NG])
        seg = sb("seg", [P, E])
        neghalf = sb("neghalf", [P, 16])
        ctxn = sb("ctxn", [P, 2, M // P, C])
        ctxT = sb("ctxT", [C, 2, M])
        stat = {n: sb("st_" + n, [P, NT]) for n in ("sum", "mean", "var", "ve", "rstd")}
        zero_r = sb("zero_r", [P, CH], F32R)
        one_r = sb("one_r", [2, P], F32R)
        xc = sb("xc", [P, NT, C])
        sq = sb("sq", [P, NT, C])
        xn = sq
        mqh = sb("mqh", [C, C], F32R)
        mql = sb("mql", [C, C], F32R)
        scope.append(ExitStack())
        xTp = sb("xTp", [C, B, S + 1])
        bA = sb("bA", [C, B, S])
        dec = sb("dec", [C, T])
        kq = sb("kq", [C, T])
        rp = sb("rp", [C, NH, T])
        scope.append(ExitStack())
        raw = sb("raw", [P, NSPLIT])
        raw_s = sb("raw_s", [P, NSTACK])
        scope.pop().close()
        vv = sb("vv", [P, NT, C])
        gT = sb("gT", [C, T])
        dsum = sb("dsum", [P, NT, NH])
        at = sb("at", [P, 2, 4, NH, P])
        scope.append(ExitStack())
        HF = sb("HF", [P, NS * T], F32R)
        tmp_s = xc[:].rearrange("p a b -> p (a b)").rearrange("p (k t) -> p k t", t=CH)
        x5 = xn[:].rearrange("p a b -> p (a b)").rearrange("p (k t) -> p k t", t=CH)
        x5h = sb("x5h", [C, NS, CH], F32R)
        x5l = sb("x5l", [C, NS, CH], F32R)
        hT = tmp_s
        xx = sb("xx", [C, CH])
        w1 = sb("w1", [P, CH])
        w1s = sb("w1s", [P, CH], F32R)
        xxh, xxl = x5h, x5l
        g1a = xx
        g1ah = sb("g1ah", [P, CH], F32R)
        g1al = sb("g1al", [P, CH], F32R)
        g1b = sb("g1b", [P, CH])
        g1bs = sb("g1bs", [P, CH], F32R)
        ruk = g1b
        scope.pop().close()
        scope.append(ExitStack())
        at2 = sb("at2", [P, 2, 2, NH, P])
        tot = [None] + [sb(f"tot{j}", [C, 2, CH >> j]) for j in range(1, LEVELS - 1)]
        yc = sb("yc", [P, 2, 8, HD])
        gstat = {n: sb("gs_" + n, [P, 2, 8]) for n in ("sum", "mean", "var", "ve", "rstd")}
        yxc = yc
        ysq = sb("ysq", [P, 2, 8, HD])
        yn = ysq
        z1 = sb("z1", [C, 2, CH])
        z = z1
        scope.pop().close()
        scope.pop().close()
        qh = sb("qh", [C, 2, S], F32R)
        ql = sb("ql", [C, 2, S], F32R)
        cth = sb("cth", [C, 2, M], F32R)
        ctl = sb("ctl", [C, 2, M], F32R)
        cnm = sb("cnm", [P, 2, M // P, C])
        cnh = sb("cnh", [P, 2, M // P, C], F32R)
        cnl = sb("cnl", [P, 2, M // P, C], F32R)
        nmax = sb("nmax", [P, 4])
        psum_ = sb("psums", [P, 4])
        rsum = sb("rsum", [P, 4])
        pr = sb("pr", [P, 4, M])
        pws = sb("pws", [P, 2, C])
        t1s = sb("t1s", [C, 2 * C])
        xpb = sb("xpb", [P, NT, C])
        xh = sb("xh", [C, T], F32R)
        xl = sb("xl", [C, T], F32R)
        rth = sb("rth", [C, E], F32R)
        rtl = sb("rtl", [C, E], F32R)
        R = {n: sb("r_" + n, [P, NT, E]) for n in ("e", "e1", "sc", "s", "m", "gt", "eq", "cum", "le", "sel", "tw")}
        pair = sb("pair", [P, NT * NG, 6])
        gs = sb("gsc", [P, NT * NG])
        ggt = sb("ggt", [P, NT, NG * NG])
        geq = sb("geq", [P, NT, NG * NG])
        grk = sb("grk", [P, NT * NG])
        gm = sb("gm", [P, NT * NG])
        gm1 = sb("gm1", [P, NT * NG])
        top8 = sb("top8", [P, NT, 8])
        ngt = sb("ngt", [P, NT])
        tws = sb("tws", [P, NT])
        twr = sb("twr", [P, NT])
        combT = sb("combT", [EX, T])
        combh = sb("combh", [EX, T], F32R)
        combl = sb("combl", [EX, T], F32R)
        wf = sb("wf", [P, WB, 3 * C])
        wfh = sb("wfh", [P, WB, 3 * C], F32R)
        wfl = sb("wfl", [P, WB, 3 * C], F32R)
        twrow = sb("twrow", [2, WB, 2 * CH], F32R)
        scope.append(ExitStack())
        xqh = sb("xqh", [C, T], F32R)
        xql = sb("xql", [C, T], F32R)
        t0h = sb("t0h", [P, M // P, 2 * C], F32R)
        t0l = sb("t0l", [P, M // P, 2 * C], F32R)
        scope.pop().close()
        sg = sb("sg", [P, 2, CH])
        stw = sb("stw", [P, 2, CH])
        aa = sb("aa", [P, 2, CH])
        ah = sb("ah", [P, 2, CH], F32R)
        al = sb("al", [P, 2, CH], F32R)
        yTs = pr[:, 0:2, :]

        d_x, d_w, d_small = sem("d_x"), sem("d_w"), sem("d_small")
        d_split, d_stack = sem("d_split"), sem("d_stack")
        d_ctx = [sem(f"d_ctx{i}") for i in range(2)]
        wh_done, wla_done, wl_done = sem("wh_done", "act"), sem("wla_done", "dve"), sem("wl_done", "pool")
        d_tw, d_out = sem("d_tw"), sem("d_out")
        d_wf = [sem(f"d_wf{i}") for i in range(WB)]
        init_v, init_p = sem("init_v", "dve"), sem("init_p", "pool")
        ln_sum, ln_mean, ln_xc, ln_var, ln_xn = (sem(n, "dve") for n in ("ln_sum", "ln_mean", "ln_xc", "ln_var", "ln_xn"))
        ln_sq = sem("ln_sq", "act")
        ln_ve, ln_rstd = sem("ln_ve", "pool"), sem("ln_rstd", "pool")
        tr = sem("tr", "pe")
        tr_act, tr_dve = sem("tr_act", "act"), sem("tr_dve", "dve")
        ba_done, xx_done = sem("ba_done", "dve"), sem("xx_done", "dve")
        xxh_done, xxl_done = sem("xxh_done", "act"), sem("xxl_done", "dve")
        h_pe, h_act, h_lo = sem("h_pe", "pe"), sem("h_act", "act"), sem("h_lo", "dve")
        x5h_done, x5l_done = sem("x5h_done", "act"), sem("x5l_done", "dve")
        w1_lo, g1_lo = sem("w1_lo", "dve"), sem("g1_lo", "dve")
        miu_pe, miu_t, xs_done = sem("miu_pe", "pe"), sem("miu_t", "dve"), sem("xs_done", "pool")
        w1_pe, w1_act, w2_pe, dec_done = sem("w1_pe", "pe"), sem("w1_act", "act"), sem("w2_pe", "pe"), sem("dec_done", "act")
        k_pe, k_done = sem("k_pe", "pe"), sem("k_done", "dve")
        v_pe, v_done = sem("v_pe", "pe"), sem("v_done", "act")
        r_pe, r_done = sem("r_pe", "pe"), sem("r_done", "act")
        ruk_done, ds_pe, ds_done = sem("ruk_done", "dve"), sem("ds_pe", "pe"), sem("ds_done", "act")
        g1_pe, g1_act, g_pe, g_done = sem("g1_pe", "pe"), sem("g1_act", "act"), sem("g_pe", "pe"), sem("g_done", "act")
        lv = [sem(f"lv{q}", "pe") for q in range(2)]
        lv_at = [sem(f"lv_at{q}", "dve") for q in range(2)]
        lv_act = [sem(f"lv_act{q}", "act") for q in range(2)]
        rp_up = [sem(f"rp_up{q}", "dve") for q in range(2)]
        kq_up = [sem(f"kq_up{q}", "pool") for q in range(2)]
        tot_up = [sem(f"tot_up{q}", "pool") for q in range(2)]
        y_pe, y_done = sem("y_pe", "pe"), sem("y_done", "dve")
        gn_sum, gn_mean, gn_xc, gn_var, gn_yn = (sem(n, "dve") for n in ("gn_sum", "gn_mean", "gn_xc", "gn_var", "gn_yn"))
        gn_sq = sem("gn_sq", "act")
        gn_ve, gn_rstd = sem("gn_ve", "pool"), sem("gn_rstd", "pool")
        yt_pe, z1_done, z_done = sem("yt_pe", "pe"), sem("z1_done", "dve"), sem("z_done", "dve")
        wo_pe, x1_done = sem("wo_pe", "pe"), sem("x1_done", "dve")
        m_pe, m_act, m_lo = sem("m_pe", "pe"), sem("m_act", "act"), sem("m_lo", "dve")
        q_pe, q_act, q_lo = sem("q_pe", "pe"), sem("q_act", "act"), sem("q_lo", "dve")
        s_pe, mx_done, ex_done = sem("s_pe", "pe"), sem("mx_done", "dve"), sem("ex_done", "act")
        rs_done, pws_done = sem("rs_done", "dve"), sem("pws_done", "dve")
        cth_done, cnh_done = sem("cth_done", "act"), sem("cnh_done", "act")
        ctl_done, cnm_done, cnl_done = sem("ctl_done", "pool"), sem("cnm_done", "pool"), sem("cnl_done", "pool")
        t0_pe, t0_act, t0_lo = sem("t0_pe", "pe"), sem("t0_act", "act"), sem("t0_lo", "dve")
        t1_pe, t1_done = sem("t1_pe", "pe"), sem("t1_done", "act")
        fin_pe, x2_done = sem("fin_pe", "pe"), sem("x2_done", "dve")
        xpb_done = sem("xpb_done", "pool")
        lg_pe, lg_act = sem("lg_pe", "pe"), sem("lg_act", "act")
        rth_done, rtl_done = sem("rth_done", "act"), sem("rtl_done", "dve")
        chain = sem("chain", "dve")
        ct_pe, ct_act, ch_done, cl_done = sem("ct_pe", "pe"), sem("ct_act", "act"), sem("ch_done", "act"), sem("cl_done", "dve")
        wfh_done, wfl_done = sem("wfh_done", "act"), sem("wfl_done", "pool")
        h2_pe, u2_pe, tw_pe = sem("h2_pe", "pe"), sem("u2_pe", "pe"), sem("tw_pe", "pe")
        sg_done, stw_done, aa_done = sem("sg_done", "act"), sem("stw_done", "dve"), sem("aa_done", "dve")
        ah_done, al_done = sem("ah_done", "act"), sem("al_done", "pool")
        y2_pe, yacc_pe = sem("y2_pe", "pe"), sem("yacc_pe", "pe")
        yts_done, yo_pe, out_done = sem("yts_done", "act"), sem("yo_pe", "pe"), sem("out_done", "dve")

        carrier = {n: sem("carrier_" + n) for n in ("pool",)}

        block = stack.enter_context(nc.Block())

        def credit(eng, name):
            for s in producers[name]:
                eng.sem_inc(s, CREDIT)

        def carry(eng, which):
            eng.sem_inc(carrier[which], 1)

        GROUP = [[slice(c * (SQ * S) + q * CH, c * (SQ * S) + (q + 1) * CH) for q in range(2)] for c in range(NSC)]

        def halves(ap, h):
            return ap.rearrange("p (n two h) -> p n two h", two=2, h=h)

        def total(c, j, q):
            t_ = dec[:, GROUP[c][q]] if j == 0 else tot[j][:, q, :]
            return t_.rearrange("p (n two) -> p n two", two=2)

        def turned(k, c):
            return (0, 6 * (c % 2), 5 if c == NCH - 1 else 4)[k]

        def half_of(h):
            return slice(h * (NT // 2), (h + 1) * (NT // 2))

        LOGITS = (4, 7)

        @block.sync
        def _(sp):
            sp.dma_start(xtok[:].rearrange("p (b h) c -> p b (h c)", h=2), x_v).then_inc(d_x, 16)
            sp.dma_start(pack[:], pack_d).then_inc(d_w, 16)
            sp.dma_start(raw[:], split_d).then_inc(d_split, 16)
            sp.dma_start(raw_s[:], stack_d).then_inc(d_stack, 16)
            sp.dma_start(lvl[:], lvl_d).then_inc(d_small, 16)
            sp.dma_start(tri[:], tri_d[:, 0:NG * NG]).then_inc(d_small, 16)
            sp.dma_start(seg[:], tri_d[:, NG * NG:NG * NG + E]).then_inc(d_small, 16)
            sp.dma_start(mask_i[:], maskc_d).then_inc(d_small, 16)
            sp.dma_start(pb_row[:], rows_d[0:C].unsqueeze(0).to_broadcast([P, C])).then_inc(d_small, 16)
            sp.dma_start(bias_row[:], rows_d[C:C + E].unsqueeze(0).to_broadcast([P, E])).then_inc(d_small, 16)
            with sp.Fori(0, B // 2) as bp2:
                for par in range(2):
                    sp.wait_ge(ctl_done, 2 * bp2 + par + after(0) - 1)
                    sp.wait_ge(cnm_done, 2 * bp2 + par + after(0) - 1)
                    sp.dma_start(ctxT[:, par, :], ctxT_d[:, bass.ds((bp2 * 2 + par) * M, M)]).then_inc(d_ctx[par], 16)
                    sp.dma_start(ctxn[:, par], ctx_d[:, bass.ds((bp2 * 2 + par) * (M // P), M // P), :]).then_inc(d_ctx[par], 16)
            def store_combine(h):
                tok = slice(h * 2 * CH, (h + 1) * 2 * CH)
                sp.wait_ge(ch_done, after(h + 1))
                sp.dma_start(tw_d[:, 0, tok], combh[:, tok].bitcast(F32)).then_inc(d_tw, 16)
                sp.wait_ge(cl_done, after(h + 1))
                sp.dma_start(tw_d[:, 1, tok], combl[:, tok].bitcast(F32)).then_inc(d_tw, 16)
                sp.wait_ge(d_tw, 32 * (h + 1))

            def load_experts(hf, turn):
                for par in range(WB):
                    n, e = hf * EX + turn * WB + par, turn * WB + par
                    sp.wait_ge(wfl_done, after(n) - (WB - 1))
                    sp.wait_ge(tw_pe, 2 * n + after(0) - 2 * (WB - 1))
                    sp.dma_start(wf[:, par, :], wffn_d[bass.ds(e, 1), :, :].rearrange("o p n -> (o p) n")).then_inc(d_wf[par], 16)
                    sp.dma_start(twrow[:, par, :].bitcast(F32), tw_d[bass.ds(e, 1), :, hf * 2 * CH:(hf + 1) * 2 * CH]
                                 .rearrange("o k n -> (o k) n")).then_inc(d_wf[par], 16)

            for hf in range(2):
                store_combine(hf)
                with sp.Fori(0, TURNS) as turn:
                    load_experts(hf, turn)
            for hf in range(2):
                sp.wait_ge(out_done, after(2 * (hf + 1)))
                sp.dma_start(out_v[:, 4 * hf:4 * hf + 4, :],
                             xtok[:, 8 * hf:8 * hf + 8, :].rearrange("p (b h) c -> p b (h c)", h=2)).then_inc(d_out, 16)
            sp.wait_ge(d_out, 32)

        @block.gpsimd
        def _(pool):
            credit(pool, "pool")
            g = nc.gpsimd
            g.memset(neghalf[:], -0.5).then_inc(init_p, 1)
            g.memset(xTp[:], 0.0).then_inc(init_p, 1)
            g.memset(rp[:], 0.0).then_inc(init_p, 1)

            def norm_rstd(k, chunks=range(NCH)):
                for c in chunks:
                    ti = slice(4 * c, 4 * c + 4)
                    pool.wait_ge(ln_var, after(k * NCH + c + 1))
                    g.tensor_scalar(stat["ve"][:, ti], stat["var"][:, ti], 1.0 / C, 1e-5, ALU.mult, ALU.add).then_inc(ln_ve, 1)
                    pool.wait_ge(ln_ve, after(k * NCH + c + 1))
                    g.tensor_tensor(stat["rstd"][:, ti], stat["ve"][:, ti], neghalf[:, ti], ALU.pow).then_inc(ln_rstd, 1)

            norm_rstd(0)
            pool.wait_ge(wh_done, after(2))
            na = SPLIT["A"][1]
            g.tensor_tensor(wl_all[:, na:], raw[:, na:], wh_all[:, na:].bitcast(F32), ALU.subtract).then_inc(wl_done, 1)
            pool.wait_ge(wh_done, after(3))
            for k, o in enumerate((LR, 3 * LR)):
                pool.wait_ge(wl_done, after(k + 1))
                g.tensor_tensor(wst[o:o + LR, :], raw_s[o:o + LR, :], wst[o:o + LR, :].bitcast(F32), ALU.subtract).then_inc(wl_done, 1)
            pool.wait_ge(wl_done, after(3))
            g.memset(at[:], 0.0).then_inc(init_p, 1)

            def x_sum(c, p):
                n = c * NS + p
                pool.wait_ge(miu_t, n + after(1))
                pool.wait_ge(x5l_done, n + after(0) - 1)
                carry(pool, "pool")
                g.tensor_tensor(x5[:, SLOT[p], :].rearrange("p (b t) -> p b t", b=2), tmp_s[:, SLOT[p], :].rearrange("p (b t) -> p b t", b=2),
                                xTp[:, bass.ds(c * 2, 2), 1:S + 1], ALU.add).then_inc(xs_done, 1)

            with pool.Fori(0, NCH) as c:
                for p in range(NS):
                    x_sum(c, p)
            def group_rstd(c):
                for hf in range(2):
                    pool.wait_ge(gn_var, after(c * 2 + hf + 1))
                    g.tensor_scalar(gstat["ve"][:, hf, :], gstat["var"][:, hf, :], 1.0 / HD, 1e-5 * NH, ALU.mult, ALU.add).then_inc(gn_ve, 1)
                    pool.wait_ge(gn_ve, after(c * 2 + hf + 1))
                    g.tensor_tensor(gstat["rstd"][:, hf, :], gstat["ve"][:, hf, :], neghalf[:, 0:8], ALU.pow).then_inc(gn_rstd, 1)

            for c in range(NSC):
                for j in range(LEVELS - 1):
                    h = 1 << j
                    for q in range(2):
                        kqv, tv = halves(kq[:, GROUP[c][q]], h), total(c, j, q)
                        pool.wait_ge(lv[q], after(c * LEVELS + j + 1))
                        if j > 0:
                            pool.wait_ge(tot_up[q], after(c * (LEVELS - 2) + j))
                            pool.wait_ge(kq_up[q], after(c * (LEVELS - 1) + j))
                        g.tensor_tensor(kqv[:, :, 0, :], kqv[:, :, 0, :], bc(tv[:, :, 1], [P, CH // 2 // h, h]), ALU.mult).then_inc(kq_up[q], 1)
                        if j < LEVELS - 2:
                            pool.wait_ge(rp_up[q], after(c * (LEVELS - 1)))
                            g.tensor_tensor(tot[j + 1][:, q, :], tv[:, :, 0], tv[:, :, 1], ALU.mult).then_inc(tot_up[q], 1)
                    if c > 0 and j == 1:
                        group_rstd(c - 1)
            group_rstd(NSC - 1)

            def ctxT_low(b, par):
                pool.wait_ge(cth_done, b + after(1))
                g.tensor_tensor(ctl[:, par, :], ctxT[:, par, :], cth[:, par, :].bitcast(F32), ALU.subtract).then_inc(ctl_done, 1)

            def ctxn_masked(b, par, turn):
                pool.wait_ge(d_ctx[par], turn * 32 + 32)
                pool.wait_ge(cnh_done, b + after(0) - 1)
                pool.wait_ge(cnl_done, b + after(0) - 1)
                g.tensor_tensor(cnm[:, par], ctxn[:, par], bc(mask[:], [P, M // P, C]), ALU.mult).then_inc(cnm_done, 1)

            def ctxn_low(b, par):
                pool.wait_ge(cnh_done, b + after(1))
                g.tensor_tensor(cnl[:, par], cnm[:, par], cnh[:, par].bitcast(F32), ALU.subtract).then_inc(cnl_done, 1)

            pool.wait_ge(init_v, after(3))
            for b in range(2):
                ctxT_low(b, b)
                ctxn_masked(b, b, 0)
            ctxn_low(0, 0)
            norm_rstd(1)
            g.memset(combT[:], 1.0).then_inc(init_p, 1)
            pool.wait_ge(d_small, 96)
            g.tensor_tensor(xpb[:], xtok[:], pb_row[:].unsqueeze(1).to_broadcast([P, NT, C]), ALU.add).then_inc(xpb_done, 1)
            def context_turn(b, par, turn):
                ctxn_low(b + 1, 1 - par)
                ctxT_low(b + 2, par)
                ctxn_masked(b + 2, par, turn + 1)

            with pool.Fori(0, 2) as turn:
                for par in range(2):
                    context_turn(turn * 2 + par, par, turn)
            context_turn(4, 0, 2)
            norm_rstd(2, (0, 1))
            context_turn(5, 1, 2)
            ctxn_low(B - 1, 1)
            norm_rstd(2, (2, 3))

            def wf_low(n, par):
                pool.wait_ge(wfh_done, n + after(1))
                g.tensor_tensor(wfl[:, par, :], wf[:, par, :], wfh[:, par, :].bitcast(F32), ALU.subtract).then_inc(wfl_done, 1)

            def low_of(n, cc):
                pool.wait_ge(ah_done, n + after(1))
                pool.wait_ge(y2_pe, n + after(0) - 1)
                g.tensor_tensor(al[:, cc, :], aa[:, cc, :], ah[:, cc, :].bitcast(F32), ALU.subtract).then_inc(al_done, 1)

            def turn_of(hf, turn, first=False, last=False):
                for k in range(2 * WB):
                    e = hf * EX + turn * WB + k // 2
                    if not (first and k == 0):
                        low_of(e * 2 + k % 2 - 1, 1 - k % 2)
                    if k % 2 == 0 and not (last and k == 2 * WB - 2):
                        wf_low(e + 1, (k // 2 + 1) % WB)

            wf_low(0, 0)
            for hf in range(2):
                turn_of(hf, 0, first=(hf == 0))
                with pool.Fori(1, TURNS - 1) as turn:
                    turn_of(hf, turn)
                turn_of(hf, TURNS - 1, last=(hf == 1))
            low_of(4 * EX - 1, 1)

        @block.scalar
        def _(act):
            a = nc.scalar
            credit(act, "act")

            def norm_sq(k, chunks=range(NCH)):
                for c in chunks:
                    ti = slice(4 * c, 4 * c + 4)
                    act.wait_ge(ln_xc, after(k * NCH + c + 1))
                    a.activation(sq[:, ti], xc[:, ti], ACT.Square).then_inc(ln_sq, 1)

            act.preload_act_table(ACT.Exp)
            norm_sq(0)
            act.wait_ge(m_pe, after(1))
            a.activation(mqh[:], bank[7][:, 0:C], ACT.Copy).then_inc(m_act, 1)
            na = SPLIT["A"][1]
            act.wait_ge(d_split, 16)
            a.activation(wh_all[:, 0:na], raw[:, 0:na], ACT.Copy).then_inc(wh_done, 1)
            a.activation(wh_all[:, na:], raw[:, na:], ACT.Copy).then_inc(wh_done, 1)
            act.wait_ge(d_stack, 16)
            a.activation(wst[:], raw_s[:], ACT.Copy).then_inc(wh_done, 1)

            def x_in(c):
                act.wait_ge(tr, c + after(1))
                act.wait_ge(init_p, after(3))
                for q in range(2):
                    src = bank[0][:, q * S:(q + 1) * S].rearrange("p (h j) -> p h j", h=2)
                    dst = xTp[:, bass.ds(c * 2 + q, 1), 1:S + 1].rearrange("p o (j h) -> p (o h) j", h=2)
                    last = a.activation(dst, src, ACT.Copy)
                last.then_inc(tr_act, 1)

            def xx_high(c):
                act.wait_ge(xx_done, c + after(1))
                a.activation(xxh[:, bass.ds(c, 1), :].rearrange("p o n -> p (o n)"), xx[:], ACT.Copy).then_inc(xxh_done, 1)

            def tanh_of(c):
                hfv = HF[:, bass.ds(c * CH * NS, CH * NS)].rearrange("p (t i) -> p t i", i=NS)
                for i in range(NS):
                    act.wait_ge(h_pe, c * NS + after(i + 1))
                    a.activation(hfv[:, :, i], bank[1 + i][:], ACT.Tanh)
                    act.wait_ge(h_lo, c * NS + i + after(0) - 1)
                    a.activation(hT[HD:P, SLOT[i], :], bank[1 + i][HD:P, :], ACT.Tanh).then_inc(h_act, 1)

            x_in(0)
            xx_high(0)
            with act.Fori(0, NCH - 1) as c:
                x_in(c + 1)
                xx_high(c + 1)
                tanh_of(c)
            tanh_of(NCH - 1)

            def x_high(c, p):
                act.wait_ge(xs_done, c * NS + after(p + 1))
                a.activation(x5h[:, p, :], x5[:, SLOT[p], :], ACT.Copy).then_inc(x5h_done, 1)

            def project(c, nxt):
                cs = bass.ds(c * CH, CH)
                act.wait_ge(w1_pe, c + after(1))
                act.wait_ge(w2_pe, c + after(0))
                a.activation(w1s[:], bank[4][:], ACT.Tanh)
                a.activation(w1[HD:P, :], bank[4][HD:P, :], ACT.Tanh).then_inc(w1_act, 1)
                if nxt:
                    x_high(c + 1, 0)
                act.wait_ge(g1_pe, c + after(1))
                act.wait_ge(g_pe, c + after(0))
                a.activation(g1ah[:], bank[2][:], ACT.Tanh)
                a.activation(g1a[:], bank[2][:], ACT.Tanh)
                a.activation(g1bs[:], bank[3][:], ACT.Tanh)
                a.activation(g1b[HD:P, :], bank[3][HD:P, :], ACT.Tanh).then_inc(g1_act, 1)
                if nxt:
                    x_high(c + 1, 1)
                act.wait_ge(w2_pe, c + after(1))
                a.activation(dec[:, cs], bank[4][:], ACT.Exp, bias=col["td_miu"]).then_inc(dec_done, 1)
                if nxt:
                    x_high(c + 1, 2)
                act.wait_ge(r_pe, c + after(1))
                for hd in range(NH):
                    rows = slice(hd * HD, (hd + 1) * HD)
                    last = a.activation(rp[rows, hd, cs], bank[7][rows, :], ACT.Copy)
                last.then_inc(r_done, 1)
                act.wait_ge(g_pe, c + after(1))
                a.activation(gT[:, cs], bank[2][:], ACT.Copy).then_inc(g_done, 1)
                if nxt:
                    x_high(c + 1, 3)
                act.wait_ge(v_pe, c + after(1))
                a.activation(vv[:, bass.ds(c * 4, 4), :], bank[6][:].rearrange("p (i n) -> p i n", i=4), ACT.Copy).then_inc(v_done, 1)
                if nxt:
                    x_high(c + 1, 4)
                act.wait_ge(ds_pe, c + after(1))
                a.activation(dsum[:, bass.ds(c * 4, 4), :], bank[3][:, 0:4 * NH].rearrange("p (i n) -> p i n", i=4), ACT.Copy).then_inc(ds_done, 1)

            for p in range(NS):
                x_high(0, p)
            with act.Fori(0, NCH - 1) as c:
                project(c, True)
            project(NCH - 1, False)
            def group_square(c):
                for hf in range(2):
                    act.wait_ge(gn_xc, after(c * 2 + hf + 1))
                    a.activation(ysq[:, hf], yxc[:, hf], ACT.Square).then_inc(gn_sq, 1)

            for c in range(NSC):
                if c > 0:
                    group_square(c - 1)
                for q in range(2):
                    act.wait_ge(lv[q], after(c * LEVELS + MASKED + 1))
                    act.wait_ge(lv_at[q], after(c * MASKED + MASKED))
                    a.activation(at[0:HD, q, :, :, HD:P].rearrange("p k n t -> p (k n) t"),
                                 bank[q][0:HD, :].rearrange("p (k t) -> p k t", t=HD), ACT.Copy).then_inc(lv_act[q], 1)
                for q in range(2):
                    act.wait_ge(lv[q], after(c * LEVELS + LEVELS))
                    act.wait_ge(y_pe, after(c * SQ))
                    a.activation(at2[:, q].rearrange("p b n t -> p (b n t)"), bank[2 + q][:], ACT.Copy).then_inc(lv_act[q], 1)
            group_square(NSC - 1)
            def ctxT_high(b, par, turn):
                act.wait_ge(d_ctx[par], turn * 32 + 32)
                act.wait_ge(s_pe, 2 * b + after(0) - 2)
                a.activation(cth[:, par, :], ctxT[:, par, :], ACT.Copy).then_inc(cth_done, 1)

            def ctxn_high(b, par):
                act.wait_ge(cnm_done, b + after(1))
                act.wait_ge(t1_pe, b + after(0) - 1)
                a.activation(cnh[:, par], cnm[:, par], ACT.Copy).then_inc(cnh_done, 1)

            for b in range(2):
                ctxT_high(b, b, 0)
            ctxn_high(0, 0)
            a.activation(rth[:], W["rT"], ACT.Copy).then_inc(rth_done, 1)
            norm_sq(1)
            for c in range(NCH):
                act.wait_ge(tr, after(NCH + c + 1))
                for q in range(2):
                    src = bank[turned(1, c)][:, q * S:(q + 1) * S].rearrange("p (h j) -> p h j", h=2)
                    dst = xqh[:, c * CH + q * S:c * CH + (q + 1) * S].rearrange("p (j h) -> p h j", h=2)
                    last = a.activation(dst, src, ACT.Copy)
                last.then_inc(tr_act, 1)

            def q_high(b, par):
                act.wait_ge(q_pe, b + after(1))
                a.activation(qh[:, par, :], bank[2 * par][:, 0:S], ACT.Copy, scale=SCALE_QK).then_inc(q_act, 1)

            def x_probs(b, par):
                for i in range(2):
                    k = 2 * par + i
                    act.wait_ge(mx_done, 2 * b + after(i + 1))
                    act.wait_ge(t0_pe, 2 * b + after(0) - 2)
                    a.activation(pr[:, k, :], bank[k][:], ACT.Exp, bias=nmax[:, k:k + 1],
                                 accum_out=psum_[:, k:k + 1]).then_inc(ex_done, 1)

            def t0_high(b):
                for i in range(2):
                    act.wait_ge(t0_pe, 2 * b + after(i + 1))
                    act.wait_ge(t1_pe, b + after(0))
                    a.activation(t0h[:, 2 * i:2 * i + 2, :].rearrange("p k n -> p (k n)"), bank[5 + i][:], ACT.Copy).then_inc(t0_act, 1)

            def t1_copy(b):
                act.wait_ge(t1_pe, b + after(1))
                act.wait_ge(fin_pe, b + after(0))
                a.activation(t1s[:], bank[7][:, 0:2 * C], ACT.Copy).then_inc(t1_done, 1)

            def x_turn(b, par, turn, more, most, between=None):
                if more:
                    q_high(b + 1, 1 - par)
                t0_high(b)
                if more:
                    x_probs(b + 1, 1 - par)
                    ctxn_high(b + 1, 1 - par)
                if between:
                    between()
                t1_copy(b)
                if most:
                    ctxT_high(b + 2, par, turn + 1)

            def x_in3(c):
                act.wait_ge(tr, after(2 * NCH + c + 1))
                a.activation(xh[:, c * CH:(c + 1) * CH], bank[turned(2, c)][:], ACT.Copy).then_inc(tr_act, 1)

            def router_exp(h):
                act.wait_ge(lg_pe, after(h + 1))
                a.activation(R["e"][:, half_of(h)], bank[LOGITS[h]][:, 0:NT // 2 * E].rearrange("p (t e) -> p t e", e=E),
                             ACT.Exp, scale=-1.0).then_inc(lg_act, 1)

            def combine_rows(h, k, b_):
                act.wait_ge(ct_pe, after(2 * h + k + 1))
                act.wait_ge(init_p, after(5))
                o = (2 * h + k) * CH
                a.activation(combT[0:E, o:o + CH], bank[b_][0:E, :], ACT.Copy).then_inc(ct_act, 1)

            def combine_high(h):
                tok = slice(h * 2 * CH, (h + 1) * 2 * CH)
                act.wait_ge(ct_act, after(2 * h + 2))
                a.activation(combh[:, tok], combT[:, tok], ACT.Copy).then_inc(ch_done, 1)

            q_high(0, 0)
            x_probs(0, 0)
            with act.Fori(0, 2) as turn:
                for par in range(2):
                    x_turn(turn * 2 + par, par, turn, True, True)
            x_turn(4, 0, 2, True, True)
            norm_sq(2, (0, 1))
            x_turn(5, 1, 2, True, True)
            x_in3(0)
            x_turn(6, 0, 3, True, False, between=lambda: x_in3(1))
            router_exp(0)
            x_turn(7, 1, 3, False, False)
            combine_rows(0, 0, 0)
            combine_rows(0, 1, 1)
            combine_high(0)
            norm_sq(2, (2, 3))
            x_in3(2)
            x_in3(3)
            router_exp(1)
            act.preload_act_table(ACT.Silu)

            def wf_high(n, par, loads):
                act.wait_ge(d_wf[par], loads * 32)
                act.wait_ge(y2_pe, 2 * n + after(0) - 2 * (WB - 1))
                a.activation(wfh[:, par, :], wf[:, par, :], ACT.Copy).then_inc(wfh_done, 1)

            def silu_of(n, cc):
                act.wait_ge(h2_pe, n + after(1))
                act.wait_ge(stw_done, n + after(0) - 1)
                a.activation(sg[:, cc, :], bank[2 + cc][:], ACT.Silu).then_inc(sg_done, 1)

            def high_of(n, cc):
                act.wait_ge(aa_done, n + after(1))
                act.wait_ge(y2_pe, n + after(0) - 1)
                a.activation(ah[:, cc, :], aa[:, cc, :], ACT.Copy).then_inc(ah_done, 1)

            def turn_of(hf, turn, first=False, last=False, sums=None, combine=False):
                for k in range(2 * WB):
                    e = hf * EX + turn * WB + k // 2
                    silu_of(e * 2 + k % 2, k % 2)
                    if combine and k in (2, 4):
                        combine_rows(1, k // 2 - 1, 7)
                    if combine and k == 5:
                        combine_high(1)
                    if not (first and k == 0):
                        high_of(e * 2 + k % 2 - 1, 1 - k % 2)
                    if sums is not None and k == 1:
                        sums_out(sums)
                    if k % 2 == 0 and not (last and k == 2 * WB - 2):
                        par = (k // 2 + 1) % WB
                        loads = hf * TURNS + turn + (2 if k == 2 * WB - 2 else 1)
                        wf_high(e + 1, par, loads)

            def sums_out(hf):
                for cc in range(2):
                    act.wait_ge(yacc_pe, after(hf + 1))
                    act.wait_ge(yo_pe, after(hf * 2))
                    a.activation(yTs[:, cc, :], bank[cc][:], ACT.Copy).then_inc(yts_done, 1)

            wf_high(0, 0, 1)
            turn_of(0, 0, first=True)
            for turn in range(1, SIDE - 1):
                turn_of(0, turn)
            turn_of(0, SIDE - 1, combine=True)
            with act.Fori(SIDE, TURNS) as turn:
                turn_of(0, turn)
            turn_of(1, 0, sums=0)
            with act.Fori(1, TURNS - 1) as turn:
                turn_of(1, turn)
            turn_of(1, TURNS - 1, last=True)
            high_of(4 * EX - 1, 1)
            sums_out(1)

        @block.vector
        def _(dve):
            v = nc.vector
            credit(dve, "dve")
            v.memset(zero_r[:].bitcast(F32), 0.0).then_inc(init_v, 1)
            v.memset(one_r[:].bitcast(F32), 1.0).then_inc(init_v, 1)

            def centre(k, c):
                ti = slice(4 * c, 4 * c + 4)
                n = k * NCH + c + 1
                v.tensor_reduce(stat["sum"][:, ti], xtok[:, ti], X, ALU.add).then_inc(ln_sum, 1)
                dve.wait_ge(ln_sum, after(n))
                v.tensor_scalar(stat["mean"][:, ti], stat["sum"][:, ti], 1.0 / C, None, ALU.mult).then_inc(ln_mean, 1)
                dve.wait_ge(ln_mean, after(n))
                v.tensor_tensor(xc[:, ti], xtok[:, ti], bc(stat["mean"][:, ti], [P, 4, C]), ALU.subtract).then_inc(ln_xc, 1)

            def variance(k, c):
                ti = slice(4 * c, 4 * c + 4)
                dve.wait_ge(ln_sq, after(k * NCH + c + 1))
                v.tensor_reduce(stat["var"][:, ti], sq[:, ti], X, ALU.add).then_inc(ln_var, 1)

            def scaled(k, c):
                ti = slice(4 * c, 4 * c + 4)
                dve.wait_ge(ln_rstd, after(k * NCH + c + 1))
                dve.wait_ge(ln_xc, after(k * NCH + c + 1))
                v.tensor_tensor(xn[:, ti], xc[:, ti], bc(stat["rstd"][:, ti], [P, 4, C]), ALU.mult).then_inc(ln_xn, 1)

            def norm(k):
                for c in range(NCH + 2):
                    if c < NCH:
                        centre(k, c)
                    if 1 <= c <= NCH:
                        variance(k, c - 1)
                    if c >= 2:
                        scaled(k, c - 2)

            dve.wait_ge(d_x, 16)
            norm(0)
            dve.wait_ge(m_act, after(1))
            v.tensor_tensor(mql[:], bank[7][:, 0:C], mqh[:].bitcast(F32), ALU.subtract).then_inc(m_lo, 1)
            dve.wait_ge(wh_done, after(1))
            na = SPLIT["A"][1]
            v.tensor_tensor(wl_all[:, 0:na], raw[:, 0:na], wh_all[:, 0:na].bitcast(F32), ALU.subtract).then_inc(wla_done, 1)
            dve.wait_ge(d_w, 16)

            def shifted(c):
                two = bass.ds(c * 2, 2)
                dve.wait_ge(tr_act, c + after(1))
                v.tensor_tensor(bA[:, two, :], xTp[:, two, 0:S], xTp[:, two, 1:S + 1], ALU.subtract).then_inc(ba_done, 1)
                dve.wait_ge(ba_done, c + after(1))
                dve.wait_ge(xxh_done, c + after(0))
                dve.wait_ge(xxl_done, c + after(0))
                v.scalar_tensor_tensor(xx[:].rearrange("p (b t) -> p b t", b=2), bA[:, two, :], col["miu_x"], xTp[:, two, 1:S + 1],
                                       ALU.mult, ALU.add).then_inc(xx_done, 1)

            def xx_low(c):
                dve.wait_ge(xxh_done, c + after(1))
                of = lambda buf: buf[:, bass.ds(c, 1), :].rearrange("p o n -> p (o n)")
                v.tensor_tensor(of(xxl), xx[:], of(xxh).bitcast(F32), ALU.subtract).then_inc(xxl_done, 1)

            def h_low(c):
                hfv = HF[HD:P, bass.ds(c * CH * NS, CH * NS)].rearrange("p (t i) -> p t i", i=NS)
                for i in range(NS):
                    dve.wait_ge(h_act, c * NS + i + after(1))
                    v.tensor_tensor(hfv[:, :, i], hT[HD:P, SLOT[i], :], hfv[:, :, i].bitcast(F32), ALU.subtract).then_inc(h_lo, 1)

            shifted(0)
            xx_low(0)
            with dve.Fori(0, NCH - 1) as c:
                shifted(c + 1)
                xx_low(c + 1)
                h_low(c)
            h_low(NCH - 1)
            dve.wait_ge(d_small, 96)
            v.tensor_scalar(mask[:], mask_i[:], 0.0, None, ALU.not_equal).then_inc(init_v, 1)

            def shift(c, p):
                n = c * NS + p
                dve.wait_ge(miu_pe, n + after(1))
                dve.wait_ge(xs_done, n + after(0) - 1)
                v.scalar_tensor_tensor(tmp_s[:, SLOT[p], :].rearrange("p (b t) -> p b t", b=2),
                                       bank[p % 2][:].rearrange("p (b t) -> p b t", b=2), col[f"lam{STREAMS[p]}"],
                                       bA[:, bass.ds(c * 2, 2), :], ALU.add, ALU.mult).then_inc(miu_t, 1)

            def x_low(c, p):
                dve.wait_ge(x5h_done, c * NS + after(p + 1))
                v.tensor_tensor(x5l[:, p, :], x5[:, SLOT[p], :], x5h[:, p, :].bitcast(F32), ALU.subtract).then_inc(x5l_done, 1)

            def project(c, nxt):
                cs = bass.ds(c * CH, CH)
                if nxt:
                    shift(c + 1, 0)
                dve.wait_ge(w1_act, c + after(1))
                v.tensor_tensor(w1s[HD:P, :], w1[HD:P, :], w1s[HD:P, :].bitcast(F32), ALU.subtract).then_inc(w1_lo, 1)
                if nxt:
                    shift(c + 1, 1)
                    x_low(c + 1, 0)
                dve.wait_ge(g1_act, c + after(1))
                dve.wait_ge(g_pe, c + after(0))
                v.tensor_tensor(g1al[:], g1a[:], g1ah[:].bitcast(F32), ALU.subtract)
                v.tensor_tensor(g1bs[HD:P, :], g1b[HD:P, :], g1bs[HD:P, :].bitcast(F32), ALU.subtract).then_inc(g1_lo, 1)
                if nxt:
                    shift(c + 1, 2)
                    x_low(c + 1, 1)
                dve.wait_ge(k_pe, c + after(1))
                dve.wait_ge(dec_done, c + after(1))
                v.scalar_tensor_tensor(kq[:, cs], dec[:, cs], 1.0, bank[5][:], ALU.min, ALU.mult).then_inc(k_done, 1)
                if nxt:
                    shift(c + 1, 3)
                    x_low(c + 1, 2)
                dve.wait_ge(r_done, c + after(1))
                dve.wait_ge(k_done, c + after(1))
                dve.wait_ge(ds_pe, c + after(0))
                v.scalar_tensor_tensor(ruk[:], bank[7][:], col["u"], kq[:, cs], ALU.mult, ALU.mult).then_inc(ruk_done, 1)
                if nxt:
                    shift(c + 1, 4)
                    x_low(c + 1, 3)
                    x_low(c + 1, 4)

            for p in range(NS):
                shift(0, p)
                if p > 0:
                    x_low(0, p - 1)
            x_low(0, NS - 1)
            with dve.Fori(0, NCH - 1) as c:
                project(c, True)
            project(NCH - 1, False)
            def group_centre(c):
                for hf in range(2):
                    dve.wait_ge(y_done, after(c * SQ + 2 * hf + 2))
                    v.tensor_reduce(gstat["sum"][:, hf, :], yc[:, hf], X, ALU.add).then_inc(gn_sum, 1)
                for hf in range(2):
                    dve.wait_ge(gn_sum, after(c * 2 + hf + 1))
                    v.tensor_scalar(gstat["mean"][:, hf, :], gstat["sum"][:, hf, :], 1.0 / HD, None, ALU.mult).then_inc(gn_mean, 1)
                for hf in range(2):
                    dve.wait_ge(gn_mean, after(c * 2 + hf + 1))
                    v.tensor_tensor(yxc[:, hf], yc[:, hf], bc(gstat["mean"][:, hf, :], [P, 8, HD]), ALU.subtract).then_inc(gn_xc, 1)

            def group_variance(c):
                for hf in range(2):
                    dve.wait_ge(gn_sq, after(c * 2 + hf + 1))
                    v.tensor_reduce(gstat["var"][:, hf, :], ysq[:, hf], X, ALU.add).then_inc(gn_var, 1)

            def group_scaled(c):
                for hf in range(2):
                    dve.wait_ge(gn_rstd, after(c * 2 + hf + 1))
                    dve.wait_ge(gn_xc, after(c * 2 + hf + 1))
                    v.tensor_tensor(yn[:, hf], yxc[:, hf], bc(gstat["rstd"][:, hf, :], [P, 8, HD]), ALU.mult).then_inc(gn_yn, 1)

            def gated(c):
                for hf in range(2):
                    dve.wait_ge(yt_pe, after(c * 2 + hf + 1))
                    dve.wait_ge(wo_pe, after(c * 2))
                    v.tensor_scalar(z1[:, hf, :], bank[4 + hf][:], col["gamma"], col["beta"], ALU.mult, ALU.add).then_inc(z1_done, 1)
                for hf in range(2):
                    dve.wait_ge(z1_done, after(c * 2 + hf + 1))
                    v.tensor_tensor(z[:, hf, :], z1[:, hf, :], gT[:, GROUP[c][hf]], ALU.mult).then_inc(z_done, 1)

            def residual(c):
                for hf in range(2):
                    dve.wait_ge(wo_pe, after(c * 2 + hf + 1))
                    xt4 = xtok[:, c * 8 + hf * 4:c * 8 + hf * 4 + 4, :]
                    v.tensor_tensor(xt4, xt4, bank[6 + hf][:].rearrange("p (i n) -> p i n", i=4), ALU.add).then_inc(x1_done, 1)

            TAIL = {0: group_centre, 1: group_variance, 2: group_scaled, 4: gated, 6: residual}
            dve.wait_ge(init_p, after(4))
            dve.wait_ge(d_small, 96)
            for c in range(NSC):
                for j in range(LEVELS - 1):
                    h = 1 << j
                    for q in range(2):
                        dve.wait_ge(lv[q], after(c * LEVELS + j + 1))
                        if 0 < j < MASKED:
                            dve.wait_ge(lv_at[q], after(c * MASKED + j))
                        rpv = rp[:, :, GROUP[c][q]].rearrange("p k (n two h) -> p k n two h", two=2, h=h)[:, :, :, 1, :]
                        if j > 0:
                            dve.wait_ge(tot_up[q], after(c * (LEVELS - 2) + j))
                            dve.wait_ge(rp_up[q], after(c * (LEVELS - 1) + j))
                        before = total(c, j, q)[:, :, 0].unsqueeze(1).unsqueeze(3).to_broadcast([P, NH, CH // 2 // h, h])
                        v.tensor_tensor(rpv, rpv, before, ALU.mult).then_inc(rp_up[q], 1)
                        if j == 0:
                            dve.wait_ge(y_pe, after(c * SQ))
                        if j < MASKED:
                            n = P // (2 * h)
                            dst = at[:, q].rearrange("p k m (n two h) -> p (k m) n two h", two=2, h=h)[:, :, :, 1, :]
                            src = bank[2 * (j % 2) + q][:].rearrange("p (k n h) -> p k n h", k=4 * NH, h=h)
                            msk = lvl[:, j, :].rearrange("p (n h) -> p n h", h=h).unsqueeze(1).to_broadcast([P, 4 * NH, n, h])
                            v.copy_predicated(dst, msk, src).then_inc(lv_at[q], 1)
                    if c > 0 and j in TAIL:
                        TAIL[j](c - 1)
                for q in range(SQ):
                    hf = q // 2
                    dve.wait_ge(y_pe, after(c * SQ + q + 1))
                    dve.wait_ge(gn_yn, after(c * 2))
                    for k in range(2):
                        for hd in range(NH):
                            tile = c * (2 * SQ) + q * 2 + k
                            last = v.scalar_tensor_tensor(yc[:, hf, (q % 2 * 2 + k) * 2 + hd, :],
                                                          vv[:, tile, hd * HD:(hd + 1) * HD], dsum[:, tile, hd:hd + 1],
                                                          bank[4 + q][:, (2 * k + hd) * HD:(2 * k + hd + 1) * HD], ALU.mult, ALU.add)
                    last.then_inc(y_done, 1)
            for stage in TAIL.values():
                stage(NSC - 1)
            dve.wait_ge(x1_done, after(NCH))
            norm(1)

            for c in range(NCH):
                dve.wait_ge(tr_act, after(NCH + c + 1))
                for q in range(2):
                    of = slice(c * CH + q * S, c * CH + (q + 1) * S)
                    src = bank[turned(1, c)][:, q * S:(q + 1) * S].rearrange("p (h j) -> p h j", h=2)
                    last = v.tensor_tensor(xql[:, of].rearrange("p (j h) -> p h j", h=2), src,
                                           xqh[:, of].bitcast(F32).rearrange("p (j h) -> p h j", h=2), ALU.subtract)
                last.then_inc(tr_dve, 1)

            dve.wait_ge(rth_done, after(1))
            v.tensor_tensor(rtl[:], W["rT"], rth[:].bitcast(F32), ALU.subtract).then_inc(rtl_done, 1)

            def q_low(b, par):
                dve.wait_ge(q_act, b + after(1))
                v.scalar_tensor_tensor(ql[:, par, :], bank[2 * par][:, 0:S], SCALE_QK, qh[:, par, :].bitcast(F32),
                                       ALU.mult, ALU.subtract).then_inc(q_lo, 1)

            def x_max(b, par):
                for i in range(2):
                    k = 2 * par + i
                    dve.wait_ge(s_pe, 2 * b + after(i + 1))
                    v.tensor_reduce(nmax[:, k:k + 1], bank[k][:], X, ALU.max, negate=True).then_inc(mx_done, 1)

            def x_scales(b, par):
                for i in range(2):
                    k = 2 * par + i
                    dve.wait_ge(ex_done, 2 * b + after(i + 1))
                    v.reciprocal(rsum[:, k:k + 1], psum_[:, k:k + 1]).then_inc(rs_done, 1)
                for i in range(2):
                    k = 2 * par + i
                    dve.wait_ge(rs_done, 2 * b + after(i + 1))
                    dve.wait_ge(t0_pe, 2 * b + after(0))
                    v.tensor_scalar(pws[:, i, :], W["pwT"], rsum[:, k:k + 1], None, ALU.mult).then_inc(pws_done, 1)

            def t0_low(b):
                for i in range(2):
                    dve.wait_ge(t0_act, 2 * b + after(i + 1))
                    half = slice(2 * i, 2 * i + 2)
                    flat = lambda buf: buf[:, half, :].rearrange("p k n -> p (k n)")
                    v.tensor_tensor(flat(t0l), bank[5 + i][:], flat(t0h).bitcast(F32), ALU.subtract).then_inc(t0_lo, 1)

            def x_sum(b):
                dve.wait_ge(fin_pe, b + after(1))
                dve.wait_ge(xpb_done, after(1))
                v.tensor_tensor(xtok[:, bass.ds(b * 2, 2), :], xpb[:, bass.ds(b * 2, 2), :],
                                bank[7][:, 2 * C:4 * C].rearrange("p (i n) -> p i n", i=2), ALU.add).then_inc(x2_done, 1)

            def x_turn(b, par, more, between=None):
                if more:
                    q_low(b + 1, 1 - par)
                t0_low(b)
                if more:
                    x_max(b + 1, 1 - par)
                    x_scales(b + 1, 1 - par)
                if between:
                    between()
                x_sum(b)

            def x_in3(c):
                of = slice(c * CH, (c + 1) * CH)
                dve.wait_ge(tr_act, after(2 * NCH + c + 1))
                v.tensor_tensor(xl[:, of], bank[turned(2, c)][:], xh[:, of].bitcast(F32), ALU.subtract).then_inc(tr_dve, 1)

            count = [0]

            def step(ins):
                count[0] += 1
                ins.then_inc(chain, 1)
                dve.wait_ge(chain, after(count[0]))

            NH2 = NT // 2

            def of_half(h):
                groups = slice(h * NH2 * NG, (h + 1) * NH2 * NG)
                r = {n: buf[:, half_of(h)] for n, buf in R.items()}
                r.update({n: buf[:, groups] for n, buf in (("pair", pair), ("gs", gs), ("grk", grk), ("gm", gm), ("gm1", gm1))})
                r.update({n: buf[:, half_of(h)] for n, buf in (("ggt", ggt), ("geq", geq), ("top8", top8), ("ngt", ngt),
                                                                ("tws", tws), ("twr", twr))})
                r["s4"] = r["s"].rearrange("p t (g k) -> p (t g) k", k=EPG)
                r["m4"] = r["m"].rearrange("p t (g k) -> p (t g) k", k=EPG)
                return r

            def router_scores(h):
                r = of_half(h)
                dve.wait_ge(lg_act, after(h + 1))
                step(v.tensor_scalar(r["e1"], r["e"], 1.0, None, ALU.add))
                step(v.reciprocal(r["sc"], r["e1"]))
                step(v.tensor_tensor(r["s"], r["sc"], bias_row[:].unsqueeze(1).to_broadcast([P, NH2, E]), ALU.add))
                s4, pr6 = r["s4"], r["pair"]
                v.tensor_tensor(pr6[:, :, 0:3], s4[:, :, 0:3], s4[:, :, 1:4], ALU.add)
                v.tensor_tensor(pr6[:, :, 3:5], s4[:, :, 0:2], s4[:, :, 2:4], ALU.add)
                step(v.tensor_tensor(pr6[:, :, 5:6], s4[:, :, 0:1], s4[:, :, 3:4], ALU.add))
                step(v.tensor_reduce(r["gs"], pr6, X, ALU.max))

            def router_ranks(h):
                r = of_half(h)
                g3 = r["gs"].rearrange("p (t g) -> p t g", g=NG)
                other = g3.unsqueeze(2).to_broadcast([P, NH2, NG, NG])
                own = g3.unsqueeze(3).to_broadcast([P, NH2, NG, NG])
                v4 = lambda t: t.rearrange("p t (g k) -> p t g k", k=NG)
                v.tensor_tensor(v4(r["ggt"]), other, own, ALU.is_gt)
                step(v.tensor_tensor(v4(r["geq"]), other, own, ALU.is_equal))
                step(v.tensor_tensor(r["geq"], r["geq"], tri[:].unsqueeze(1).to_broadcast([P, NH2, NG * NG]), ALU.mult))
                step(v.tensor_tensor(r["ggt"], r["ggt"], r["geq"], ALU.add))
                step(v.tensor_reduce(r["grk"], r["ggt"].rearrange("p t (g k) -> p (t g) k", k=NG), X, ALU.add))
                step(v.tensor_scalar(r["gm"], r["grk"], float(TOPG), None, ALU.is_lt))

            def router_top(h):
                r = of_half(h)
                step(v.tensor_scalar(r["gm1"], r["gm"], -1.0, None, ALU.add))
                step(v.tensor_tensor(r["m4"], r["s4"], bc(r["gm"], [P, NH2 * NG, EPG]), ALU.mult))
                step(v.tensor_tensor(r["m4"], r["m4"], bc(r["gm1"], [P, NH2 * NG, EPG]), ALU.add))
                for t in range(NH2):
                    last = v.max(r["top8"][:, t, :], r["m"][:, t, :])
                step(last)

            def router_chosen(h):
                r = of_half(h)
                fourth = r["top8"][:, :, TOPK - 1:TOPK].to_broadcast([P, NH2, E])
                v.tensor_tensor(r["gt"], r["m"], fourth, ALU.is_gt)
                step(v.tensor_tensor(r["eq"], r["m"], fourth, ALU.is_equal))
                v.tensor_reduce(r["ngt"], r["gt"], X, ALU.add)
                fl = lambda t: t.rearrange("p t e -> p (t e)")
                step(v.tensor_copy(r["le"], seg[:].unsqueeze(1).to_broadcast([P, NH2, E])))
                step(v.tensor_tensor_scan(fl(r["cum"]), fl(r["le"]), fl(r["eq"]), 0.0, ALU.mult, ALU.add))
                step(v.tensor_tensor(r["cum"], r["cum"], bc(r["ngt"], [P, NH2, E]), ALU.add))
                step(v.scalar_tensor_tensor(fl(r["le"]), fl(r["cum"]), float(TOPK), fl(r["eq"]), ALU.is_le, ALU.mult))
                step(v.tensor_tensor(r["sel"], r["gt"], r["le"], ALU.add))

            def router_weights(h):
                r = of_half(h)
                step(v.tensor_tensor(r["tw"], r["sc"], r["sel"], ALU.mult))
                step(v.tensor_reduce(r["tws"], r["tw"], X, ALU.add))
                step(v.tensor_scalar(r["tws"], r["tws"], 1e-20, None, ALU.add))
                step(v.reciprocal(r["twr"], r["tws"]))
                step(v.tensor_tensor(r["tw"], r["tw"], bc(r["twr"], [P, NH2, E]), ALU.mult))
                step(v.tensor_scalar(r["tw"], r["tw"], SCALE_TW, None, ALU.mult))
                assert count[0] == (h + 1) * N_ROUTER

            def combine_low(h):
                tok = slice(h * 2 * CH, (h + 1) * 2 * CH)
                dve.wait_ge(ch_done, after(h + 1))
                v.tensor_tensor(combl[:, tok], combT[:, tok], combh[:, tok].bitcast(F32), ALU.subtract).then_inc(cl_done, 1)

            def norm3_centre(h):
                for c in (2 * h, 2 * h + 1):
                    dve.wait_ge(x2_done, after(2 * c + 2))
                    centre(2, c)

            def norm3_scaled(h):
                for c in (2 * h, 2 * h + 1):
                    scaled(2, c)

            q_low(0, 0)
            x_max(0, 0)
            x_scales(0, 0)
            with dve.Fori(0, 2) as turn:
                for par in range(2):
                    x_turn(turn * 2 + par, par, True)
            x_turn(4, 0, True)
            norm3_centre(0)
            variance(2, 0)
            variance(2, 1)
            x_turn(5, 1, True, between=lambda: norm3_scaled(0))
            x_in3(0)
            x_turn(6, 0, True, between=lambda: x_in3(1))
            x_turn(7, 1, False, between=lambda: router_scores(0))
            router_ranks(0)
            router_top(0)
            router_chosen(0)
            router_weights(0)
            norm3_centre(1)
            combine_low(0)
            variance(2, 2)
            variance(2, 3)
            norm3_scaled(1)
            x_in3(2)
            x_in3(3)

            def weigh_of(n, cc):
                dve.wait_ge(sg_done, n + after(1))
                dve.wait_ge(tw_pe, n + after(1))
                dve.wait_ge(aa_done, n + after(0) - 1)
                v.tensor_tensor(stw[:, cc, :], sg[:, cc, :], bank[6][:], ALU.mult).then_inc(stw_done, 1)
                dve.wait_ge(stw_done, n + after(1))
                dve.wait_ge(u2_pe, n + after(1))
                dve.wait_ge(al_done, n + after(0) - 1)
                v.tensor_tensor(aa[:, cc, :], stw[:, cc, :], bank[4 + cc][:], ALU.mult).then_inc(aa_done, 1)

            def turn_of(hf, turn, beside=()):
                for k in range(2 * WB):
                    weigh_of((hf * EX + turn * WB) * 2 + k, k % 2)
                    if k in beside:
                        beside[k]()

            def add_sums(hf, cc, b_):
                dve.wait_ge(yo_pe, after(hf * 2 + cc + 1))
                o = xtok[:, hf * 8 + cc * 4:hf * 8 + cc * 4 + 4, :]
                v.tensor_tensor(o, o, bank[b_][:].rearrange("p (i n) -> p i n", i=4), ALU.add).then_inc(out_done, 1)

            turn_of(0, 0, {3: lambda: router_scores(1)})
            turn_of(0, 1, {0: lambda: router_ranks(1), 3: lambda: router_top(1)})
            turn_of(0, 2, {0: lambda: router_chosen(1), 3: lambda: router_weights(1)})
            turn_of(0, 3)
            combine_low(1)
            with dve.Fori(SIDE, TURNS) as turn:
                turn_of(0, turn)
            turn_of(1, 0, {3: lambda: add_sums(0, 0, 7), 5: lambda: add_sums(0, 1, 7)})
            with dve.Fori(1, TURNS) as turn:
                turn_of(1, turn)
            for cc in range(2):
                add_sums(1, cc, 2 + cc)

        @block.tensor
        def _(pe):
            t = nc.tensor
            credit(pe, "pe")
            pe.wait_ge(d_w, 16)

            t.matmul(bank[7][:, 0:C], W["wq"], W["wk"], start=True, stop=True).then_inc(m_pe, 1)

            def transpose_chunk(c, k):
                for i in range(4):
                    last = t.transpose(bank[turned(k, c)][:, i * P:(i + 1) * P], xn[:, c * 4 + i, :], ident)
                last.then_inc(tr, 1)

            def split_mm(dst, wh, wl, mh, ml, first, last_):
                t.matmul(dst, wh, mh, start=first, stop=False)
                t.matmul(dst, wh, ml, start=False, stop=False)
                return t.matmul(dst, wl, mh, start=False, stop=last_)

            def h_blocks(c):
                pe.wait_ge(xxl_done, after(c + 1))
                for i in range(NS):
                    pe.wait_ge(h_act, after(c * NS + i) - NS + 1)
                    bl = slice(i * P, (i + 1) * P)
                    split_mm(bank[1 + i][:], WH["A"][:, bl], WL["A"][:, bl], xxh[:, c, :], xxl[:, c, :], True, True).then_inc(h_pe, 1)

            for c in range(NCH):
                pe.wait_ge(ln_xn, after(c + 1))
                pe.wait_ge(tr_act, after(c))
                transpose_chunk(c, 0)
                if c == 1:
                    pe.wait_ge(wla_done, after(1))
                if c > 0:
                    h_blocks(c - 1)
            h_blocks(NCH - 1)
            pe.wait_ge(h_lo, after(NCH * NS))
            pe.wait_ge(wl_done, after(3))

            def miu(c, p):
                n = c * NS + p
                pe.wait_ge(miu_t, n + after(0) - (1 if p else 0))
                s = STREAMS[p]
                t.matmul(bank[p % 2][:], wst[:, s * C:(s + 1) * C], HF[:, bass.ds(c * CH + s * T, CH)],
                         start=True, stop=True).then_inc(miu_pe, 1)

            def project(c, nxt):
                def of(name, dst, p):
                    return split_mm(dst, WH[name], WL[name], x5h[:, p, :], x5l[:, p, :], True, True)

                def got(p):
                    pe.wait_ge(x5l_done, c * NS + after(p + 1))

                got(0)
                pe.wait_ge(dec_done, c + after(0))
                of("tdA", bank[4][:], 0).then_inc(w1_pe, 1)
                if nxt:
                    miu(c + 1, 0)
                got(1)
                pe.wait_ge(g_done, c + after(0))
                of("Wg1a", bank[2][:], 1)
                pe.wait_ge(ds_done, c + after(0))
                of("Wg1b", bank[3][:], 1).then_inc(g1_pe, 1)
                if nxt:
                    miu(c + 1, 1)
                got(2)
                pe.wait_ge(k_done, c + after(0))
                of("WkT", bank[5][:], 2).then_inc(k_pe, 1)
                pe.wait_ge(w1_lo, c + after(1))
                t.matmul(bank[4][:], WH["tdB"], w1s[:], start=True, stop=False)
                t.matmul(bank[4][:], WL["tdB"], w1s[:], start=False, stop=True).then_inc(w2_pe, 1)
                if nxt:
                    miu(c + 1, 2)
                got(3)
                pe.wait_ge(ruk_done, c + after(0))
                of("WrT", bank[7][:], 3).then_inc(r_pe, 1)
                if nxt:
                    miu(c + 1, 3)
                pe.wait_ge(g1_lo, c + after(1))
                split_mm(bank[2][:], WH["Wg2a"], WL["Wg2a"], g1ah[:], g1al[:], True, False)
                t.matmul(bank[2][:], wst[:, NS * C:NS * C + C], g1bs[:], start=False, stop=True).then_inc(g_pe, 1)
                if nxt:
                    miu(c + 1, 4)
                got(4)
                pe.wait_ge(v_done, c + after(0))
                for i in range(4):
                    ts = slice(i * P, (i + 1) * P)
                    last = split_mm(bank[6][:, i * C:(i + 1) * C], x5h[:, 4, ts], x5l[:, 4, ts], WH["WvT"], WL["WvT"], True, True)
                last.then_inc(v_pe, 1)
                pe.wait_ge(ruk_done, c + after(1))
                for i in range(4):
                    last = t.matmul(bank[3][:, i * NH:(i + 1) * NH], ruk[:, i * P:(i + 1) * P], W["hsel"], start=True, stop=True)
                last.then_inc(ds_pe, 1)

            for p in range(NS):
                miu(0, p)
            with pe.Fori(0, NCH - 1) as c:
                project(c, True)
            project(NCH - 1, False)
            pe.wait_ge(ds_done, after(NCH))
            pe.wait_ge(g_done, after(NCH))
            def group_turned(c):
                for hf in range(2):
                    pe.wait_ge(gn_yn, after(c * 2 + hf + 1))
                    for i in range(4):
                        last = t.transpose(bank[4 + hf][:, i * P:(i + 1) * P], yn[:, hf, 2 * i:2 * i + 2, :].rearrange("p a b -> p (a b)"), ident)
                    last.then_inc(yt_pe, 1)

            def out_product(c):
                for hf in range(2):
                    pe.wait_ge(z_done, after(c * 2 + hf + 1))
                    zv = z[:, hf, :].rearrange("p (q j h) -> p q h j", q=2, h=2)
                    for q in range(2):
                        for hh in range(2):
                            i = 2 * q + hh
                            last = t.matmul(bank[6 + hf][:, i * C:(i + 1) * C], zv[:, q, hh, :], W["WoT"], start=True, stop=True)
                    last.then_inc(wo_pe, 1)

            for c in range(NSC):
                for j in range(LEVELS):
                    h = 1 << j
                    for q in range(2):
                        if j > 0:
                            pe.wait_ge(rp_up[q], after(c * (LEVELS - 1) + j))
                            pe.wait_ge(kq_up[q], after(c * (LEVELS - 1) + j))
                        if j < 2:
                            pe.wait_ge(lv_act[q], after(c * 2))
                        else:
                            pe.wait_ge(lv_at[q], after(c * MASKED + j - 1))
                        dst = bank[2 * (j % 2) + q]
                        t0 = c * (SQ * S) + q * CH
                        if j == LEVELS - 1:
                            for b in range(2):
                                o = t0 + b * S
                                last = t.matmul(dst[:, b * S:(b + 1) * S].rearrange("p (n t) -> p n t", n=NH), kq[:, o:o + P],
                                                rp[:, :, o + P:o + 2 * P], start=True, stop=True)
                        else:
                            m = P if j < MASKED else HD
                            for k in range(4):
                                o = t0 + k * P
                                odd = rp[:, :, o:o + P].rearrange("p m (n two h) -> p m n two h", two=2, h=h)[:, :, :, 1, :]
                                last = t.matmul(dst[0:m, k * P:(k + 1) * P].rearrange("p (m n h) -> p m n h", m=NH, h=h),
                                                kq[:, o:o + m], odd, start=True, stop=True)
                        last.then_inc(lv[q], 1)
                    if c > 0 and j == 3:
                        group_turned(c - 1)
                    if c > 0 and j == 5:
                        out_product(c - 1)
                pe.wait_ge(x1_done, after(c * 2))
                for q in range(SQ):
                    grp, b = q // 2, q % 2
                    pe.wait_ge(lv_at[grp], after(c * MASKED + MASKED))
                    pe.wait_ge(lv_act[grp], after(c * 2 + 2))
                    for k in range(2):
                        for hd in range(NH):
                            dst = bank[4 + q][:, (2 * k + hd) * HD:(2 * k + hd + 1) * HD]
                            vt = lambda kk: vv[:, c * (2 * SQ) + q * 2 + kk, hd * HD:(hd + 1) * HD]
                            last = t.matmul(dst, at[:, grp, 2 * b + k, hd, :], vt(k), start=True, stop=(k == 0))
                            if k == 1:
                                last = t.matmul(dst, at2[:, grp, b, hd, :], vt(0), start=False, stop=True)
                    last.then_inc(y_pe, 1)
            group_turned(NSC - 1)
            out_product(NSC - 1)
            for c in range(NCH):
                pe.wait_ge(ln_xn, after(NCH + c + 1))
                pe.wait_ge(tr_act, after(NCH))
                pe.wait_ge(tr_dve, after(c) - 1)
                transpose_chunk(c, 1)
            pe.wait_ge(tr_dve, after(NCH))
            pe.wait_ge(x1_done, after(NCH))
            pe.wait_ge(m_lo, after(1))

            def project_q(b, par):
                pe.wait_ge(ex_done, 2 * b + after(0) - 2)
                tok = bass.ds(b * S, S)
                split_mm(bank[2 * par][:, 0:S], mqh[:], mql[:], xqh[:, tok], xql[:, tok], True, True).then_inc(q_pe, 1)

            def scores(b, par):
                pe.wait_ge(q_lo, b + after(1))
                pe.wait_ge(ctl_done, b + after(1))
                for i in range(2):
                    n = slice(i * P, (i + 1) * P)
                    split_mm(bank[2 * par + i][:], qh[:, par, n], ql[:, par, n], cth[:, par, :], ctl[:, par, :], True, True).then_inc(s_pe, 1)

            def x_t0(b, par):
                pe.wait_ge(pws_done, 2 * b + after(2))
                for half in range(2):
                    pe.wait_ge(t0_lo, 2 * b + after(half) - 1)
                    for k in range(2):
                        for i in range(2):
                            m = slice((2 * half + k) * P, (2 * half + k + 1) * P)
                            last = t.matmul(bank[5 + half][:, (2 * k + i) * C:(2 * k + i + 1) * C], pr[:, 2 * par + i, m], pws[:, i, :],
                                            start=True, stop=True)
                    last.then_inc(t0_pe, 1)

            def x_rest(b, par):
                pe.wait_ge(x2_done, b + after(0))
                pe.wait_ge(cnl_done, b + after(1))
                for k in range(4):
                    if k % 2 == 0:
                        pe.wait_ge(t0_lo, 2 * b + after(k // 2 + 1))
                    last = split_mm(bank[7][:, 0:2 * C], cnh[:, par, k, :], cnl[:, par, k, :], t0h[:, k, :], t0l[:, k, :], k == 0, k == 3)
                last.then_inc(t1_pe, 1)
                pe.wait_ge(t1_done, b + after(1))
                t.matmul(bank[7][:, 2 * C:4 * C], W["xvT"], t1s[:], start=True, stop=True).then_inc(fin_pe, 1)

            def x_turn(b, par, more, between=None):
                if more:
                    project_q(b + 1, 1 - par)
                x_t0(b, par)
                if more:
                    scores(b + 1, 1 - par)
                if between:
                    between()
                x_rest(b, par)

            def turn3(c):
                pe.wait_ge(ln_xn, after(2 * NCH + c + 1))
                pe.wait_ge(tr_dve, after(NCH + c))
                transpose_chunk(c, 2)

            def logits(h):
                pe.wait_ge(tr_dve, after(NCH + 2 * h + 2))
                pe.wait_ge(rtl_done, after(1))
                for i in range(NT // 2):
                    o = (h * (NT // 2) + i) * P
                    last = split_mm(bank[LOGITS[h]][:, i * E:(i + 1) * E], xh[:, o:o + P], xl[:, o:o + P], rth[:], rtl[:], True, True)
                last.then_inc(lg_pe, 1)

            def combine_turned(h, k, b_):
                pe.wait_ge(chain, after((h + 1) * N_ROUTER))
                for i in range(4):
                    last = t.transpose(bank[b_][0:E, i * P:(i + 1) * P], R["tw"][:, h * (NT // 2) + 4 * k + i, :], ident)
                last.then_inc(ct_pe, 1)

            project_q(0, 0)
            scores(0, 0)
            with pe.Fori(0, 2) as turn:
                for par in range(2):
                    x_turn(turn * 2 + par, par, True)
            x_turn(4, 0, True)
            x_turn(5, 1, True)
            turn3(0)
            x_turn(6, 0, True, between=lambda: turn3(1))
            logits(0)
            x_turn(7, 1, False)
            for k in range(2):
                combine_turned(0, k, k)
            turn3(2)
            turn3(3)
            logits(1)

            def front(hf, n, par, cc):
                cs = slice((hf * 2 + cc) * CH, (hf * 2 + cc + 1) * CH)
                wh = lambda m: wfh[:, par, m * C:(m + 1) * C]
                wl = lambda m: wfl[:, par, m * C:(m + 1) * C]
                pe.wait_ge(sg_done, n + after(0) - 1)
                split_mm(bank[2 + cc][:], wh(0), wl(0), xh[:, cs], xl[:, cs], True, True).then_inc(h2_pe, 1)
                pe.wait_ge(aa_done, n + after(0) - 1)
                split_mm(bank[4 + cc][:], wh(1), wl(1), xh[:, cs], xl[:, cs], True, True).then_inc(u2_pe, 1)
                pe.wait_ge(stw_done, n + after(0))
                t.matmul(bank[6][:], one_r[:], twrow[:, par, cc * CH:(cc + 1) * CH], start=True, stop=True).then_inc(tw_pe, 1)

            def back(n, par, cc):
                pe.wait_ge(al_done, n + after(1))
                split_mm(bank[cc][:], wfh[:, par, 2 * C:3 * C], wfl[:, par, 2 * C:3 * C], ah[:, cc, :], al[:, cc, :],
                         False, False).then_inc(y2_pe, 1)

            def clear_sums(hf):
                pe.wait_ge(ct_act, after(2))
                pe.wait_ge(yts_done, after(hf * 2))
                for cc in range(2):
                    t.matmul(bank[cc][:], zero_r[:, 0:P], zero_r[:], start=True, stop=False)

            def close_sums():
                for cc in range(2):
                    last = t.matmul(bank[cc][:], zero_r[:, 0:P], zero_r[:], start=False, stop=True)
                last.then_inc(yacc_pe, 1)

            def turn_sums(hf, cc, b_):
                pe.wait_ge(yts_done, after(hf * 2 + cc + 1))
                if hf == 0:
                    pe.wait_ge(out_done, after(cc))
                for i in range(4):
                    last = t.transpose(bank[b_][:, i * P:(i + 1) * P], yTs[:, cc, i * P:(i + 1) * P], ident)
                last.then_inc(yo_pe, 1)

            def turn_of(hf, turn, first=False, beside=()):
                for k in range(2 * WB):
                    e = hf * EX + turn * WB + k // 2
                    n = (hf * EX + turn * WB) * 2 + k
                    if k % 2 == 0:
                        pe.wait_ge(wfl_done, e + after(1))
                    front(hf, n, k // 2, k % 2)
                    if first and k == 2:
                        clear_sums(hf)
                    if not (first and hf == 0 and k < 2):
                        back(n - 2, (k - 2) % (2 * WB) // 2, k % 2)
                    if first and hf == 1 and k == 1:
                        close_sums()
                    if k in beside:
                        beside[k]()

            turn_of(0, 0, first=True)
            turn_of(0, 1)
            turn_of(0, 2)

            def second_combine(k):
                pe.wait_ge(lg_act, after(2))
                pe.wait_ge(ct_act, after(2 + k))
                combine_turned(1, k, 7)

            turn_of(0, 3, beside={1: lambda: second_combine(0), 3: lambda: second_combine(1)})
            with pe.Fori(SIDE, TURNS) as turn:
                turn_of(0, turn)
            pe.wait_ge(ct_act, after(4))
            turn_of(1, 0, first=True, beside={3: lambda: turn_sums(0, 0, 7), 5: lambda: turn_sums(0, 1, 7)})
            with pe.Fori(1, TURNS) as turn:
                turn_of(1, turn)
            for k in range(2):
                back(4 * EX - 2 + k, WB - 1, k)
            close_sums()
            for cc in range(2):
                turn_sums(1, cc, 2 + cc)


N_ROUTER = 26
_INS = ("x", "pack", "split", "stack", "ctx", "ctxT", "rows", "maskc", "lvl", "wffn", "tri")


def _lay_out(i):
    g = lambda n: np.asarray(i[n])
    pack = np.zeros((P, NPACK), np.float32)

    def put(name, a):
        o, n = PACK[name]
        pack[:a.shape[0], o:o + a.shape[1]] = a

    parts = {"A": np.concatenate([np.tile(g("L0_attn_A")[:, i * LR:(i + 1) * LR], 4) for i in range(NS)], axis=1),
             "tdA": np.tile(g("L0_attn_tdA"), 2), "WkT": g("L0_attn_Wk").T, "WvT": g("L0_attn_Wv").T,
             "WrT": g("L0_attn_Wr").T, "Wg1a": g("L0_attn_Wg1")[:, :P], "Wg1b": np.tile(g("L0_attn_Wg1")[:, P:], 4),
             "tdB": np.tile(g("L0_attn_tdB"), (2, 1)), "Wg2a": g("L0_attn_Wg2")[:P]}
    stack = np.concatenate([g("L0_attn_Bp").transpose(1, 0, 2).reshape(LR, NS * C), g("L0_attn_Wg2")[P:]], axis=1)

    put("WoT", g("L0_attn_Wo").T)
    qkv = g("L0_xattn_qkv_w")
    put("wq", qkv[:C])
    put("wk", qkv[C:2 * C])
    put("xvT", qkv[2 * C:].T)
    put("pwT", g("L0_xattn_proj_w").T)
    put("rT", g("L0_ffn_router_w").T)
    put("ident", np.eye(P, dtype=np.float32))
    put("hsel", np.repeat(np.eye(NH, dtype=np.float32), HD, axis=0))
    cols = [g("L0_attn_miu_x").reshape(1, C), g("L0_attn_lam").reshape(NS, C), g("L0_attn_td_miu").reshape(1, C),
            g("L0_attn_u").reshape(1, C), g("L0_attn_gamma").reshape(1, C), g("L0_attn_beta").reshape(1, C)]
    put("cols", np.concatenate(cols).T)
    ctx = g("ctx_1024")
    levels = np.zeros((P, MASKED, HD), np.int32)
    for j in range(MASKED):
        h = 1 << j
        for s in range(P):
            for n in range(HD // h):
                levels[s, j, n * h:(n + 1) * h] = s // h == 2 * n
    tri = np.zeros((P, NG * NG + E), np.float32)
    tri[:, :NG * NG] = (np.arange(NG)[None, :] < np.arange(NG)[:, None]).reshape(1, -1)
    tri[:, NG * NG + 1:] = 1.0
    split = lambda a: a.reshape(C, 2, C).transpose(1, 0, 2)
    gate = np.concatenate([g("L0_ffn_gate_w"), split(g("L0_ffn_sh_gate_w"))])
    up = np.concatenate([g("L0_ffn_up_w"), split(g("L0_ffn_sh_up_w"))])
    down = np.concatenate([g("L0_ffn_down_w"), g("L0_ffn_sh_down_w").reshape(2, C, C)])
    return {
        "x": g("x"), "pack": pack,
        "split": np.concatenate([parts[name] for name in SPLIT], axis=1),
        "stack": np.tile(stack, (4, 1)),
        "ctx": ctx.reshape(B * (M // P), P, C).transpose(1, 0, 2),
        "ctxT": ctx.transpose(2, 0, 1).reshape(C, B * M),
        "rows": np.concatenate([g("L0_xattn_proj_b"), g("L0_ffn_bias")]),
        "maskc": g("mask_S2_ik0").reshape(M // P, P).T,
        "lvl": levels, "tri": tri,
        "wffn": np.concatenate([gate, up, down], axis=2),
    }


def kernel(**inputs):
    import concourse.bacc as bacc
    from concourse.bass_utils import run_bass_kernel_spmd

    nc = bacc.Bacc("TRN2", target_bir_lowering=False, num_devices=1)
    laid = _lay_out(inputs)
    arrays, args = {}, []
    for name in _INS:
        arr = np.ascontiguousarray(laid[name])
        arrays["in_" + name] = arr
        args.append(nc.dram_tensor("in_" + name, arr.shape, mybir.dt.from_np(arr.dtype), kind="ExternalInput").ap())
    args.append(nc.dram_tensor("out_0", (B, S, C), F32, kind="ExternalOutput").ap())
    args.append(nc.dram_tensor("combine_rows", (EX, 2, T), F32, kind="Internal").ap())
    decoder_layer(nc, *args)
    r = run_bass_kernel_spmd(nc, [arrays], core_ids=[0])
    return r.results[0]["out_0"]
```

```python
from contextlib import ExitStack

import numpy as np
import concourse.bass as bass
from concourse import mybir

F32 = mybir.dt.float32
F32R = mybir.dt.float32r
I32 = mybir.dt.int32
ALU = mybir.AluOpType
ACT = mybir.ActivationFunctionType
X = mybir.AxisListType.X

P = 128
B = 8
S = 256
M = 512
C = 128
T = B * S
NT = T // P
CH = 512
NCH = T // CH
HD = 64
NH = C // HD
NS = 5
LR = 32
GR = 160
TDR = 64
E = 16
EX = E + 2
NG = 4
EPG = E // NG
TOPG = 2
TOPK = 4
SCALE_TW = 2.5
WB = 3
TURNS = EX // WB
UNITS = 2 * EX
LEVELS = 8
MASKED = 6
SQ = 4
NSC = B // SQ
SCALE_QK = 0.25

PACK = {}
_at = 0
for _name, _n in (("WoT", C), ("wq", C), ("wk", C), ("xvT", C), ("pwT", C), ("rT", E),
                  ("ident", P), ("cols", 10), ("hsel", NH)):
    PACK[_name] = (_at, _n)
    _at += _n
NPACK = _at
SPLIT = {}
_at = 0
for _name, _n in (("A", NS * P), ("tdA", P), ("WkT", C), ("WvT", C), ("WrT", C), ("Wg1a", P), ("Wg1b", P),
                  ("tdB", C), ("Wg2a", C)):
    SPLIT[_name] = (_at, _n)
    _at += _n
NSPLIT = _at
NSTACK = NS * C + C
STREAMS = (0, 4, 1, 3, 2)
SLOT = (0, 1, 2, 0, 1)
COL = {n: i for i, n in enumerate(("miu_x", "lam0", "lam1", "lam2", "lam3", "lam4", "td_miu", "u", "gamma", "beta"))}


CREDIT = 5


def after(n):
    return n + CREDIT


def bc(ap, shape):
    return ap.unsqueeze(len(shape) - 1).to_broadcast(shape)


def decoder_layer(nc, x_d, pack_d, split_d, stack_d, ctx_d, ctxT_d, rows_d, maskc_d, lvl_d, wffn_d, tri_d, out_d, tw_d):
    x_v = x_d.rearrange("b (p h) c -> p b (h c)", h=2)
    out_v = out_d.rearrange("b (p h) c -> p b (h c)", h=2)

    with ExitStack() as stack:
        scope = [stack]

        def sb(name, shape, dt=F32):
            return scope[-1].enter_context(nc.sbuf_tensor(name, shape, dt))

        producers = {}

        def sem(name, eng=None):
            s = stack.enter_context(nc.semaphore(name))
            if eng:
                producers.setdefault(eng, []).append(s)
            return s

        bank = [stack.enter_context(nc.psum_tensor(f"bank{i}", [P, 512], F32)) for i in range(8)]

        xtok = sb("xtok", [P, NT, C])
        pack = sb("pack", [P, NPACK])
        W = {n: pack[:, o:o + w] for n, (o, w) in PACK.items()}
        col = {n: W["cols"][:, i:i + 1] for n, i in COL.items()}
        ident = W["ident"]
        wh_all = sb("wh_all", [P, NSPLIT], F32R)
        wl_all = sb("wl_all", [P, NSPLIT], F32R)
        WH = {n: wh_all[:, o:o + w] for n, (o, w) in SPLIT.items()}
        WL = {n: wl_all[:, o:o + w] for n, (o, w) in SPLIT.items()}
        wst = sb("wst", [P, NSTACK], F32R)
        pb_row = sb("pb_row", [P, C])
        bias_row = sb("bias_row", [P, E])
        mask_i = sb("mask_i", [P, M // P], I32)
        mask = sb("mask", [P, M // P])
        lvl = sb("lvl", [P, MASKED, HD], I32)
        tri = sb("tri", [P, NG * NG])
        seg = sb("seg", [P, E])
        neghalf = sb("neghalf", [P, 16])
        ctxn = sb("ctxn", [P, 2, M // P, C])
        ctxT = sb("ctxT", [C, 2, M])
        stat = {n: sb("st_" + n, [P, NT]) for n in ("sum", "mean", "var", "ve", "rstd")}
        zero_r = sb("zero_r", [P, CH], F32R)
        one_r = sb("one_r", [2, P], F32R)
        xc = sb("xc", [P, NT, C])
        sq = sb("sq", [P, NT, C])
        xn = sq
        mqh = sb("mqh", [C, C], F32R)
        mql = sb("mql", [C, C], F32R)
        scope.append(ExitStack())
        xTp = sb("xTp", [C, B, S + 1])
        bA = sb("bA", [C, B, S])
        dec = sb("dec", [C, T])
        kq = sb("kq", [C, T])
        rp = sb("rp", [C, NH, T])
        scope.append(ExitStack())
        raw = sb("raw", [P, NSPLIT])
        raw_s = sb("raw_s", [P, NSTACK])
        scope.pop().close()
        vv = sb("vv", [P, NT, C])
        gT = sb("gT", [C, T])
        dsum = sb("dsum", [P, NT, NH])
        at = sb("at", [P, 2, 4, NH, P])
        scope.append(ExitStack())
        HF = sb("HF", [P, NS * T], F32R)
        tmp_s = xc[:].rearrange("p a b -> p (a b)").rearrange("p (k t) -> p k t", t=CH)
        x5 = xn[:].rearrange("p a b -> p (a b)").rearrange("p (k t) -> p k t", t=CH)
        x5h = sb("x5h", [C, NS, CH], F32R)
        x5l = sb("x5l", [C, NS, CH], F32R)
        hT = tmp_s
        xx = sb("xx", [C, CH])
        w1 = sb("w1", [P, CH])
        w1s = sb("w1s", [P, CH], F32R)
        xxh, xxl = x5h, x5l
        g1a = xx
        g1ah = sb("g1ah", [P, CH], F32R)
        g1al = sb("g1al", [P, CH], F32R)
        g1b = sb("g1b", [P, CH])
        g1bs = sb("g1bs", [P, CH], F32R)
        ruk = g1b
        scope.pop().close()
        scope.append(ExitStack())
        at2 = sb("at2", [P, 2, 2, NH, P])
        tot = [None] + [sb(f"tot{j}", [C, 2, CH >> j]) for j in range(1, LEVELS - 1)]
        yc = sb("yc", [P, 2, 8, HD])
        gstat = {n: sb("gs_" + n, [P, 2, 8]) for n in ("sum", "mean", "var", "ve", "rstd")}
        yxc = yc
        vd = sb("vd", [P, 2 * SQ, NH, HD])
        ysq = sb("ysq", [P, 2, 8, HD])
        yn = ysq
        z1 = sb("z1", [C, 2, CH])
        z = z1
        scope.pop().close()
        scope.pop().close()
        qh = sb("qh", [C, 2, S], F32R)
        ql = sb("ql", [C, 2, S], F32R)
        cth = sb("cth", [C, 2, M], F32R)
        ctl = sb("ctl", [C, 2, M], F32R)
        cnm = sb("cnm", [P, 2, M // P, C])
        cnh = sb("cnh", [P, 2, M // P, C], F32R)
        cnl = sb("cnl", [P, 2, M // P, C], F32R)
        nmax = sb("nmax", [P, 4])
        psum_ = sb("psums", [P, 4])
        rsum = sb("rsum", [P, 4])
        pr = sb("pr", [P, 4, M])
        pws = sb("pws", [P, 2, C])
        t1s = sb("t1s", [C, 2 * C])
        xpb = sb("xpb", [P, NT, C])
        xh = sb("xh", [C, T], F32R)
        xl = sb("xl", [C, T], F32R)
        rth = sb("rth", [C, E], F32R)
        rtl = sb("rtl", [C, E], F32R)
        R = {n: sb("r_" + n, [P, NT, E]) for n in ("e", "e1", "sc", "s", "m", "gt", "eq", "cum", "le", "sel", "tw")}
        pair = sb("pair", [P, NT * NG, 6])
        gs = sb("gsc", [P, NT * NG])
        ggt = sb("ggt", [P, NT, NG * NG])
        geq = sb("geq", [P, NT, NG * NG])
        grk = sb("grk", [P, NT * NG])
        gm = sb("gm", [P, NT * NG])
        gm1 = sb("gm1", [P, NT * NG])
        top8 = sb("top8", [P, NT, 8])
        ngt = sb("ngt", [P, NT])
        tws = sb("tws", [P, NT])
        twr = sb("twr", [P, NT])
        combT = sb("combT", [E, T])
        combh = sb("combh", [E, T], F32R)
        combl = sb("combl", [E, T], F32R)
        wf = sb("wf", [P, WB, 3 * C])
        wfh = sb("wfh", [P, WB, 3 * C], F32R)
        wfl = sb("wfl", [P, WB, 3 * C], F32R)
        twrow = sb("twrow", [2, WB, 2 * CH], F32R)
        scope.append(ExitStack())
        xqh = sb("xqh", [C, T], F32R)
        xql = sb("xql", [C, T], F32R)
        t0h = sb("t0h", [P, M // P, 2 * C], F32R)
        t0l = sb("t0l", [P, M // P, 2 * C], F32R)
        scope.pop().close()
        sg = sb("sg", [P, 2, CH])
        stw = sb("stw", [P, 2, CH])
        aa = sb("aa", [P, 2, CH])
        ah = sb("ah", [P, 2, CH], F32R)
        al = sb("al", [P, 2, CH], F32R)
        yTs = pr[:, 0:2, :]

        d_x, d_w, d_small = sem("d_x"), sem("d_w"), sem("d_small")
        d_split, d_stack = sem("d_split"), sem("d_stack")
        d_ctx = [sem(f"d_ctx{i}") for i in range(2)]
        wh_done, wla_done, wl_done = sem("wh_done", "act"), sem("wla_done", "dve"), sem("wl_done", "pool")
        d_tw, d_out = sem("d_tw"), sem("d_out")
        d_wf = [sem(f"d_wf{i}") for i in range(WB)]
        d_row = [sem(f"d_row{i}") for i in range(WB)]
        init_v, init_p = sem("init_v", "dve"), sem("init_p", "pool")
        ln_sum, ln_mean, ln_xc, ln_var, ln_xn = (sem(n, "dve") for n in ("ln_sum", "ln_mean", "ln_xc", "ln_var", "ln_xn"))
        ln_sq = sem("ln_sq", "act")
        ln_ve, ln_rstd = sem("ln_ve", "pool"), sem("ln_rstd", "pool")
        tr = sem("tr", "pe")
        tr_act, tr_dve = sem("tr_act", "act"), sem("tr_dve", "dve")
        ba_done, xx_done = sem("ba_done", "dve"), sem("xx_done", "dve")
        xxh_done, xxl_done = sem("xxh_done", "act"), sem("xxl_done", "dve")
        h_pe, h_act, h_lo = sem("h_pe", "pe"), sem("h_act", "act"), sem("h_lo", "dve")
        x5h_done, x5l_done = sem("x5h_done", "act"), sem("x5l_done", "dve")
        w1_lo, g1_lo = sem("w1_lo", "dve"), sem("g1_lo", "dve")
        miu_pe, miu_t, xs_done = sem("miu_pe", "pe"), sem("miu_t", "dve"), sem("xs_done", "pool")
        w1_pe, w1_act, w2_pe, dec_done = sem("w1_pe", "pe"), sem("w1_act", "act"), sem("w2_pe", "pe"), sem("dec_done", "act")
        k_pe, k_done = sem("k_pe", "pe"), sem("k_done", "dve")
        v_pe, v_done = sem("v_pe", "pe"), sem("v_done", "act")
        r_pe, r_done = sem("r_pe", "pe"), sem("r_done", "act")
        ruk_done, ds_pe, ds_done = sem("ruk_done", "dve"), sem("ds_pe", "pe"), sem("ds_done", "act")
        g1_pe, g1_act, g_pe, g_done = sem("g1_pe", "pe"), sem("g1_act", "act"), sem("g_pe", "pe"), sem("g_done", "act")
        lv = [sem(f"lv{q}", "pe") for q in range(2)]
        lv_at = [sem(f"lv_at{q}", "dve") for q in range(2)]
        lv_act = [sem(f"lv_act{q}", "act") for q in range(2)]
        rp_up = [sem(f"rp_up{q}", "dve") for q in range(2)]
        kq_up = [sem(f"kq_up{q}", "pool") for q in range(2)]
        tot_up = [sem(f"tot_up{q}", "pool") for q in range(2)]
        y_pe, y_done, vd_done = sem("y_pe", "pe"), sem("y_done", "dve"), sem("vd_done", "pool")
        gn_sum, gn_mean, gn_xc, gn_var, gn_yn = (sem(n, "dve") for n in ("gn_sum", "gn_mean", "gn_xc", "gn_var", "gn_yn"))
        gn_sq = sem("gn_sq", "act")
        gn_ve, gn_rstd = sem("gn_ve", "pool"), sem("gn_rstd", "pool")
        yt_pe, z1_done, z_done = sem("yt_pe", "pe"), sem("z1_done", "dve"), sem("z_done", "dve")
        wo_pe, x1_done = sem("wo_pe", "pe"), sem("x1_done", "dve")
        m_pe, m_act, m_lo = sem("m_pe", "pe"), sem("m_act", "act"), sem("m_lo", "dve")
        q_pe, q_act, q_lo = sem("q_pe", "pe"), sem("q_act", "act"), sem("q_lo", "dve")
        s_pe, mx_done, ex_done = sem("s_pe", "pe"), sem("mx_done", "dve"), sem("ex_done", "act")
        rs_done, pws_done = sem("rs_done", "dve"), sem("pws_done", "dve")
        cth_done, cnh_done = sem("cth_done", "act"), sem("cnh_done", "act")
        ctl_done, cnm_done, cnl_done = sem("ctl_done", "pool"), sem("cnm_done", "pool"), sem("cnl_done", "pool")
        t0_pe, t0_act, t0_lo = sem("t0_pe", "pe"), sem("t0_act", "act"), sem("t0_lo", "dve")
        t1_pe, t1_done = sem("t1_pe", "pe"), sem("t1_done", "dve")
        fin_pe, x2_done = sem("fin_pe", "pe"), sem("x2_done", "dve")
        xpb_done = sem("xpb_done", "pool")
        lg_pe, lg_act = sem("lg_pe", "pe"), sem("lg_act", "act")
        rth_done, rtl_done = sem("rth_done", "act"), sem("rtl_done", "dve")
        chain = sem("chain", "dve")
        ct_pe, ct_act, ch_done, cl_done = sem("ct_pe", "pe"), sem("ct_act", "act"), sem("ch_done", "act"), sem("cl_done", "dve")
        wfh_done, wfl_done = sem("wfh_done", "act"), sem("wfl_done", "pool")
        h2_pe, u2_pe, tw_pe = sem("h2_pe", "pe"), sem("u2_pe", "pe"), sem("tw_pe", "pe")
        sg_done, stw_done, aa_done = sem("sg_done", "act"), sem("stw_done", "dve"), sem("aa_done", "dve")
        ah_done, al_done = sem("ah_done", "act"), sem("al_done", "pool")
        al_last, y2_pe = sem("al_last", "dve"), sem("y2_pe", "pe")
        yts_done, yo_pe, out_done = sem("yts_done", "act"), sem("yo_pe", "pe"), sem("out_done", "dve")

        carrier = {n: sem("carrier_" + n) for n in ("pool",)}

        block = stack.enter_context(nc.Block())

        def credit(eng, name):
            for s in producers[name]:
                eng.sem_inc(s, CREDIT)

        def carry(eng, which):
            eng.sem_inc(carrier[which], 1)

        GROUP = [[slice(c * (SQ * S) + q * CH, c * (SQ * S) + (q + 1) * CH) for q in range(2)] for c in range(NSC)]

        def halves(ap, h):
            return ap.rearrange("p (n two h) -> p n two h", two=2, h=h)

        def total(c, j, q):
            t_ = dec[:, GROUP[c][q]] if j == 0 else tot[j][:, q, :]
            return t_.rearrange("p (n two) -> p n two", two=2)

        def turned(k, c):
            return (0, min(2 + c, 4), 4 if c < 2 else 7)[k]

        def half_of(h):
            return slice(h * (NT // 2), (h + 1) * (NT // 2))

        LOGITS = (4, 7)

        @block.sync
        def _(sp):
            sp.dma_start(xtok[:].rearrange("p (b h) c -> p b (h c)", h=2), x_v).then_inc(d_x, 16)
            sp.dma_start(pack[:], pack_d).then_inc(d_w, 16)
            sp.dma_start(raw[:], split_d).then_inc(d_split, 16)
            sp.dma_start(raw_s[:], stack_d).then_inc(d_stack, 16)
            sp.dma_start(lvl[:], lvl_d).then_inc(d_small, 16)
            sp.dma_start(tri[:], tri_d[:, 0:NG * NG]).then_inc(d_small, 16)
            sp.dma_start(seg[:], tri_d[:, NG * NG:NG * NG + E]).then_inc(d_small, 16)
            sp.dma_start(mask_i[:], maskc_d).then_inc(d_small, 16)
            sp.dma_start(pb_row[:], rows_d[0:C].unsqueeze(0).to_broadcast([P, C])).then_inc(d_small, 16)
            sp.dma_start(bias_row[:], rows_d[C:C + E].unsqueeze(0).to_broadcast([P, E])).then_inc(d_small, 16)
            sp.wait_ge(init_v, after(2))
            sp.dma_start(tw_d[0:2, 0, :].rearrange("e (k n) -> e k n", n=P), one_r[:].bitcast(F32).unsqueeze(1).to_broadcast([2, T // P, P])).then_inc(d_tw, 16)
            sp.dma_start(tw_d[0:2, 1, :].rearrange("e (k n) -> e k n", n=CH), zero_r[0:2, :].bitcast(F32).unsqueeze(1).to_broadcast([2, NCH, CH])).then_inc(d_tw, 16)
            with sp.Fori(0, B // 2) as bp2:
                for par in range(2):
                    sp.wait_ge(ctl_done, 2 * bp2 + par + after(0) - 1)
                    sp.wait_ge(cnm_done, 2 * bp2 + par + after(0) - 1)
                    sp.dma_start(ctxT[:, par, :], ctxT_d[:, bass.ds((bp2 * 2 + par) * M, M)]).then_inc(d_ctx[par], 16)
                    sp.dma_start(ctxn[:, par], ctx_d[:, bass.ds((bp2 * 2 + par) * (M // P), M // P), :]).then_inc(d_ctx[par], 16)
            def store_combine(h):
                tok = slice(h * 2 * CH, (h + 1) * 2 * CH)
                sp.wait_ge(ch_done, after(h + 1))
                sp.dma_start(tw_d[2:EX, 0, tok], combh[:, tok].bitcast(F32)).then_inc(d_tw, 16)
                sp.wait_ge(cl_done, after(h + 1))
                sp.dma_start(tw_d[2:EX, 1, tok], combl[:, tok].bitcast(F32)).then_inc(d_tw, 16)
                sp.wait_ge(d_tw, 32 * (h + 2))

            def load_weights(hf, turn, par):
                sp.wait_ge(wfl_done, hf * EX + turn * WB + par + after(0) - (WB - 1))
                sp.dma_start(wf[:, par, :], wffn_d[bass.ds(turn * WB + par, 1), :, :].rearrange("o p n -> (o p) n")).then_inc(d_wf[par], 16)

            def load_row(hf, turn, par):
                sp.wait_ge(tw_pe, (hf * EX + turn * WB + par) * 2 + after(0) - 2 * (WB - 1))
                sp.dma_start(twrow[:, par, :].bitcast(F32), tw_d[bass.ds(turn * WB + par, 1), :, hf * 2 * CH:(hf + 1) * 2 * CH]
                             .rearrange("o k n -> (o k) n")).then_inc(d_row[par], 16)

            def load_experts(hf, turn):
                for par in range(WB):
                    load_weights(hf, turn, par)
                    load_row(hf, turn, par)

            sp.wait_ge(d_tw, 32)
            for par in range(WB):
                load_weights(0, 0, par)
            for par in range(2):
                load_row(0, 0, par)
            store_combine(0)
            load_row(0, 0, 2)
            with sp.Fori(1, TURNS) as turn:
                load_experts(0, turn)
            store_combine(1)
            with sp.Fori(0, TURNS) as turn:
                load_experts(1, turn)
            for c in range(NCH):
                sp.wait_ge(out_done, after(c + 1))
                sp.dma_start(out_v[:, 2 * c:2 * c + 2, :],
                             xtok[:, 4 * c:4 * c + 4, :].rearrange("p (b h) c -> p b (h c)", h=2)).then_inc(d_out, 16)
            sp.wait_ge(d_out, 16 * NCH)

        @block.gpsimd
        def _(pool):
            credit(pool, "pool")
            g = nc.gpsimd
            g.memset(neghalf[:], -0.5).then_inc(init_p, 1)
            g.memset(xTp[:], 0.0).then_inc(init_p, 1)
            g.memset(rp[:], 0.0).then_inc(init_p, 1)

            def norm_rstd(k, chunks=range(NCH)):
                for c in chunks:
                    ti = slice(4 * c, 4 * c + 4)
                    pool.wait_ge(ln_var, after(k * NCH + c + 1))
                    g.tensor_scalar(stat["ve"][:, ti], stat["var"][:, ti], 1.0 / C, 1e-5, ALU.mult, ALU.add).then_inc(ln_ve, 1)
                    pool.wait_ge(ln_ve, after(k * NCH + c + 1))
                    g.tensor_tensor(stat["rstd"][:, ti], stat["ve"][:, ti], neghalf[:, ti], ALU.pow).then_inc(ln_rstd, 1)

            norm_rstd(0)
            pool.wait_ge(wh_done, after(2))
            na = SPLIT["A"][1]
            g.tensor_tensor(wl_all[:, na:], raw[:, na:], wh_all[:, na:].bitcast(F32), ALU.subtract).then_inc(wl_done, 1)
            pool.wait_ge(wh_done, after(3))
            for k, o in enumerate((LR, 3 * LR)):
                pool.wait_ge(wl_done, after(k + 1))
                g.tensor_tensor(wst[o:o + LR, :], raw_s[o:o + LR, :], wst[o:o + LR, :].bitcast(F32), ALU.subtract).then_inc(wl_done, 1)
            pool.wait_ge(wl_done, after(3))
            g.memset(at[:], 0.0).then_inc(init_p, 1)

            def x_sum(c, p):
                n = c * NS + p
                pool.wait_ge(miu_t, n + after(1))
                pool.wait_ge(x5l_done, n + after(0) - 1)
                carry(pool, "pool")
                g.tensor_tensor(x5[:, SLOT[p], :].rearrange("p (b t) -> p b t", b=2), tmp_s[:, SLOT[p], :].rearrange("p (b t) -> p b t", b=2),
                                xTp[:, bass.ds(c * 2, 2), 1:S + 1], ALU.add).then_inc(xs_done, 1)

            with pool.Fori(0, NCH) as c:
                for p in range(NS):
                    x_sum(c, p)
            def group_rstd(c):
                for hf in range(2):
                    pool.wait_ge(gn_var, after(c * 2 + hf + 1))
                    g.tensor_scalar(gstat["ve"][:, hf, :], gstat["var"][:, hf, :], 1.0 / HD, 1e-5 * NH, ALU.mult, ALU.add).then_inc(gn_ve, 1)
                    pool.wait_ge(gn_ve, after(c * 2 + hf + 1))
                    g.tensor_tensor(gstat["rstd"][:, hf, :], gstat["ve"][:, hf, :], neghalf[:, 0:8], ALU.pow).then_inc(gn_rstd, 1)

            for c in range(NSC):
                for j in range(LEVELS - 1):
                    h = 1 << j
                    for q in range(2):
                        kqv, tv = halves(kq[:, GROUP[c][q]], h), total(c, j, q)
                        pool.wait_ge(lv[q], after(c * LEVELS + j + 1))
                        if j > 0:
                            pool.wait_ge(tot_up[q], after(c * (LEVELS - 2) + j))
                            pool.wait_ge(kq_up[q], after(c * (LEVELS - 1) + j))
                        g.tensor_tensor(kqv[:, :, 0, :], kqv[:, :, 0, :], bc(tv[:, :, 1], [P, CH // 2 // h, h]), ALU.mult).then_inc(kq_up[q], 1)
                        if j < LEVELS - 2:
                            pool.wait_ge(rp_up[q], after(c * (LEVELS - 1)))
                            g.tensor_tensor(tot[j + 1][:, q, :], tv[:, :, 0], tv[:, :, 1], ALU.mult).then_inc(tot_up[q], 1)
                    if c > 0 and j == 1:
                        group_rstd(c - 1)
                    if j == MASKED - 1:
                        pool.wait_ge(ds_done, after(NCH))
                        pool.wait_ge(y_done, after(c * SQ))
                        tiles = slice(c * 2 * SQ, (c + 1) * 2 * SQ)
                        g.tensor_tensor(vd[:], vv[:, tiles, :].rearrange("p t (n i) -> p t n i", n=NH),
                                        bc(dsum[:, tiles, :], [P, 2 * SQ, NH, HD]), ALU.mult).then_inc(vd_done, 1)

            def ctxT_low(b, par):
                pool.wait_ge(cth_done, b + after(1))
                g.tensor_tensor(ctl[:, par, :], ctxT[:, par, :], cth[:, par, :].bitcast(F32), ALU.subtract).then_inc(ctl_done, 1)

            def ctxn_masked(b, par, turn):
                pool.wait_ge(d_ctx[par], turn * 32 + 32)
                pool.wait_ge(cnh_done, b + after(0) - 1)
                pool.wait_ge(cnl_done, b + after(0) - 1)
                g.tensor_tensor(cnm[:, par], ctxn[:, par], bc(mask[:], [P, M // P, C]), ALU.mult).then_inc(cnm_done, 1)

            def ctxn_low(b, par):
                pool.wait_ge(cnh_done, b + after(1))
                g.tensor_tensor(cnl[:, par], cnm[:, par], cnh[:, par].bitcast(F32), ALU.subtract).then_inc(cnl_done, 1)

            pool.wait_ge(init_v, after(3))
            ctxT_low(0, 0)
            ctxn_masked(0, 0, 0)
            ctxn_low(0, 0)
            ctxT_low(1, 1)
            ctxn_masked(1, 1, 0)
            group_rstd(NSC - 1)
            norm_rstd(1, (0, 1))

            def with_bias(h):
                pool.wait_ge(x1_done, after(2 * h + 2))
                g.tensor_tensor(xpb[:, half_of(h)], xtok[:, half_of(h)], pb_row[:].unsqueeze(1).to_broadcast([P, NT // 2, C]), ALU.add).then_inc(xpb_done, 1)

            pool.wait_ge(d_small, 96)
            with_bias(0)

            def context_turn(b, par, turn):
                ctxn_low(b + 1, 1 - par)
                ctxT_low(b + 2, par)
                ctxn_masked(b + 2, par, turn + 1)

            context_turn(0, 0, 0)
            norm_rstd(1, (2, 3))
            context_turn(1, 1, 0)
            with_bias(1)
            context_turn(2, 0, 1)
            context_turn(3, 1, 1)
            context_turn(4, 0, 2)
            norm_rstd(2, (0, 1))
            context_turn(5, 1, 2)
            ctxn_low(B - 1, 1)

            def wf_low(n, par):
                pool.wait_ge(wfh_done, n + after(1))
                g.tensor_tensor(wfl[:, par, :], wf[:, par, :], wfh[:, par, :].bitcast(F32), ALU.subtract).then_inc(wfl_done, 1)

            def low_of(n, cc):
                pool.wait_ge(ah_done, n + after(1))
                pool.wait_ge(y2_pe, n + after(0) - 1)
                g.tensor_tensor(al[:, cc, :], aa[:, cc, :], ah[:, cc, :].bitcast(F32), ALU.subtract).then_inc(al_done, 1)

            def turn_of(hf, turn, first=False, last=False, beside=None):
                for k in range(2 * WB):
                    e = hf * EX + turn * WB + k // 2
                    if not (first and k == 0):
                        low_of(e * 2 + k % 2 - 1, 1 - k % 2)
                    if k % 2 == 0 and not (last and k == 2 * WB - 2):
                        wf_low(e + 1, (k // 2 + 1) % WB)
                    if beside and k in beside:
                        beside[k]()

            wf_low(0, 0)
            turn_of(0, 0, first=True)
            turn_of(0, 1, beside={1: lambda: norm_rstd(2, (2, 3))})
            with pool.Fori(2, TURNS) as turn:
                turn_of(0, turn)
            with pool.Fori(0, TURNS - 1) as turn:
                turn_of(1, turn)
            turn_of(1, TURNS - 1, last=True)

        @block.scalar
        def _(act):
            a = nc.scalar
            credit(act, "act")

            def norm_sq(k, chunks=range(NCH)):
                for c in chunks:
                    ti = slice(4 * c, 4 * c + 4)
                    act.wait_ge(ln_xc, after(k * NCH + c + 1))
                    a.activation(sq[:, ti], xc[:, ti], ACT.Square).then_inc(ln_sq, 1)

            act.preload_act_table(ACT.Exp)
            norm_sq(0)
            act.wait_ge(m_pe, after(1))
            a.activation(mqh[:], bank[7][:, 0:C], ACT.Copy).then_inc(m_act, 1)
            na = SPLIT["A"][1]
            act.wait_ge(d_split, 16)
            a.activation(wh_all[:, 0:na], raw[:, 0:na], ACT.Copy).then_inc(wh_done, 1)
            a.activation(wh_all[:, na:], raw[:, na:], ACT.Copy).then_inc(wh_done, 1)
            act.wait_ge(d_stack, 16)
            a.activation(wst[:], raw_s[:], ACT.Copy).then_inc(wh_done, 1)

            def x_in(c):
                act.wait_ge(tr, c + after(1))
                act.wait_ge(init_p, after(3))
                for q in range(2):
                    src = bank[0][:, q * S:(q + 1) * S].rearrange("p (h j) -> p h j", h=2)
                    dst = xTp[:, bass.ds(c * 2 + q, 1), 1:S + 1].rearrange("p o (j h) -> p (o h) j", h=2)
                    last = a.activation(dst, src, ACT.Copy)
                last.then_inc(tr_act, 1)

            def xx_high(c):
                act.wait_ge(xx_done, c + after(1))
                a.activation(xxh[:, bass.ds(c, 1), :].rearrange("p o n -> p (o n)"), xx[:], ACT.Copy).then_inc(xxh_done, 1)

            def tanh_of(c, blocks=range(NS)):
                hfv = HF[:, bass.ds(c * CH * NS, CH * NS)].rearrange("p (t i) -> p t i", i=NS)
                for i in blocks:
                    act.wait_ge(h_pe, c * NS + after(i + 1))
                    a.activation(hfv[:, :, i], bank[1 + i][:], ACT.Tanh)
                    act.wait_ge(h_lo, c * NS + i + after(0) - 1)
                    a.activation(hT[HD:P, SLOT[i], :], bank[1 + i][HD:P, :], ACT.Tanh).then_inc(h_act, 1)

            x_in(0)
            xx_high(0)
            with act.Fori(0, NCH - 1) as c:
                x_in(c + 1)
                tanh_of(c, range(2))
                xx_high(c + 1)
                tanh_of(c, range(2, NS))
            tanh_of(NCH - 1)

            def x_high(c, p):
                act.wait_ge(xs_done, c * NS + after(p + 1))
                a.activation(x5h[:, p, :], x5[:, SLOT[p], :], ACT.Copy).then_inc(x5h_done, 1)

            def project(c, nxt):
                cs = bass.ds(c * CH, CH)
                act.wait_ge(w1_pe, c + after(1))
                act.wait_ge(w2_pe, c + after(0))
                a.activation(w1s[:], bank[4][:], ACT.Tanh)
                a.activation(w1[HD:P, :], bank[4][HD:P, :], ACT.Tanh).then_inc(w1_act, 1)
                act.wait_ge(g1_pe, c + after(1))
                act.wait_ge(g_pe, c + after(0))
                a.activation(g1ah[:], bank[2][:], ACT.Tanh)
                a.activation(g1a[:], bank[2][:], ACT.Tanh)
                a.activation(g1bs[:], bank[3][:], ACT.Tanh)
                a.activation(g1b[HD:P, :], bank[3][HD:P, :], ACT.Tanh).then_inc(g1_act, 1)
                if nxt:
                    x_high(c + 1, 0)
                act.wait_ge(w2_pe, c + after(1))
                a.activation(dec[:, cs], bank[4][:], ACT.Exp, bias=col["td_miu"]).then_inc(dec_done, 1)
                if nxt:
                    x_high(c + 1, 1)
                act.wait_ge(r_pe, c + after(1))
                for hd in range(NH):
                    rows = slice(hd * HD, (hd + 1) * HD)
                    last = a.activation(rp[rows, hd, cs], bank[7][rows, :], ACT.Copy)
                last.then_inc(r_done, 1)
                if nxt:
                    x_high(c + 1, 2)
                act.wait_ge(g_pe, c + after(1))
                a.activation(gT[:, cs], bank[2][:], ACT.Copy).then_inc(g_done, 1)
                if nxt:
                    x_high(c + 1, 3)
                act.wait_ge(v_pe, c + after(1))
                a.activation(vv[:, bass.ds(c * 4, 4), :], bank[6][:].rearrange("p (i n) -> p i n", i=4), ACT.Copy).then_inc(v_done, 1)
                if nxt:
                    x_high(c + 1, 4)
                act.wait_ge(ds_pe, c + after(1))
                a.activation(dsum[:, bass.ds(c * 4, 4), :], bank[3][:, 0:4 * NH].rearrange("p (i n) -> p i n", i=4), ACT.Copy).then_inc(ds_done, 1)

            for p in range(NS):
                x_high(0, p)
            with act.Fori(0, NCH - 1) as c:
                project(c, True)
            project(NCH - 1, False)
            def group_square(c):
                for hf in range(2):
                    act.wait_ge(gn_xc, after(c * 2 + hf + 1))
                    a.activation(ysq[:, hf], yxc[:, hf], ACT.Square).then_inc(gn_sq, 1)

            for c in range(NSC):
                if c > 0:
                    group_square(c - 1)
                for q in range(2):
                    act.wait_ge(lv[q], after(c * LEVELS + MASKED + 1))
                    act.wait_ge(lv_at[q], after(c * MASKED + MASKED))
                    a.activation(at[0:HD, q, :, :, HD:P].rearrange("p k n t -> p (k n) t"),
                                 bank[q][0:HD, :].rearrange("p (k t) -> p k t", t=HD), ACT.Copy).then_inc(lv_act[q], 1)
                for q in range(2):
                    act.wait_ge(lv[q], after(c * LEVELS + LEVELS))
                    act.wait_ge(y_pe, after(c * SQ))
                    a.activation(at2[:, q].rearrange("p b n t -> p (b n t)"), bank[2 + q][:], ACT.Copy).then_inc(lv_act[q], 1)
            def ctxT_high(b, par, turn):
                act.wait_ge(d_ctx[par], turn * 32 + 32)
                act.wait_ge(s_pe, 2 * b + after(0) - 2)
                a.activation(cth[:, par, :], ctxT[:, par, :], ACT.Copy).then_inc(cth_done, 1)

            def ctxn_high(b, par):
                act.wait_ge(cnm_done, b + after(1))
                act.wait_ge(t1_pe, b + after(0) - 1)
                a.activation(cnh[:, par], cnm[:, par], ACT.Copy).then_inc(cnh_done, 1)

            for b in range(2):
                ctxT_high(b, b, 0)
            ctxn_high(0, 0)
            group_square(NSC - 1)
            norm_sq(1, (0, 1))
            a.activation(rth[:], W["rT"], ACT.Copy).then_inc(rth_done, 1)

            def x_in2(c):
                act.wait_ge(tr, after(NCH + c + 1))
                for q in range(2):
                    src = bank[turned(1, c)][:, q * S:(q + 1) * S].rearrange("p (h j) -> p h j", h=2)
                    dst = xqh[:, c * CH + q * S:c * CH + (q + 1) * S].rearrange("p (j h) -> p h j", h=2)
                    last = a.activation(dst, src, ACT.Copy)
                last.then_inc(tr_act, 1)

            x_in2(0)
            x_in2(1)

            def q_high(b, par):
                act.wait_ge(q_pe, b + after(1))
                a.activation(qh[:, par, :], bank[2 * par][:, 0:S], ACT.Copy, scale=SCALE_QK).then_inc(q_act, 1)

            def x_probs(b, par):
                for i in range(2):
                    k = 2 * par + i
                    act.wait_ge(mx_done, 2 * b + after(i + 1))
                    act.wait_ge(t0_pe, 2 * b + after(0) - 2)
                    a.activation(pr[:, k, :], bank[k][:], ACT.Exp, bias=nmax[:, k:k + 1],
                                 accum_out=psum_[:, k:k + 1]).then_inc(ex_done, 1)

            def t0_high(b):
                for i in range(2):
                    act.wait_ge(t0_pe, 2 * b + after(i + 1))
                    act.wait_ge(t1_pe, b + after(0))
                    a.activation(t0h[:, 2 * i:2 * i + 2, :].rearrange("p k n -> p (k n)"), bank[5 + i][:], ACT.Copy).then_inc(t0_act, 1)

            def x_turn(b, par, turn, more, most, between=None):
                if more:
                    q_high(b + 1, 1 - par)
                t0_high(b)
                if more:
                    x_probs(b + 1, 1 - par)
                    ctxn_high(b + 1, 1 - par)
                if between:
                    between()
                if most:
                    ctxT_high(b + 2, par, turn + 1)

            def x_in3(c):
                act.wait_ge(tr, after(2 * NCH + c + 1))
                a.activation(xh[:, c * CH:(c + 1) * CH], bank[turned(2, c)][:], ACT.Copy).then_inc(tr_act, 1)

            def router_exp(h):
                act.wait_ge(lg_pe, after(h + 1))
                a.activation(R["e"][:, half_of(h)], bank[LOGITS[h]][:, 0:NT // 2 * E].rearrange("p (t e) -> p t e", e=E),
                             ACT.Exp, scale=-1.0).then_inc(lg_act, 1)

            def combine_rows(h, k, b_):
                act.wait_ge(ct_pe, after(2 * h + k + 1))
                o = (2 * h + k) * CH
                a.activation(combT[0:E, o:o + CH], bank[b_][0:E, :], ACT.Copy).then_inc(ct_act, 1)

            def combine_high(h):
                tok = slice(h * 2 * CH, (h + 1) * 2 * CH)
                act.wait_ge(ct_act, after(2 * h + 2))
                a.activation(combh[:, tok], combT[:, tok], ACT.Copy).then_inc(ch_done, 1)

            q_high(0, 0)
            x_probs(0, 0)
            x_turn(0, 0, 0, True, True, between=lambda: norm_sq(1, (2,)))
            norm_sq(1, (3,))
            x_turn(1, 1, 0, True, True)
            x_in2(2)
            x_turn(2, 0, 1, True, True, between=lambda: x_in2(3))
            x_turn(3, 1, 1, True, True)
            x_turn(4, 0, 2, True, True)
            norm_sq(2, (0, 1))
            x_turn(5, 1, 2, True, True, between=lambda: x_in3(0))
            x_in3(1)
            x_turn(6, 0, 3, True, False, between=lambda: router_exp(0))
            def wf_high(n, par, loads):
                act.wait_ge(d_wf[par], loads * 16)
                act.wait_ge(y2_pe, 2 * n + after(0) - 2 * (WB - 1))
                a.activation(wfh[:, par, :], wf[:, par, :], ACT.Copy).then_inc(wfh_done, 1)

            def silu_of(n, cc):
                act.wait_ge(h2_pe, n + after(1))
                act.wait_ge(stw_done, n + after(0) - 1)
                a.activation(sg[:, cc, :], bank[2 + cc][:], ACT.Silu).then_inc(sg_done, 1)

            def high_of(n, cc):
                act.wait_ge(aa_done, n + after(1))
                act.wait_ge(y2_pe, n + after(0) - 1)
                a.activation(ah[:, cc, :], aa[:, cc, :], ACT.Copy).then_inc(ah_done, 1)

            def turn_of(hf, turn, first=False, last=False, beside=None):
                for k in range(2 * WB):
                    e = hf * EX + turn * WB + k // 2
                    silu_of(e * 2 + k % 2, k % 2)
                    if not (first and k == 0):
                        high_of(e * 2 + k % 2 - 1, 1 - k % 2)
                    if k % 2 == 0 and not (last and k == 2 * WB - 2):
                        par = (k // 2 + 1) % WB
                        loads = hf * TURNS + turn + (2 if k == 2 * WB - 2 else 1)
                        wf_high(e + 1, par, loads)
                    if beside and k in beside:
                        beside[k]()

            def sums_out(hf):
                for cc in range(2):
                    act.wait_ge(y2_pe, after((hf + 1) * UNITS - 1 + cc))
                    act.wait_ge(yo_pe, after(hf * 2))
                    a.activation(yTs[:, cc, :], bank[cc][:], ACT.Copy).then_inc(yts_done, 1)

            wf_high(0, 0, 1)
            x_turn(7, 1, 3, False, False)
            act.preload_act_table(ACT.Silu)

            def first_combine():
                for k in range(2):
                    combine_rows(0, k, k)
                combine_high(0)

            def second_exp():
                act.preload_act_table(ACT.Exp)
                router_exp(1)
                act.preload_act_table(ACT.Silu)

            def second_combine():
                combine_rows(1, 1, 7)
                combine_high(1)

            turn_of(0, 0, first=True, beside={1: first_combine, 3: lambda: norm_sq(2, (2,)), 4: lambda: norm_sq(2, (3,))})
            turn_of(0, 1, beside={5: lambda: x_in3(2)})
            turn_of(0, 2, beside={2: lambda: x_in3(3), 4: second_exp})
            turn_of(0, 3)
            turn_of(0, 4, beside={4: lambda: combine_rows(1, 0, 7), 5: second_combine})
            turn_of(0, 5)
            turn_of(1, 0, beside={1: lambda: sums_out(0)})
            with act.Fori(1, TURNS - 1) as turn:
                turn_of(1, turn)
            turn_of(1, TURNS - 1, last=True)
            high_of(4 * EX - 1, 1)
            sums_out(1)

        @block.vector
        def _(dve):
            v = nc.vector
            credit(dve, "dve")
            v.memset(zero_r[:].bitcast(F32), 0.0).then_inc(init_v, 1)
            v.memset(one_r[:].bitcast(F32), 1.0).then_inc(init_v, 1)

            def centre(k, c):
                ti = slice(4 * c, 4 * c + 4)
                n = k * NCH + c + 1
                v.tensor_reduce(stat["sum"][:, ti], xtok[:, ti], X, ALU.add).then_inc(ln_sum, 1)
                dve.wait_ge(ln_sum, after(n))
                v.tensor_scalar(stat["mean"][:, ti], stat["sum"][:, ti], 1.0 / C, None, ALU.mult).then_inc(ln_mean, 1)
                dve.wait_ge(ln_mean, after(n))
                v.tensor_tensor(xc[:, ti], xtok[:, ti], bc(stat["mean"][:, ti], [P, 4, C]), ALU.subtract).then_inc(ln_xc, 1)

            def variance(k, c):
                ti = slice(4 * c, 4 * c + 4)
                dve.wait_ge(ln_sq, after(k * NCH + c + 1))
                v.tensor_reduce(stat["var"][:, ti], sq[:, ti], X, ALU.add).then_inc(ln_var, 1)

            def scaled(k, c):
                ti = slice(4 * c, 4 * c + 4)
                dve.wait_ge(ln_rstd, after(k * NCH + c + 1))
                dve.wait_ge(ln_xc, after(k * NCH + c + 1))
                v.tensor_tensor(xn[:, ti], xc[:, ti], bc(stat["rstd"][:, ti], [P, 4, C]), ALU.mult).then_inc(ln_xn, 1)

            def norm(k):
                for c in range(NCH + 2):
                    if c < NCH:
                        centre(k, c)
                    if 1 <= c <= NCH:
                        variance(k, c - 1)
                    if c >= 2:
                        scaled(k, c - 2)

            dve.wait_ge(d_x, 16)
            norm(0)
            dve.wait_ge(m_act, after(1))
            v.tensor_tensor(mql[:], bank[7][:, 0:C], mqh[:].bitcast(F32), ALU.subtract).then_inc(m_lo, 1)
            dve.wait_ge(wh_done, after(1))
            na = SPLIT["A"][1]
            v.tensor_tensor(wl_all[:, 0:na], raw[:, 0:na], wh_all[:, 0:na].bitcast(F32), ALU.subtract).then_inc(wla_done, 1)
            dve.wait_ge(d_w, 16)

            def shifted(c):
                two = bass.ds(c * 2, 2)
                dve.wait_ge(tr_act, c + after(1))
                v.tensor_tensor(bA[:, two, :], xTp[:, two, 0:S], xTp[:, two, 1:S + 1], ALU.subtract).then_inc(ba_done, 1)
                dve.wait_ge(ba_done, c + after(1))
                dve.wait_ge(xxh_done, c + after(0))
                dve.wait_ge(xxl_done, c + after(0))
                v.scalar_tensor_tensor(xx[:].rearrange("p (b t) -> p b t", b=2), bA[:, two, :], col["miu_x"], xTp[:, two, 1:S + 1],
                                       ALU.mult, ALU.add).then_inc(xx_done, 1)

            def xx_low(c):
                dve.wait_ge(xxh_done, c + after(1))
                of = lambda buf: buf[:, bass.ds(c, 1), :].rearrange("p o n -> p (o n)")
                v.tensor_tensor(of(xxl), xx[:], of(xxh).bitcast(F32), ALU.subtract).then_inc(xxl_done, 1)

            def h_low(c, blocks=range(NS)):
                hfv = HF[HD:P, bass.ds(c * CH * NS, CH * NS)].rearrange("p (t i) -> p t i", i=NS)
                for i in blocks:
                    dve.wait_ge(h_act, c * NS + i + after(1))
                    v.tensor_tensor(hfv[:, :, i], hT[HD:P, SLOT[i], :], hfv[:, :, i].bitcast(F32), ALU.subtract).then_inc(h_lo, 1)

            shifted(0)
            xx_low(0)
            with dve.Fori(0, NCH - 1) as c:
                shifted(c + 1)
                h_low(c, range(1))
                xx_low(c + 1)
                h_low(c, range(1, NS))
            h_low(NCH - 1)
            dve.wait_ge(d_small, 96)
            v.tensor_scalar(mask[:], mask_i[:], 0.0, None, ALU.not_equal).then_inc(init_v, 1)

            def shift(c, p):
                n = c * NS + p
                dve.wait_ge(miu_pe, n + after(1))
                dve.wait_ge(xs_done, n + after(0) - 1)
                v.scalar_tensor_tensor(tmp_s[:, SLOT[p], :].rearrange("p (b t) -> p b t", b=2),
                                       bank[p % 2][:].rearrange("p (b t) -> p b t", b=2), col[f"lam{STREAMS[p]}"],
                                       bA[:, bass.ds(c * 2, 2), :], ALU.add, ALU.mult).then_inc(miu_t, 1)

            def x_low(c, p):
                dve.wait_ge(x5h_done, c * NS + after(p + 1))
                v.tensor_tensor(x5l[:, p, :], x5[:, SLOT[p], :], x5h[:, p, :].bitcast(F32), ALU.subtract).then_inc(x5l_done, 1)

            def project(c, nxt):
                cs = bass.ds(c * CH, CH)
                if nxt:
                    shift(c + 1, 0)
                dve.wait_ge(w1_act, c + after(1))
                v.tensor_tensor(w1s[HD:P, :], w1[HD:P, :], w1s[HD:P, :].bitcast(F32), ALU.subtract).then_inc(w1_lo, 1)
                if nxt:
                    shift(c + 1, 1)
                dve.wait_ge(g1_act, c + after(1))
                dve.wait_ge(g_pe, c + after(0))
                v.tensor_tensor(g1al[:], g1a[:], g1ah[:].bitcast(F32), ALU.subtract)
                v.tensor_tensor(g1bs[HD:P, :], g1b[HD:P, :], g1bs[HD:P, :].bitcast(F32), ALU.subtract).then_inc(g1_lo, 1)
                if nxt:
                    x_low(c + 1, 0)
                    shift(c + 1, 2)
                dve.wait_ge(k_pe, c + after(1))
                dve.wait_ge(dec_done, c + after(1))
                v.scalar_tensor_tensor(kq[:, cs], dec[:, cs], 1.0, bank[5][:], ALU.min, ALU.mult).then_inc(k_done, 1)
                if nxt:
                    x_low(c + 1, 1)
                    shift(c + 1, 3)
                dve.wait_ge(r_done, c + after(1))
                dve.wait_ge(k_done, c + after(1))
                dve.wait_ge(ds_pe, c + after(0))
                v.scalar_tensor_tensor(ruk[:], bank[7][:], col["u"], kq[:, cs], ALU.mult, ALU.mult).then_inc(ruk_done, 1)
                if nxt:
                    x_low(c + 1, 2)
                    shift(c + 1, 4)
                    x_low(c + 1, 3)
                    x_low(c + 1, 4)

            for p in range(NS):
                shift(0, p)
                if p > 1:
                    x_low(0, p - 2)
            x_low(0, NS - 2)
            x_low(0, NS - 1)
            with dve.Fori(0, NCH - 1) as c:
                project(c, True)
            project(NCH - 1, False)
            def group_centre(c):
                for hf in range(2):
                    dve.wait_ge(y_done, after(c * SQ + 2 * hf + 2))
                    v.tensor_reduce(gstat["sum"][:, hf, :], yc[:, hf], X, ALU.add).then_inc(gn_sum, 1)
                for hf in range(2):
                    dve.wait_ge(gn_sum, after(c * 2 + hf + 1))
                    v.tensor_scalar(gstat["mean"][:, hf, :], gstat["sum"][:, hf, :], 1.0 / HD, None, ALU.mult).then_inc(gn_mean, 1)
                for hf in range(2):
                    dve.wait_ge(gn_mean, after(c * 2 + hf + 1))
                    v.tensor_tensor(yxc[:, hf], yc[:, hf], bc(gstat["mean"][:, hf, :], [P, 8, HD]), ALU.subtract).then_inc(gn_xc, 1)

            def group_variance(c):
                for hf in range(2):
                    dve.wait_ge(gn_sq, after(c * 2 + hf + 1))
                    v.tensor_reduce(gstat["var"][:, hf, :], ysq[:, hf], X, ALU.add).then_inc(gn_var, 1)

            def group_scaled(c):
                for hf in range(2):
                    dve.wait_ge(gn_rstd, after(c * 2 + hf + 1))
                    dve.wait_ge(gn_xc, after(c * 2 + hf + 1))
                    v.tensor_tensor(yn[:, hf], yxc[:, hf], bc(gstat["rstd"][:, hf, :], [P, 8, HD]), ALU.mult).then_inc(gn_yn, 1)

            def gated(c):
                for hf in range(2):
                    dve.wait_ge(yt_pe, after(c * 2 + hf + 1))
                    dve.wait_ge(wo_pe, after(c * 2))
                    v.tensor_scalar(z1[:, hf, :], bank[4 + hf][:], col["gamma"], col["beta"], ALU.mult, ALU.add).then_inc(z1_done, 1)
                for hf in range(2):
                    dve.wait_ge(z1_done, after(c * 2 + hf + 1))
                    v.tensor_tensor(z[:, hf, :], z1[:, hf, :], gT[:, GROUP[c][hf]], ALU.mult).then_inc(z_done, 1)

            def residual(c):
                for hf in range(2):
                    dve.wait_ge(wo_pe, after(c * 2 + hf + 1))
                    xt4 = xtok[:, c * 8 + hf * 4:c * 8 + hf * 4 + 4, :]
                    v.tensor_tensor(xt4, xt4, bank[6 + hf][:].rearrange("p (i n) -> p i n", i=4), ALU.add).then_inc(x1_done, 1)

            TAIL = {0: group_centre, 1: group_variance, 2: group_scaled, 4: gated, 6: residual}
            dve.wait_ge(init_p, after(4))
            dve.wait_ge(d_small, 96)
            for c in range(NSC):
                for j in range(LEVELS - 1):
                    h = 1 << j
                    for q in range(2):
                        dve.wait_ge(lv[q], after(c * LEVELS + j + 1))
                        if 0 < j < MASKED:
                            dve.wait_ge(lv_at[q], after(c * MASKED + j))
                        rpv = rp[:, :, GROUP[c][q]].rearrange("p k (n two h) -> p k n two h", two=2, h=h)[:, :, :, 1, :]
                        if j > 0:
                            dve.wait_ge(tot_up[q], after(c * (LEVELS - 2) + j))
                            dve.wait_ge(rp_up[q], after(c * (LEVELS - 1) + j))
                        before = total(c, j, q)[:, :, 0].unsqueeze(1).unsqueeze(3).to_broadcast([P, NH, CH // 2 // h, h])
                        v.tensor_tensor(rpv, rpv, before, ALU.mult).then_inc(rp_up[q], 1)
                        if j == 0:
                            dve.wait_ge(y_pe, after(c * SQ))
                        if j < MASKED:
                            n = P // (2 * h)
                            dst = at[:, q].rearrange("p k m (n two h) -> p (k m) n two h", two=2, h=h)[:, :, :, 1, :]
                            src = bank[2 * (j % 2) + q][:].rearrange("p (k n h) -> p k n h", k=4 * NH, h=h)
                            msk = lvl[:, j, :].rearrange("p (n h) -> p n h", h=h).unsqueeze(1).to_broadcast([P, 4 * NH, n, h])
                            v.copy_predicated(dst, msk, src).then_inc(lv_at[q], 1)
                    if c > 0 and j in TAIL:
                        TAIL[j](c - 1)
                for q in range(SQ):
                    hf = q // 2
                    dve.wait_ge(y_pe, after(c * SQ + q + 1))
                    dve.wait_ge(gn_yn, after(c * 2))
                    dve.wait_ge(vd_done, after(c + 1))
                    half = slice(q % 2 * 4, q % 2 * 4 + 4)
                    v.tensor_tensor(yc[:, hf, half, :], vd[:, 2 * q:2 * q + 2].rearrange("p t n i -> p (t n) i"),
                                    bank[4 + q][:, 0:2 * P].rearrange("p (m i) -> p m i", i=HD), ALU.add).then_inc(y_done, 1)
            def x_in2(c):
                dve.wait_ge(tr_act, after(NCH + c + 1))
                for q in range(2):
                    of = slice(c * CH + q * S, c * CH + (q + 1) * S)
                    src = bank[turned(1, c)][:, q * S:(q + 1) * S].rearrange("p (h j) -> p h j", h=2)
                    last = v.tensor_tensor(xql[:, of].rearrange("p (j h) -> p h j", h=2), src,
                                           xqh[:, of].bitcast(F32).rearrange("p (j h) -> p h j", h=2), ALU.subtract)
                last.then_inc(tr_dve, 1)

            group_centre(NSC - 1)
            dve.wait_ge(x1_done, after(2))
            centre(1, 0)
            group_variance(NSC - 1)
            centre(1, 1)
            variance(1, 0)
            group_scaled(NSC - 1)
            variance(1, 1)
            gated(NSC - 1)
            scaled(1, 0)
            scaled(1, 1)
            x_in2(0)
            x_in2(1)
            residual(NSC - 1)
            dve.wait_ge(rth_done, after(1))
            v.tensor_tensor(rtl[:], W["rT"], rth[:].bitcast(F32), ALU.subtract).then_inc(rtl_done, 1)

            def q_low(b, par):
                dve.wait_ge(q_act, b + after(1))
                v.scalar_tensor_tensor(ql[:, par, :], bank[2 * par][:, 0:S], SCALE_QK, qh[:, par, :].bitcast(F32),
                                       ALU.mult, ALU.subtract).then_inc(q_lo, 1)

            def x_max(b, par):
                for i in range(2):
                    k = 2 * par + i
                    dve.wait_ge(s_pe, 2 * b + after(i + 1))
                    v.tensor_reduce(nmax[:, k:k + 1], bank[k][:], X, ALU.max, negate=True).then_inc(mx_done, 1)

            def x_scales(b, par):
                for i in range(2):
                    k = 2 * par + i
                    dve.wait_ge(ex_done, 2 * b + after(i + 1))
                    v.reciprocal(rsum[:, k:k + 1], psum_[:, k:k + 1]).then_inc(rs_done, 1)
                for i in range(2):
                    k = 2 * par + i
                    dve.wait_ge(rs_done, 2 * b + after(i + 1))
                    dve.wait_ge(t0_pe, 2 * b + after(0))
                    v.tensor_scalar(pws[:, i, :], W["pwT"], rsum[:, k:k + 1], None, ALU.mult).then_inc(pws_done, 1)

            def t0_low(b):
                for i in range(2):
                    dve.wait_ge(t0_act, 2 * b + after(i + 1))
                    half = slice(2 * i, 2 * i + 2)
                    flat = lambda buf: buf[:, half, :].rearrange("p k n -> p (k n)")
                    v.tensor_tensor(flat(t0l), bank[5 + i][:], flat(t0h).bitcast(F32), ALU.subtract).then_inc(t0_lo, 1)

            def x_sum(b, h):
                dve.wait_ge(fin_pe, b + after(1))
                dve.wait_ge(xpb_done, after(h + 1))
                v.tensor_tensor(xtok[:, bass.ds(b * 2, 2), :], xpb[:, bass.ds(b * 2, 2), :],
                                bank[7][:, 2 * C:4 * C].rearrange("p (i n) -> p i n", i=2), ALU.add).then_inc(x2_done, 1)

            def x_turn(b, par, more, early=None, middle=None, between=None, h=1):
                if more:
                    q_low(b + 1, 1 - par)
                t0_low(b)
                if early:
                    early()
                if more:
                    x_max(b + 1, 1 - par)
                if middle:
                    middle()
                dve.wait_ge(t1_pe, b + after(1))
                dve.wait_ge(fin_pe, b + after(0))
                v.tensor_copy(t1s[:], bank[7][:, 0:2 * C]).then_inc(t1_done, 1)
                if more:
                    x_scales(b + 1, 1 - par)
                if between:
                    between()
                x_sum(b, h)

            def x_in3(c):
                of = slice(c * CH, (c + 1) * CH)
                dve.wait_ge(tr_act, after(2 * NCH + c + 1))
                v.tensor_tensor(xl[:, of], bank[turned(2, c)][:], xh[:, of].bitcast(F32), ALU.subtract).then_inc(tr_dve, 1)

            count = [0]

            def step(ins):
                count[0] += 1
                ins.then_inc(chain, 1)
                dve.wait_ge(chain, after(count[0]))

            NH2 = NT // 2

            def of_half(h):
                groups = slice(h * NH2 * NG, (h + 1) * NH2 * NG)
                r = {n: buf[:, half_of(h)] for n, buf in R.items()}
                r.update({n: buf[:, groups] for n, buf in (("pair", pair), ("gs", gs), ("grk", grk), ("gm", gm), ("gm1", gm1))})
                r.update({n: buf[:, half_of(h)] for n, buf in (("ggt", ggt), ("geq", geq), ("top8", top8), ("ngt", ngt),
                                                                ("tws", tws), ("twr", twr))})
                r["s4"] = r["s"].rearrange("p t (g k) -> p (t g) k", k=EPG)
                r["m4"] = r["m"].rearrange("p t (g k) -> p (t g) k", k=EPG)
                return r

            def router_scores(h):
                r = of_half(h)
                dve.wait_ge(lg_act, after(h + 1))
                step(v.tensor_scalar(r["e1"], r["e"], 1.0, None, ALU.add))
                step(v.reciprocal(r["sc"], r["e1"]))

            def router_groups(h):
                r = of_half(h)
                step(v.tensor_tensor(r["s"], r["sc"], bias_row[:].unsqueeze(1).to_broadcast([P, NH2, E]), ALU.add))
                s4, pr6 = r["s4"], r["pair"]
                v.tensor_tensor(pr6[:, :, 0:3], s4[:, :, 0:3], s4[:, :, 1:4], ALU.add)
                v.tensor_tensor(pr6[:, :, 3:5], s4[:, :, 0:2], s4[:, :, 2:4], ALU.add)
                step(v.tensor_tensor(pr6[:, :, 5:6], s4[:, :, 0:1], s4[:, :, 3:4], ALU.add))
                step(v.tensor_reduce(r["gs"], pr6, X, ALU.max))

            def router_ranks(h):
                r = of_half(h)
                g3 = r["gs"].rearrange("p (t g) -> p t g", g=NG)
                other = g3.unsqueeze(2).to_broadcast([P, NH2, NG, NG])
                own = g3.unsqueeze(3).to_broadcast([P, NH2, NG, NG])
                v4 = lambda t: t.rearrange("p t (g k) -> p t g k", k=NG)
                v.tensor_tensor(v4(r["ggt"]), other, own, ALU.is_gt)
                step(v.tensor_tensor(v4(r["geq"]), other, own, ALU.is_equal))
                step(v.tensor_tensor(r["geq"], r["geq"], tri[:].unsqueeze(1).to_broadcast([P, NH2, NG * NG]), ALU.mult))

            def router_allowed(h):
                r = of_half(h)
                step(v.tensor_tensor(r["ggt"], r["ggt"], r["geq"], ALU.add))
                step(v.tensor_reduce(r["grk"], r["ggt"].rearrange("p t (g k) -> p (t g) k", k=NG), X, ALU.add))
                step(v.tensor_scalar(r["gm"], r["grk"], float(TOPG), None, ALU.is_lt))

            def router_masked(h):
                r = of_half(h)
                step(v.tensor_scalar(r["gm1"], r["gm"], -1.0, None, ALU.add))
                step(v.tensor_tensor(r["m4"], r["s4"], bc(r["gm"], [P, NH2 * NG, EPG]), ALU.mult))
                step(v.tensor_tensor(r["m4"], r["m4"], bc(r["gm1"], [P, NH2 * NG, EPG]), ALU.add))

            def router_top(h):
                r = of_half(h)
                for t in range(NH2):
                    last = v.max(r["top8"][:, t, :], r["m"][:, t, :])
                step(last)

            def router_chosen(h):
                r = of_half(h)
                fourth = r["top8"][:, :, TOPK - 1:TOPK].to_broadcast([P, NH2, E])
                v.tensor_tensor(r["gt"], r["m"], fourth, ALU.is_gt)
                step(v.tensor_tensor(r["eq"], r["m"], fourth, ALU.is_equal))
                v.tensor_reduce(r["ngt"], r["gt"], X, ALU.add)
                step(v.tensor_copy(r["le"], seg[:].unsqueeze(1).to_broadcast([P, NH2, E])))

            def router_ties(h):
                r = of_half(h)
                fl = lambda t: t.rearrange("p t e -> p (t e)")
                step(v.tensor_tensor_scan(fl(r["cum"]), fl(r["le"]), fl(r["eq"]), 0.0, ALU.mult, ALU.add))
                step(v.tensor_tensor(r["cum"], r["cum"], bc(r["ngt"], [P, NH2, E]), ALU.add))
                step(v.scalar_tensor_tensor(fl(r["le"]), fl(r["cum"]), float(TOPK), fl(r["eq"]), ALU.is_le, ALU.mult))
                step(v.tensor_tensor(r["sel"], r["gt"], r["le"], ALU.add))

            def router_weights(h):
                r = of_half(h)
                step(v.tensor_tensor(r["tw"], r["sc"], r["sel"], ALU.mult))
                step(v.tensor_reduce(r["tws"], r["tw"], X, ALU.add))

            def router_scaled(h):
                r = of_half(h)
                step(v.tensor_scalar(r["tws"], r["tws"], 1e-20, None, ALU.add))
                step(v.reciprocal(r["twr"], r["tws"]))
                step(v.tensor_tensor(r["tw"], r["tw"], bc(r["twr"], [P, NH2, E]), ALU.mult))
                step(v.tensor_scalar(r["tw"], r["tw"], SCALE_TW, None, ALU.mult))
                assert count[0] == (h + 1) * N_ROUTER

            def combine_low(h):
                tok = slice(h * 2 * CH, (h + 1) * 2 * CH)
                dve.wait_ge(ch_done, after(h + 1))
                v.tensor_tensor(combl[:, tok], combT[:, tok], combh[:, tok].bitcast(F32), ALU.subtract).then_inc(cl_done, 1)

            def norm3_centre(c):
                dve.wait_ge(x2_done, after(2 * c + 2))
                centre(2, c)

            def norm3_scaled():
                scaled(2, 0)
                scaled(2, 1)

            def norm2_scaled():
                scaled(1, 2)
                scaled(1, 3)

            q_low(0, 0)
            dve.wait_ge(x1_done, after(NCH))
            centre(1, 2)
            x_max(0, 0)
            x_scales(0, 0)
            x_turn(0, 0, True, h=0, between=lambda: centre(1, 3))
            variance(1, 2)
            variance(1, 3)
            x_turn(1, 1, True, h=0, between=norm2_scaled)
            x_in2(2)
            x_turn(2, 0, True, h=0, between=lambda: x_in2(3))
            x_turn(3, 1, True, h=0)
            x_turn(4, 0, True)
            norm3_centre(0)
            norm3_centre(1)
            variance(2, 0)
            variance(2, 1)
            x_turn(5, 1, True, early=norm3_scaled, between=lambda: x_in3(0))
            x_in3(1)
            x_turn(6, 0, True, middle=lambda: router_scores(0), between=lambda: router_groups(0))

            def early_router():
                router_ranks(0)
                router_allowed(0)
                router_masked(0)

            def top_chosen():
                router_top(0)
                router_chosen(0)

            x_turn(7, 1, False, early=early_router, between=top_chosen)
            router_ties(0)
            router_weights(0)
            router_scaled(0)

            def weigh_of(n, cc):
                dve.wait_ge(sg_done, n + after(1))
                dve.wait_ge(tw_pe, n + after(1))
                dve.wait_ge(aa_done, n + after(0) - 1)
                v.tensor_tensor(stw[:, cc, :], sg[:, cc, :], bank[6][:], ALU.mult).then_inc(stw_done, 1)
                dve.wait_ge(stw_done, n + after(1))
                dve.wait_ge(u2_pe, n + after(1))
                dve.wait_ge(al_done, n + after(0) - 1)
                v.tensor_tensor(aa[:, cc, :], stw[:, cc, :], bank[4 + cc][:], ALU.mult).then_inc(aa_done, 1)

            def turn_of(hf, turn, beside=()):
                for k in range(2 * WB):
                    weigh_of((hf * EX + turn * WB) * 2 + k, k % 2)
                    if k in beside:
                        beside[k]()

            def add_sums(hf, cc, b_):
                dve.wait_ge(yo_pe, after(hf * 2 + cc + 1))
                o = xtok[:, hf * 8 + cc * 4:hf * 8 + cc * 4 + 4, :]
                v.tensor_tensor(o, o, bank[b_][:].rearrange("p (i n) -> p i n", i=4), ALU.add).then_inc(out_done, 1)

            turn_of(0, 0, {1: lambda: combine_low(0), 2: lambda: norm3_centre(2), 3: lambda: norm3_centre(3),
                           4: lambda: variance(2, 2), 5: lambda: variance(2, 3)})
            turn_of(0, 1, {2: lambda: scaled(2, 2), 3: lambda: scaled(2, 3), 5: lambda: x_in3(2)})
            turn_of(0, 2, {2: lambda: x_in3(3), 5: lambda: router_scores(1)})
            turn_of(0, 3, {0: lambda: router_groups(1), 1: lambda: router_ranks(1), 2: lambda: router_allowed(1),
                           3: lambda: router_masked(1), 4: lambda: router_top(1), 5: lambda: router_chosen(1)})
            turn_of(0, 4, {0: lambda: router_ties(1), 1: lambda: router_weights(1), 2: lambda: router_scaled(1)})
            turn_of(0, 5, {0: lambda: combine_low(1)})
            turn_of(1, 0, {3: lambda: add_sums(0, 0, 7), 5: lambda: add_sums(0, 1, 7)})
            with dve.Fori(1, TURNS) as turn:
                turn_of(1, turn)
            dve.wait_ge(ah_done, after(2 * UNITS))
            dve.wait_ge(y2_pe, after(2 * UNITS - 2))
            v.tensor_tensor(al[:, 1, :], aa[:, 1, :], ah[:, 1, :].bitcast(F32), ALU.subtract).then_inc(al_last, 1)
            for cc in range(2):
                add_sums(1, cc, 2 + cc)

        @block.tensor
        def _(pe):
            t = nc.tensor
            credit(pe, "pe")
            pe.wait_ge(d_w, 16)

            t.matmul(bank[7][:, 0:C], W["wq"], W["wk"], start=True, stop=True).then_inc(m_pe, 1)

            def transpose_chunk(c, k):
                for i in range(4):
                    last = t.transpose(bank[turned(k, c)][:, i * P:(i + 1) * P], xn[:, c * 4 + i, :], ident)
                last.then_inc(tr, 1)

            def split_mm(dst, wh, wl, mh, ml, first, last_):
                t.matmul(dst, wh, mh, start=first, stop=False)
                t.matmul(dst, wh, ml, start=False, stop=False)
                return t.matmul(dst, wl, mh, start=False, stop=last_)

            def h_blocks(c):
                pe.wait_ge(xxl_done, after(c + 1))
                for i in range(NS):
                    pe.wait_ge(h_act, after(c * NS + i) - NS + 1)
                    bl = slice(i * P, (i + 1) * P)
                    split_mm(bank[1 + i][:], WH["A"][:, bl], WL["A"][:, bl], xxh[:, c, :], xxl[:, c, :], True, True).then_inc(h_pe, 1)

            for c in range(NCH):
                pe.wait_ge(ln_xn, after(c + 1))
                pe.wait_ge(tr_act, after(c))
                transpose_chunk(c, 0)
                if c == 1:
                    pe.wait_ge(wla_done, after(1))
                if c > 0:
                    h_blocks(c - 1)
            h_blocks(NCH - 1)
            pe.wait_ge(h_lo, after(NCH * NS))
            pe.wait_ge(wl_done, after(3))

            def miu(c, p):
                n = c * NS + p
                pe.wait_ge(miu_t, n + after(0) - (1 if p else 0))
                s = STREAMS[p]
                t.matmul(bank[p % 2][:], wst[:, s * C:(s + 1) * C], HF[:, bass.ds(c * CH + s * T, CH)],
                         start=True, stop=True).then_inc(miu_pe, 1)

            def project(c, nxt):
                def of(name, dst, p):
                    return split_mm(dst, WH[name], WL[name], x5h[:, p, :], x5l[:, p, :], True, True)

                def got(p):
                    pe.wait_ge(x5l_done, c * NS + after(p + 1))

                got(0)
                pe.wait_ge(dec_done, c + after(0))
                of("tdA", bank[4][:], 0).then_inc(w1_pe, 1)
                if nxt:
                    miu(c + 1, 0)
                got(1)
                pe.wait_ge(g_done, c + after(0))
                of("Wg1a", bank[2][:], 1)
                pe.wait_ge(ds_done, c + after(0))
                of("Wg1b", bank[3][:], 1).then_inc(g1_pe, 1)
                if nxt:
                    miu(c + 1, 1)
                got(2)
                pe.wait_ge(k_done, c + after(0))
                of("WkT", bank[5][:], 2).then_inc(k_pe, 1)
                pe.wait_ge(w1_lo, c + after(1))
                t.matmul(bank[4][:], WH["tdB"], w1s[:], start=True, stop=False)
                t.matmul(bank[4][:], WL["tdB"], w1s[:], start=False, stop=True).then_inc(w2_pe, 1)
                if nxt:
                    miu(c + 1, 2)
                got(3)
                pe.wait_ge(ruk_done, c + after(0))
                of("WrT", bank[7][:], 3).then_inc(r_pe, 1)
                if nxt:
                    miu(c + 1, 3)
                pe.wait_ge(g1_lo, c + after(1))
                split_mm(bank[2][:], WH["Wg2a"], WL["Wg2a"], g1ah[:], g1al[:], True, False)
                t.matmul(bank[2][:], wst[:, NS * C:NS * C + C], g1bs[:], start=False, stop=True).then_inc(g_pe, 1)
                if nxt:
                    miu(c + 1, 4)
                got(4)
                pe.wait_ge(v_done, c + after(0))
                for i in range(4):
                    ts = slice(i * P, (i + 1) * P)
                    last = split_mm(bank[6][:, i * C:(i + 1) * C], x5h[:, 4, ts], x5l[:, 4, ts], WH["WvT"], WL["WvT"], True, True)
                last.then_inc(v_pe, 1)
                pe.wait_ge(ruk_done, c + after(1))
                for i in range(4):
                    last = t.matmul(bank[3][:, i * NH:(i + 1) * NH], ruk[:, i * P:(i + 1) * P], W["hsel"], start=True, stop=True)
                last.then_inc(ds_pe, 1)

            for p in range(NS):
                miu(0, p)
            with pe.Fori(0, NCH - 1) as c:
                project(c, True)
            project(NCH - 1, False)
            pe.wait_ge(ds_done, after(NCH))
            pe.wait_ge(g_done, after(NCH))
            def group_turned(c):
                for hf in range(2):
                    pe.wait_ge(gn_yn, after(c * 2 + hf + 1))
                    for i in range(4):
                        last = t.transpose(bank[4 + hf][:, i * P:(i + 1) * P], yn[:, hf, 2 * i:2 * i + 2, :].rearrange("p a b -> p (a b)"), ident)
                    last.then_inc(yt_pe, 1)

            def out_product(c):
                for hf in range(2):
                    pe.wait_ge(z_done, after(c * 2 + hf + 1))
                    zv = z[:, hf, :].rearrange("p (q j h) -> p q h j", q=2, h=2)
                    for q in range(2):
                        for hh in range(2):
                            i = 2 * q + hh
                            last = t.matmul(bank[6 + hf][:, i * C:(i + 1) * C], zv[:, q, hh, :], W["WoT"], start=True, stop=True)
                    last.then_inc(wo_pe, 1)

            for c in range(NSC):
                for j in range(LEVELS):
                    h = 1 << j
                    for q in range(2):
                        if j > 0:
                            pe.wait_ge(rp_up[q], after(c * (LEVELS - 1) + j))
                            pe.wait_ge(kq_up[q], after(c * (LEVELS - 1) + j))
                        if j < 2:
                            pe.wait_ge(lv_act[q], after(c * 2))
                        else:
                            pe.wait_ge(lv_at[q], after(c * MASKED + j - 1))
                        dst = bank[2 * (j % 2) + q]
                        t0 = c * (SQ * S) + q * CH
                        if j == LEVELS - 1:
                            for b in range(2):
                                o = t0 + b * S
                                last = t.matmul(dst[:, b * S:(b + 1) * S].rearrange("p (n t) -> p n t", n=NH), kq[:, o:o + P],
                                                rp[:, :, o + P:o + 2 * P], start=True, stop=True)
                        else:
                            m = P if j < MASKED else HD
                            for k in range(4):
                                o = t0 + k * P
                                odd = rp[:, :, o:o + P].rearrange("p m (n two h) -> p m n two h", two=2, h=h)[:, :, :, 1, :]
                                last = t.matmul(dst[0:m, k * P:(k + 1) * P].rearrange("p (m n h) -> p m n h", m=NH, h=h),
                                                kq[:, o:o + m], odd, start=True, stop=True)
                        last.then_inc(lv[q], 1)
                    if c > 0 and j == 3:
                        group_turned(c - 1)
                    if c > 0 and j == 5:
                        out_product(c - 1)
                pe.wait_ge(x1_done, after(c * 2))
                for q in range(SQ):
                    grp, b = q // 2, q % 2
                    pe.wait_ge(lv_at[grp], after(c * MASKED + MASKED))
                    pe.wait_ge(lv_act[grp], after(c * 2 + 2))
                    for k in range(2):
                        for hd in range(NH):
                            dst = bank[4 + q][:, (2 * k + hd) * HD:(2 * k + hd + 1) * HD]
                            vt = lambda kk: vv[:, c * (2 * SQ) + q * 2 + kk, hd * HD:(hd + 1) * HD]
                            last = t.matmul(dst, at[:, grp, 2 * b + k, hd, :], vt(k), start=True, stop=(k == 0))
                            if k == 1:
                                last = t.matmul(dst, at2[:, grp, b, hd, :], vt(0), start=False, stop=True)
                    last.then_inc(y_pe, 1)
            group_turned(NSC - 1)

            def turn2(c):
                pe.wait_ge(ln_xn, after(NCH + c + 1))
                transpose_chunk(c, 1)

            out_product(NSC - 1)
            turn2(0)
            turn2(1)
            pe.wait_ge(m_lo, after(1))

            def project_q(b, par):
                pe.wait_ge(ex_done, 2 * b + after(0) - 2)
                tok = bass.ds(b * S, S)
                split_mm(bank[2 * par][:, 0:S], mqh[:], mql[:], xqh[:, tok], xql[:, tok], True, True).then_inc(q_pe, 1)

            def scores(b, par):
                pe.wait_ge(q_lo, b + after(1))
                pe.wait_ge(ctl_done, b + after(1))
                for i in range(2):
                    n = slice(i * P, (i + 1) * P)
                    split_mm(bank[2 * par + i][:], qh[:, par, n], ql[:, par, n], cth[:, par, :], ctl[:, par, :], True, True).then_inc(s_pe, 1)

            def x_t0(b, par):
                pe.wait_ge(pws_done, 2 * b + after(2))
                for half in range(2):
                    pe.wait_ge(t0_lo, 2 * b + after(half) - 1)
                    for k in range(2):
                        for i in range(2):
                            m = slice((2 * half + k) * P, (2 * half + k + 1) * P)
                            last = t.matmul(bank[5 + half][:, (2 * k + i) * C:(2 * k + i + 1) * C], pr[:, 2 * par + i, m], pws[:, i, :],
                                            start=True, stop=True)
                    last.then_inc(t0_pe, 1)

            def x_rest(b, par):
                pe.wait_ge(x2_done, b + after(0))
                pe.wait_ge(cnl_done, b + after(1))
                for k in range(4):
                    if k % 2 == 0:
                        pe.wait_ge(t0_lo, 2 * b + after(k // 2 + 1))
                    last = split_mm(bank[7][:, 0:2 * C], cnh[:, par, k, :], cnl[:, par, k, :], t0h[:, k, :], t0l[:, k, :], k == 0, k == 3)
                last.then_inc(t1_pe, 1)
                pe.wait_ge(t1_done, b + after(1))
                t.matmul(bank[7][:, 2 * C:4 * C], W["xvT"], t1s[:], start=True, stop=True).then_inc(fin_pe, 1)

            def x_turn(b, par, more, between=None):
                if more:
                    project_q(b + 1, 1 - par)
                x_t0(b, par)
                if more:
                    scores(b + 1, 1 - par)
                if between:
                    between()
                x_rest(b, par)

            def turn3(c):
                pe.wait_ge(ln_xn, after(2 * NCH + c + 1))
                pe.wait_ge(tr_dve, after(NCH + c))
                transpose_chunk(c, 2)

            def logits(h):
                pe.wait_ge(tr_dve, after(NCH + 2 * h + 2))
                pe.wait_ge(rtl_done, after(1))
                for i in range(NT // 2):
                    o = (h * (NT // 2) + i) * P
                    last = split_mm(bank[LOGITS[h]][:, i * E:(i + 1) * E], xh[:, o:o + P], xl[:, o:o + P], rth[:], rtl[:], True, True)
                last.then_inc(lg_pe, 1)

            def combine_turned(h, k, b_):
                pe.wait_ge(chain, after((h + 1) * N_ROUTER))
                for i in range(4):
                    last = t.transpose(bank[b_][0:E, i * P:(i + 1) * P], R["tw"][:, h * (NT // 2) + 4 * k + i, :], ident)
                last.then_inc(ct_pe, 1)

            pe.wait_ge(tr_dve, after(2))
            project_q(0, 0)
            scores(0, 0)
            x_turn(0, 0, True)
            x_turn(1, 1, True)
            turn2(2)

            def turn2_last():
                pe.wait_ge(tr_dve, after(3))
                turn2(3)

            x_turn(2, 0, True, between=turn2_last)
            x_turn(3, 1, True)
            pe.wait_ge(tr_dve, after(NCH))
            x_turn(4, 0, True)
            x_turn(5, 1, True, between=lambda: turn3(0))
            turn3(1)
            x_turn(6, 0, True, between=lambda: logits(0))
            x_turn(7, 1, False)
            def front(hf, n, par, cc, loads):
                cs = slice((hf * 2 + cc) * CH, (hf * 2 + cc + 1) * CH)
                wh = lambda m: wfh[:, par, m * C:(m + 1) * C]
                wl = lambda m: wfl[:, par, m * C:(m + 1) * C]
                pe.wait_ge(sg_done, n + after(0) - 1)
                split_mm(bank[2 + cc][:], wh(0), wl(0), xh[:, cs], xl[:, cs], True, True).then_inc(h2_pe, 1)
                pe.wait_ge(aa_done, n + after(0) - 1)
                split_mm(bank[4 + cc][:], wh(1), wl(1), xh[:, cs], xl[:, cs], True, True).then_inc(u2_pe, 1)
                pe.wait_ge(stw_done, n + after(0))
                pe.wait_ge(d_row[par], loads * 16)
                t.matmul(bank[6][:], one_r[:], twrow[:, par, cc * CH:(cc + 1) * CH], start=True, stop=True).then_inc(tw_pe, 1)

            def back(n, par, cc, first=False, last=False):
                pe.wait_ge(al_done, n + after(1))
                split_mm(bank[cc][:], wfh[:, par, 2 * C:3 * C], wfl[:, par, 2 * C:3 * C], ah[:, cc, :], al[:, cc, :],
                         first, last).then_inc(y2_pe, 1)

            def bank_free(hf, cc):
                pe.wait_ge(ct_act, after(cc + 1))
                if hf == 1:
                    pe.wait_ge(yts_done, after(cc + 1))

            def turn_sums(hf, cc, b_):
                pe.wait_ge(yts_done, after(hf * 2 + cc + 1))
                if hf == 0:
                    pe.wait_ge(out_done, after(cc))
                for i in range(4):
                    last = t.transpose(bank[b_][:, i * P:(i + 1) * P], yTs[:, cc, i * P:(i + 1) * P], ident)
                last.then_inc(yo_pe, 1)

            def turn_of(hf, turn, first=False, beside=()):
                for k in range(2 * WB):
                    e = hf * EX + turn * WB + k // 2
                    n = (hf * EX + turn * WB) * 2 + k
                    if k % 2 == 0:
                        pe.wait_ge(wfl_done, e + after(1))
                    front(hf, n, k // 2, k % 2, hf * TURNS + turn + 1)
                    if first and k in (2, 3):
                        bank_free(hf, k % 2)
                    if not (first and hf == 0 and k < 2):
                        back(n - 2, (k - 2) % (2 * WB) // 2, k % 2, first and k in (2, 3), first and k < 2)
                    if k in beside:
                        beside[k]()

            def first_combine():
                for k in range(2):
                    combine_turned(0, k, k)

            def second_combine(k):
                pe.wait_ge(ct_act, after(2 + k))
                combine_turned(1, k, 7)

            turn_of(0, 0, first=True, beside={1: first_combine})
            turn_of(0, 1, beside={5: lambda: turn3(2)})
            turn_of(0, 2, beside={2: lambda: turn3(3), 4: lambda: logits(1)})
            turn_of(0, 3)
            pe.wait_ge(lg_act, after(2))
            turn_of(0, 4, beside={4: lambda: second_combine(0), 5: lambda: second_combine(1)})
            turn_of(0, 5)
            pe.wait_ge(ct_act, after(4))
            turn_of(1, 0, first=True, beside={3: lambda: turn_sums(0, 0, 7), 5: lambda: turn_sums(0, 1, 7)})
            with pe.Fori(1, TURNS) as turn:
                turn_of(1, turn)
            back(2 * UNITS - 2, WB - 1, 0, last=True)
            pe.wait_ge(ah_done, after(2 * UNITS))
            t.matmul(bank[1][:], wfh[:, WB - 1, 2 * C:3 * C], ah[:, 1, :], start=False, stop=False)
            t.matmul(bank[1][:], wfl[:, WB - 1, 2 * C:3 * C], ah[:, 1, :], start=False, stop=False)
            pe.wait_ge(al_last, after(1))
            t.matmul(bank[1][:], wfh[:, WB - 1, 2 * C:3 * C], al[:, 1, :], start=False, stop=True).then_inc(y2_pe, 1)
            for cc in range(2):
                turn_sums(1, cc, 2 + cc)


N_ROUTER = 26
_INS = ("x", "pack", "split", "stack", "ctx", "ctxT", "rows", "maskc", "lvl", "wffn", "tri")


def _lay_out(i):
    g = lambda n: np.asarray(i[n])
    pack = np.zeros((P, NPACK), np.float32)

    def put(name, a):
        o, n = PACK[name]
        pack[:a.shape[0], o:o + a.shape[1]] = a

    parts = {"A": np.concatenate([np.tile(g("L0_attn_A")[:, i * LR:(i + 1) * LR], 4) for i in range(NS)], axis=1),
             "tdA": np.tile(g("L0_attn_tdA"), 2), "WkT": g("L0_attn_Wk").T, "WvT": g("L0_attn_Wv").T,
             "WrT": g("L0_attn_Wr").T, "Wg1a": g("L0_attn_Wg1")[:, :P], "Wg1b": np.tile(g("L0_attn_Wg1")[:, P:], 4),
             "tdB": np.tile(g("L0_attn_tdB"), (2, 1)), "Wg2a": g("L0_attn_Wg2")[:P]}
    stack = np.concatenate([g("L0_attn_Bp").transpose(1, 0, 2).reshape(LR, NS * C), g("L0_attn_Wg2")[P:]], axis=1)

    put("WoT", g("L0_attn_Wo").T)
    qkv = g("L0_xattn_qkv_w")
    put("wq", qkv[:C])
    put("wk", qkv[C:2 * C])
    put("xvT", qkv[2 * C:].T)
    put("pwT", g("L0_xattn_proj_w").T)
    put("rT", g("L0_ffn_router_w").T)
    put("ident", np.eye(P, dtype=np.float32))
    put("hsel", np.repeat(np.eye(NH, dtype=np.float32), HD, axis=0))
    cols = [g("L0_attn_miu_x").reshape(1, C), g("L0_attn_lam").reshape(NS, C), g("L0_attn_td_miu").reshape(1, C),
            g("L0_attn_u").reshape(1, C), g("L0_attn_gamma").reshape(1, C), g("L0_attn_beta").reshape(1, C)]
    put("cols", np.concatenate(cols).T)
    ctx = g("ctx_1024")
    levels = np.zeros((P, MASKED, HD), np.int32)
    for j in range(MASKED):
        h = 1 << j
        for s in range(P):
            for n in range(HD // h):
                levels[s, j, n * h:(n + 1) * h] = s // h == 2 * n
    tri = np.zeros((P, NG * NG + E), np.float32)
    tri[:, :NG * NG] = (np.arange(NG)[None, :] < np.arange(NG)[:, None]).reshape(1, -1)
    tri[:, NG * NG + 1:] = 1.0
    split = lambda a: a.reshape(C, 2, C).transpose(1, 0, 2)
    gate = np.concatenate([split(g("L0_ffn_sh_gate_w")), g("L0_ffn_gate_w")])
    up = np.concatenate([split(g("L0_ffn_sh_up_w")), g("L0_ffn_up_w")])
    down = np.concatenate([g("L0_ffn_sh_down_w").reshape(2, C, C), g("L0_ffn_down_w")])
    return {
        "x": g("x"), "pack": pack,
        "split": np.concatenate([parts[name] for name in SPLIT], axis=1),
        "stack": np.tile(stack, (4, 1)),
        "ctx": ctx.reshape(B * (M // P), P, C).transpose(1, 0, 2),
        "ctxT": ctx.transpose(2, 0, 1).reshape(C, B * M),
        "rows": np.concatenate([g("L0_xattn_proj_b"), g("L0_ffn_bias")]),
        "maskc": g("mask_S2_ik0").reshape(M // P, P).T,
        "lvl": levels, "tri": tri,
        "wffn": np.concatenate([gate, up, down], axis=2),
    }


def kernel(**inputs):
    import concourse.bacc as bacc
    from concourse.bass_utils import run_bass_kernel_spmd

    nc = bacc.Bacc("TRN2", target_bir_lowering=False, num_devices=1)
    laid = _lay_out(inputs)
    arrays, args = {}, []
    for name in _INS:
        arr = np.ascontiguousarray(laid[name])
        arrays["in_" + name] = arr
        args.append(nc.dram_tensor("in_" + name, arr.shape, mybir.dt.from_np(arr.dtype), kind="ExternalInput").ap())
    args.append(nc.dram_tensor("out_0", (B, S, C), F32, kind="ExternalOutput").ap())
    args.append(nc.dram_tensor("combine_rows", (EX, 2, T), F32, kind="Internal").ap())
    decoder_layer(nc, *args)
    r = run_bass_kernel_spmd(nc, [arrays], core_ids=[0])
    return r.results[0]["out_0"]
```
